# Optimizing a Trainium2 kernel written in Bass

```python
import numpy as np
import jax
import jax.numpy as jnp

def _softmax(x, axis=-1):
    return jax.nn.softmax(x, axis=axis)

def _gelu(x):
    return jax.nn.gelu(x, approximate=True)

def _silu(x):
    return jax.nn.silu(x)

def _sigmoid(x):
    return jax.nn.sigmoid(x)

def _layernorm(x, axis=-1, eps=1e-05):
    m = jnp.mean(x, axis=axis, keepdims=True)
    v = jnp.var(x, axis=axis, keepdims=True)
    return (x - m) / jnp.sqrt(v + eps)

def _scatter_add(tgt, idx, src, axis=0):
    return tgt.at[idx].add(src)

def _segment_sum(src, seg, n):
    return jax.ops.segment_sum(src, seg, n)
kernel_name = 'mk_adj_ffn_d2_adj_r2_79e33b'

def setup_inputs(seed: int=0):
    np.random.seed(seed)
    _w = jnp.asarray

    def _rec_inputs():
        import jax
        import jax.numpy as jnp
        _gk = jax.random.key(seed)
        x = -0.000125 + 0.9999 * jax.random.normal(jax.random.fold_in(_gk, 1), (8, 1024, 256), jnp.float32)
        _w = (1.0 + jnp.arange(1024, dtype=jnp.float32)) ** (-0.5)
        _w = _w / _w.mean()
        _pij = jnp.clip(0.015625 * _w[:, None] * _w[None, :], 0.0, 1.0)
        _a = jax.random.uniform(jax.random.fold_in(_gk, 2), (1024, 1024)) < _pij
        _af = _a.astype(jnp.float32)
        adj = _af
        return (x, adj)
    x, adj = _rec_inputs()

    def _L0_gnn_setup():
        import jax, jax.numpy as jnp
        import numpy as np
        ALPHA = 0.2
        key = jax.random.key(seed)
        k0, k1, k2, k3 = jax.random.split(key, 4)
        B, N, C, F = (64, 512, 256, 256)
        x = jax.random.normal(k0, (B, N, C), dtype=jnp.float32)
        W = jax.random.normal(k1, (C, F), dtype=jnp.float32) * (1.414 / np.sqrt(C + F))
        a = jax.random.normal(k2, (2 * F, 1), dtype=jnp.float32) * (1.414 / np.sqrt(2 * F + 1))
        beta = jnp.ones((1,), dtype=jnp.float32)
        mask = (jax.random.uniform(k3, (N, N)) < 0.3).astype(jnp.float32)
        return {'x': x, 'W': W, 'a': a, 'beta': beta, 'mask': mask}
    _L0_gnn_all = _L0_gnn_setup()
    _L0_gnn_in = {k: v for k, v in _L0_gnn_all.items() if k in ('W', 'a', 'beta')}
    del _L0_gnn_all

    def _L0_ffn_setup():
        import jax, jax.numpy as jnp
        import numpy as np
        DIM = 256
        NE = 8
        TOPK = 2
        CF = 1.2
        HID = 4 * DIM
        B, S = (8, 2048)
        key = jax.random.key(seed)
        ks = jax.random.split(key, 4)
        s = 0.02
        return {'x': jax.random.normal(ks[0], (B, S, DIM), jnp.float32), 'gate_w': jax.random.normal(ks[1], (NE, DIM), jnp.float32) * s, 'gate_b': jnp.zeros((NE,), jnp.float32), 'w1': jax.random.normal(ks[2], (NE, DIM, HID), jnp.float32) * s, 'b1': jnp.zeros((NE, HID), jnp.float32), 'w2': jax.random.normal(ks[3], (NE, HID, DIM), jnp.float32) * s, 'b2': jnp.zeros((NE, DIM), jnp.float32)}
    _L0_ffn_all = _L0_ffn_setup()
    _L0_ffn_in = {k: v for k, v in _L0_ffn_all.items() if k in ('gate_w', 'gate_b', 'w1', 'b1', 'w2', 'b2')}
    del _L0_ffn_all

    def _L1_gnn_setup():
        import jax, jax.numpy as jnp
        import numpy as np
        B, N, F_IN, F_OUT = (16, 1024, 256, 256)
        key = jax.random.key(seed)
        k1, k2, k3 = jax.random.split(key, 3)
        x = jax.random.normal(k1, (B, N, F_IN), dtype=jnp.float32)
        adj = jax.random.uniform(k2, (N, N), dtype=jnp.float32)
        bound = np.sqrt(6.0 / F_OUT)
        weight = jax.random.uniform(k3, (F_IN, F_OUT), dtype=jnp.float32, minval=-bound, maxval=bound)
        bias = jnp.zeros((F_OUT,), dtype=jnp.float32)
        return {'x': x, 'adj': adj, 'weight': weight, 'bias': bias}
    _L1_gnn_all = _L1_gnn_setup()
    _L1_gnn_in = {k: v for k, v in _L1_gnn_all.items() if k in ('weight', 'bias')}
    del _L1_gnn_all

    def _L1_ffn_setup():
        import jax, jax.numpy as jnp
        import numpy as np
        D_MODEL, D_STATE, D_CONV, D_INPUT, D_OUTPUT = (512, 16, 4, 256, 256)
        EXPAND = 2
        D_INNER = EXPAND * D_MODEL
        DT_RANK = (D_MODEL + 15) // 16
        B, L = (4, 1024)

        def _mamba(x, W_in, conv_w, conv_b, W_xproj, W_dt, b_dt, A_log, Dp, W_out):
            xz = jnp.einsum('bld,ed->ble', x, W_in)
            u, z = jnp.split(xz, 2, axis=-1)
            u_pad = jnp.pad(u, ((0, 0), (D_CONV - 1, 0), (0, 0)))
            u = sum((u_pad[:, k:k + u.shape[1], :] * conv_w[:, k] for k in range(D_CONV))) + conv_b
            u = jax.nn.silu(u)
            dbc = jnp.einsum('bld,ed->ble', u, W_xproj)
            dt, B_ssm, C_ssm = jnp.split(dbc, [DT_RANK, DT_RANK + D_STATE], axis=-1)
            delta = jax.nn.softplus(jnp.einsum('blr,dr->bld', dt, W_dt) + b_dt)
            A = -jnp.exp(A_log)

            def step(h, ins):
                d_t, B_t, C_t, u_t = ins
                dA = jnp.exp(d_t[..., None] * A)
                h = dA * h + (d_t * u_t)[..., None] * B_t[:, None, :]
                y_t = jnp.einsum('bds,bs->bd', h, C_t)
                return (h, y_t)
            h0 = jnp.zeros((u.shape[0], D_INNER, D_STATE), u.dtype)
            xs = (delta.transpose(1, 0, 2), B_ssm.transpose(1, 0, 2), C_ssm.transpose(1, 0, 2), u.transpose(1, 0, 2))
            _, y = jax.lax.scan(step, h0, xs)
            y = y.transpose(1, 0, 2) + u * Dp
            y = y * jax.nn.silu(z)
            return jnp.einsum('bld,ed->ble', y, W_out)
        key = jax.random.key(seed)
        ks = jax.random.split(key, 16)
        s = lambda fan_in: 1.0 / np.sqrt(fan_in)
        inp = {'x': jax.random.normal(ks[0], (B, L, D_INPUT), jnp.float32), 'W_fc1': jax.random.normal(ks[1], (D_MODEL, D_INPUT), jnp.float32) * s(D_INPUT), 'b_fc1': jnp.zeros((D_MODEL,), jnp.float32), 'W_in': jax.random.normal(ks[2], (2 * D_INNER, D_MODEL), jnp.float32) * s(D_MODEL), 'conv_w': jax.random.normal(ks[3], (D_INNER, D_CONV), jnp.float32) * s(D_CONV), 'conv_b': jnp.zeros((D_INNER,), jnp.float32), 'W_xproj': jax.random.normal(ks[4], (DT_RANK + 2 * D_STATE, D_INNER), jnp.float32) * s(D_INNER), 'W_dt': jax.random.normal(ks[5], (D_INNER, DT_RANK), jnp.float32) * s(DT_RANK), 'b_dt': jax.random.uniform(ks[6], (D_INNER,), jnp.float32, -4.0, -2.0), 'A_log': jnp.log(jnp.broadcast_to(jnp.arange(1, D_STATE + 1, dtype=jnp.float32), (D_INNER, D_STATE))), 'D': jnp.ones((D_INNER,), jnp.float32), 'W_out': jax.random.normal(ks[7], (D_MODEL, D_INNER), jnp.float32) * s(D_INNER), 'W_fc2': jax.random.normal(ks[8], (D_OUTPUT, D_MODEL), jnp.float32) * s(D_MODEL), 'b_fc2': jnp.zeros((D_OUTPUT,), jnp.float32)}
        return inp
    _L1_ffn_all = _L1_ffn_setup()
    _L1_ffn_in = {k: v for k, v in _L1_ffn_all.items() if k in ('W_fc1', 'b_fc1', 'W_in', 'conv_w', 'conv_b', 'W_xproj', 'W_dt', 'b_dt', 'A_log', 'D', 'W_out', 'W_fc2', 'b_fc2')}
    del _L1_ffn_all
    return {'x': x, 'adj': adj, 'L0_gnn_W': _L0_gnn_in['W'], 'L0_gnn_a': _L0_gnn_in['a'], 'L0_gnn_beta': _L0_gnn_in['beta'], 'L0_ffn_gate_w': _L0_ffn_in['gate_w'], 'L0_ffn_gate_b': _L0_ffn_in['gate_b'], 'L0_ffn_w1': _L0_ffn_in['w1'], 'L0_ffn_b1': _L0_ffn_in['b1'], 'L0_ffn_w2': _L0_ffn_in['w2'], 'L0_ffn_b2': _L0_ffn_in['b2'], 'L1_gnn_weight': _L1_gnn_in['weight'], 'L1_gnn_bias': _L1_gnn_in['bias'], 'L1_ffn_W_fc1': _L1_ffn_in['W_fc1'], 'L1_ffn_b_fc1': _L1_ffn_in['b_fc1'], 'L1_ffn_W_in': _L1_ffn_in['W_in'], 'L1_ffn_conv_w': _L1_ffn_in['conv_w'], 'L1_ffn_conv_b': _L1_ffn_in['conv_b'], 'L1_ffn_W_xproj': _L1_ffn_in['W_xproj'], 'L1_ffn_W_dt': _L1_ffn_in['W_dt'], 'L1_ffn_b_dt': _L1_ffn_in['b_dt'], 'L1_ffn_A_log': _L1_ffn_in['A_log'], 'L1_ffn_D': _L1_ffn_in['D'], 'L1_ffn_W_out': _L1_ffn_in['W_out'], 'L1_ffn_W_fc2': _L1_ffn_in['W_fc2'], 'L1_ffn_b_fc2': _L1_ffn_in['b_fc2']}

def reference(x, adj, L0_gnn_W, L0_gnn_a, L0_gnn_beta, L0_ffn_gate_w, L0_ffn_gate_b, L0_ffn_w1, L0_ffn_b1, L0_ffn_w2, L0_ffn_b2, L1_gnn_weight, L1_gnn_bias, L1_ffn_W_fc1, L1_ffn_b_fc1, L1_ffn_W_in, L1_ffn_conv_w, L1_ffn_conv_b, L1_ffn_W_xproj, L1_ffn_W_dt, L1_ffn_b_dt, L1_ffn_A_log, L1_ffn_D, L1_ffn_W_out, L1_ffn_W_fc2, L1_ffn_b_fc2):
    import jax
    import jax.numpy as jnp

    def _L0_gnn_ref(x, W, a, beta, mask):
        import jax, jax.numpy as jnp
        import numpy as np
        ALPHA = 0.2
        F_ = W.shape[1]
        h = jnp.einsum('bnc,cf->bnf', x, W)
        a1, a2 = (a[:F_, 0], a[F_:, 0])
        s1 = jnp.einsum('bnf,f->bn', h, a1)
        s2 = jnp.einsum('bnf,f->bn', h, a2)
        e = jax.nn.leaky_relu(s1[:, :, None] + s2[:, None, :], negative_slope=ALPHA)
        e = e * mask[None, :, :]
        att = jax.nn.softmax(e, axis=2)
        h_prime = jnp.einsum('bij,bjf->bif', att, h)
        return jax.nn.elu(h_prime + beta * h)

    def _L0_ffn_ref(x, gate_w, gate_b, w1, b1, w2, b2):
        import jax, jax.numpy as jnp
        import numpy as np
        DIM = 256
        NE = 8
        TOPK = 2
        CF = 1.2
        HID = 4 * DIM
        B, S = (8, 2048)
        Bq, Sq, D = x.shape
        T = Bq * Sq
        cap = int(CF * T / NE)
        xf = x.reshape(T, D)
        probs = jax.nn.softmax(xf @ gate_w.T + gate_b, axis=-1)
        topw, topi = jax.lax.top_k(probs, TOPK)
        onehot = jax.nn.one_hot(topi, NE, dtype=topw.dtype)
        w_te = jnp.einsum('tk,tke->te', topw, onehot)
        routed = onehot.sum(axis=1) > 0
        wm = jnp.where(routed, w_te, -1.0)
        sel_w, sel_idx = jax.lax.top_k(wm.T, cap)
        sel_w = jnp.maximum(sel_w, 0.0)
        xg = xf[sel_idx]
        h = jax.nn.gelu(jnp.einsum('ecd,edh->ech', xg, w1) + b1[:, None, :], approximate=False)
        out = jnp.einsum('ech,ehd->ecd', h, w2) + b2[:, None, :]
        weighted = out * sel_w[..., None]
        of = jnp.zeros((T, D), x.dtype).at[sel_idx.reshape(-1)].add(weighted.reshape(-1, D))
        return of.reshape(Bq, Sq, D)

    def _L1_gnn_ref(x, adj, weight, bias):
        import jax, jax.numpy as jnp
        import numpy as np
        B, N, F_IN, F_OUT = (16, 1024, 256, 256)
        deg = adj.sum(axis=1)
        deg_inv_sqrt = jnp.where(deg > 0, jax.lax.rsqrt(deg), 0.0)
        norm_adj = adj * deg_inv_sqrt[:, None] * deg_inv_sqrt[None, :]
        support = jnp.einsum('bni,io->bno', x, weight)
        output = jnp.einsum('nm,bmo->bno', norm_adj, support)
        return output + bias

    def _L1_ffn_ref(x, W_fc1, b_fc1, W_in, conv_w, conv_b, W_xproj, W_dt, b_dt, A_log, D, W_out, W_fc2, b_fc2):
        import jax, jax.numpy as jnp
        import numpy as np
        D_MODEL, D_STATE, D_CONV, D_INPUT, D_OUTPUT = (512, 16, 4, 256, 256)
        EXPAND = 2
        D_INNER = EXPAND * D_MODEL
        DT_RANK = (D_MODEL + 15) // 16
        B, L = (4, 1024)

        def _mamba(x, W_in, conv_w, conv_b, W_xproj, W_dt, b_dt, A_log, Dp, W_out):
            xz = jnp.einsum('bld,ed->ble', x, W_in)
            u, z = jnp.split(xz, 2, axis=-1)
            u_pad = jnp.pad(u, ((0, 0), (D_CONV - 1, 0), (0, 0)))
            u = sum((u_pad[:, k:k + u.shape[1], :] * conv_w[:, k] for k in range(D_CONV))) + conv_b
            u = jax.nn.silu(u)
            dbc = jnp.einsum('bld,ed->ble', u, W_xproj)
            dt, B_ssm, C_ssm = jnp.split(dbc, [DT_RANK, DT_RANK + D_STATE], axis=-1)
            delta = jax.nn.softplus(jnp.einsum('blr,dr->bld', dt, W_dt) + b_dt)
            A = -jnp.exp(A_log)

            def step(h, ins):
                d_t, B_t, C_t, u_t = ins
                dA = jnp.exp(d_t[..., None] * A)
                h = dA * h + (d_t * u_t)[..., None] * B_t[:, None, :]
                y_t = jnp.einsum('bds,bs->bd', h, C_t)
                return (h, y_t)
            h0 = jnp.zeros((u.shape[0], D_INNER, D_STATE), u.dtype)
            xs = (delta.transpose(1, 0, 2), B_ssm.transpose(1, 0, 2), C_ssm.transpose(1, 0, 2), u.transpose(1, 0, 2))
            _, y = jax.lax.scan(step, h0, xs)
            y = y.transpose(1, 0, 2) + u * Dp
            y = y * jax.nn.silu(z)
            return jnp.einsum('bld,ed->ble', y, W_out)
        h = jnp.einsum('bli,oi->blo', x, W_fc1) + b_fc1
        h = _mamba(h, W_in, conv_w, conv_b, W_xproj, W_dt, b_dt, A_log, D, W_out)
        return jnp.einsum('bld,od->blo', h, W_fc2) + b_fc2
    x = x + _L0_gnn_ref(_layernorm(x, axis=-1), L0_gnn_W, L0_gnn_a, L0_gnn_beta, adj)
    x = x + _L0_ffn_ref(_layernorm(x, axis=-1), L0_ffn_gate_w, L0_ffn_gate_b, L0_ffn_w1, L0_ffn_b1, L0_ffn_w2, L0_ffn_b2)
    x = x + _L1_gnn_ref(_layernorm(x, axis=-1), adj, L1_gnn_weight, L1_gnn_bias)
    x = x + _L1_ffn_ref(_layernorm(x, axis=-1), L1_ffn_W_fc1, L1_ffn_b_fc1, L1_ffn_W_in, L1_ffn_conv_w, L1_ffn_conv_b, L1_ffn_W_xproj, L1_ffn_W_dt, L1_ffn_b_dt, L1_ffn_A_log, L1_ffn_D, L1_ffn_W_out, L1_ffn_W_fc2, L1_ffn_b_fc2)
    return x

_drawn_inputs = setup_inputs


def setup_inputs(seed=0):
    import zlib

    import numpy as np

    out = dict(_drawn_inputs(seed))
    spreads = {'L0_ffn_gate_b': (0.0, 0.8),
     'L0_ffn_b1': (0.0, 0.8),
     'L0_ffn_b2': (0.0, 0.406),
     'L1_gnn_bias': (0.0, 0.1),
     'L1_ffn_b_fc1': (0.0, 0.1),
     'L1_ffn_conv_b': (0.0, 0.1),
     'L1_ffn_D': (1.0, 0.2),
     'L1_ffn_b_fc2': (0.0, 0.1)}
    factors = {'L0_gnn_a': 3.295, 'L0_ffn_w1': 2.792}
    for name, (base, spread) in spreads.items():
        noise = np.random.default_rng([zlib.crc32(name.encode()), seed]).standard_normal(out[name].shape)
        drawn = base * np.exp(spread * noise) if base else spread * noise
        out[name] = jnp.asarray(drawn.astype(out[name].dtype))
    for name, factor in factors.items():
        out[name] = (out[name] * factor).astype(out[name].dtype)
    return out
```

```python
from contextlib import ExitStack

import concourse.bass as bass
from concourse import mybir

F32 = mybir.dt.float32
BF16 = mybir.dt.bfloat16
I32 = mybir.dt.int32
U32 = mybir.dt.uint32
ACT = mybir.ActivationFunctionType
ALU = mybir.AluOpType
AX = mybir.AxisListType.X
P = 128


class Place:

    def __init__(self, nc, ctx, life, tag):
        self.nc, self.ctx, self.life, self.tag = nc, ctx, life, tag
        self.named = []

    def sb(self, name, shape, dt=F32):
        return self.ctx.enter_context(self.nc.sbuf_tensor(f"{self.tag}_{name}", shape, dt))

    def ps(self, name, shape, dt=F32):
        return self.ctx.enter_context(self.nc.psum_tensor(f"{self.tag}_ps_{name}", shape, dt))

    def sems(self, names):
        new = [self.life.enter_context(self.nc.semaphore(f"{self.tag}_{n}")) for n in names.split()]
        self.named += new
        return new


def clear(nc, sems):
    with nc.Block() as block:
        @block.sync
        def _(sp):
            for s in sems:
                sp.sem_clear(s)


class Chain:

    def __init__(self, eng, sem, base=0):
        self.eng, self.sem, self.base, self.n = eng, sem, base, 0

    def __call__(self, ins):
        ins.then_inc(self.sem, 1)
        self.n += 1

    def wait(self, back=0):
        if self.n > back:
            self.eng.wait_ge(self.sem, self.base + (self.n - back))


def identity(nc, pool, ident, s_ident):
    nc.gpsimd.memset(ident[:, :], 0.0).then_inc(s_ident, 1)
    pool.wait_ge(s_ident, 1)
    nc.gpsimd.affine_select(out=ident[:, :], in_=ident[:, :], compare_op=ALU.not_equal, fill=1.0, base=0,
                            pattern=[[-1, P]], channel_multiplier=1).then_inc(s_ident, 1)


def attention_phase(nc, life, dinv, x, adj, W, a, beta, gate_wT, gate_b, x1_d, xn2_d, logit_d, xg_d):
    B, N, C = x.shape
    NT = N // P
    KC = C // P
    E = gate_wT.shape[1]
    EPS = 1e-5
    SLOPE = 0.2
    ZN = 4
    ZW = xg_d.shape[0] * xg_d.shape[1] // P // ZN
    HX = C + 1
    with ExitStack() as ctx:
        m = Place(nc, ctx, life, "att")
        adj_sb = m.sb("adj", [P, NT, N])
        x_sb = m.sb("x", [P, 2, NT, C])
        w_sb = m.sb("w", [P, KC, HX])
        a_bc = m.sb("a_bc", [P, 2, C])
        wa = m.sb("wa", [P, KC, 2])
        wa2 = m.sb("wa2", [P, KC, P])
        scr = m.sb("scr", [P, C])
        beta_bc = m.sb("beta", [P, 1])
        gw = m.sb("gw", [P, KC, E])
        gb = m.sb("gb", [P, E])
        ident = m.sb("ident", [P, P])
        neghalf = m.sb("neghalf", [P, NT])
        st = m.sb("st", [P, NT, 6])
        mv = m.sb("mv", [P, NT, 2])
        ve = m.sb("ve", [P, NT])
        rstd = m.sb("rstd", [P, NT])
        xn = m.sb("xn", [P, NT, C])
        xnT = m.sb("xnT", [P, KC, N])
        h_sb = m.sb("h", [P, NT, HX])
        z = m.sb("z", [P, 2, N])
        lr = m.sb("lr", [P, N])
        e_sb = m.sb("e", [P, 2, N])
        mx = m.sb("mx", [P, 2])
        nmx = m.sb("nmx", [P, 2])
        rs = m.sb("rs", [P, 2])
        rr = m.sb("rr", [P, 2])
        pr = m.sb("pr", [P, 2, N])
        prT = m.sb("prT", [P, 2, N])
        bh = m.sb("bh", [P, 2, C])
        t_sb = m.sb("t", [P, 2, C])
        mn = m.sb("mn", [P, 2, C])
        ex = m.sb("ex", [P, 2, C])
        y_sb = m.sb("y", [P, C])
        x1 = m.sb("x1", [P, 2, C])
        st2 = m.sb("st2", [P, 2, 6])
        mv2 = m.sb("mv2", [P, 2, 2])
        ve2 = m.sb("ve2", [P, 2])
        rstd2 = m.sb("rstd2", [P, 2])
        xn2 = m.sb("xn2", [P, 2, C])
        xn2T = m.sb("xn2T", [P, 2, C])
        lg = m.sb("lg", [P, 2, E])
        deg = m.sb("deg", [P, NT])
        dpos = m.sb("dpos", [P, NT])
        dpow = m.sb("dpow", [P, NT])
        zero = m.sb("zero", [P, ZW])
        ps_s2 = m.ps("s2", [P, N])
        ps_tp = m.ps("tp", [P, 2, 512])
        ps_h = m.ps("h", [P, 2, 512])
        ps_a = m.ps("a", [P, 2, 512])

        (s_adj, s_w, s_cst, s_x0, s_x1, s_ident, s_half, s_pool, s_dve, s_act) = m.sems(
            "adj w cst x0 x1 ident half pool dve act")
        (s_wa, s_mv, s_rstd, s_xn, s_tp, s_xnT, s_h, s_hsb, s_s2) = m.sems("wa mv rstd xn tp xnT hps hsb s2ps")
        (s_z, s_e, s_pr, s_prT, s_at, s_bh, s_t, s_ex, s_x1r, s_mv2, s_rstd2, s_xn2, s_g, s_lg, s_xused) = m.sems(
            "z e pr prT at bh t ex x1r mv2 rstd2 xn2 g lg xused")
        (s_st0, s_st1, s_tick, s_ptick, s_deg, s_dpow, s_zero, s_zst) = m.sems("st0 st1 tick ptick deg dpow zero zst")
        s_xl = [s_x0, s_x1]
        s_st = [s_st0, s_st1]
        x_v = x.rearrange("b (t p) c -> b p t c", p=P)
        x1_v = x1_d.rearrange("(b t p) c -> b t p c", p=P, t=NT)
        xn2_v = xn2_d.rearrange("(b t p) c -> b t p c", p=P, t=NT)
        lg_v = logit_d.rearrange("(b t p) e -> b t p e", p=P, t=NT)
        block = ctx.enter_context(nc.Block())

        @block.sync
        def _(sp):
            sp.sem_inc(s_st0, 16)
            sp.sem_inc(s_st1, 16)
            sp.dma_start(w_sb[:, :, 0:C], W.rearrange("(k p) f -> p k f", p=P)).then_inc(s_w, 16)
            sp.dma_start(a_bc[:, :, :], a.rearrange("(h f) o -> o h f", h=2).broadcast_to([P, 2, C])).then_inc(s_w, 16)
            sp.dma_start(x_sb[:, 0], x_v[0]).then_inc(s_x0, 16)
            sp.dma_start(adj_sb[:, :, :], adj.rearrange("(t p) m -> p t m", p=P)).then_inc(s_adj, 16)
            sp.dma_start(x_sb[:, 1], x_v[1]).then_inc(s_x1, 16)
            sp.dma_start(gw[:, :, :], gate_wT.rearrange("(k p) e -> p k e", p=P)).then_inc(s_cst, 16)
            sp.dma_start(gb[:, :], gate_b.rearrange("(o e) -> o e", o=1).broadcast_to([P, E])).then_inc(s_cst, 16)
            sp.dma_start(beta_bc[:, :], beta.rearrange("(o e) -> o e", o=1).broadcast_to([P, 1])).then_inc(s_cst, 16)

            sp.wait_ge(s_zero, 1)
            for n in range(ZN):
                sp.dma_start(xg_d.rearrange("r c -> (r c)").rearrange("(n p w) -> n p w", n=ZN, p=P)[n], zero[:, :]).then_inc(s_zst, 16)

            def batch(b, pair, q, more):
                for i in range(NT):
                    sp.wait_ge(s_lg, b * NT + i + 2)
                    sp.dma_start(x1_v[bass.ds(b, 1), i].rearrange("o p c -> p (o c)"), x1[:, i % 2]).then_inc(s_st[i % 2], 16)
                    sp.dma_start(xn2_v[bass.ds(b, 1), i].rearrange("o p c -> p (o c)"), xn2[:, i % 2]).then_inc(s_st[i % 2], 16)
                    sp.dma_start(lg_v[bass.ds(b, 1), i].rearrange("o p c -> p (o c)"), lg[:, i % 2]).then_inc(s_st[i % 2], 16)
                if more:
                    sp.wait_ge(s_xused, b * NT + NT)
                    sp.dma_start(x_sb[:, q], x_v[bass.ds(b + 2, 1)].rearrange("o p t c -> p (o t) c")).then_inc(s_xl[q], 16)
            with sp.Fori(0, B // 2 - 1) as pair:
                for q in range(2):
                    batch(pair * 2 + q, pair, q, True)
            for q in range(2):
                batch(B - 2 + q, B // 2 - 1, q, False)
            sp.wait_ge(s_zst, 16 * ZN)
            for q in range(2):
                sp.wait_ge(s_st[q], 48 * B * NT // 2 + 16)

        @block.gpsimd
        def _(pool):
            identity(nc, pool, ident, s_ident)
            nc.gpsimd.memset(neghalf[:, :], -0.5).then_inc(s_half, 1)
            pool.wait_ge(s_half, 1)
            pool.wait_ge(s_deg, 1)
            nc.gpsimd.tensor_tensor(dpow[:, :], deg[:, :], neghalf[:, :], ALU.pow).then_inc(s_dpow, 1)
            with pool.Fori(0, B) as b:
                pool.wait_ge(s_mv, b + 1)
                pool.sem_inc(s_ptick, 1)
                nc.gpsimd.tensor_scalar(ve[:, :], mv[:, :, 1], EPS, None, ALU.add).then_inc(s_pool, 1)
                pool.wait_ge(s_pool, b * (NT + 1) + 1)
                nc.gpsimd.tensor_tensor(rstd[:, :], ve[:, :], neghalf[:, :], ALU.pow).then_inc(s_rstd, 1)
                for i in range(NT):
                    s = i % 2
                    pool.wait_ge(s_mv2, b * NT + i + 1)
                    pool.sem_inc(s_ptick, 1)
                    nc.gpsimd.tensor_scalar(ve2[:, s:s + 1], mv2[:, s, 1:2], EPS, None, ALU.add).then_inc(s_pool, 1)
                    pool.wait_ge(s_pool, b * (NT + 1) + i + 2)
                    nc.gpsimd.tensor_tensor(rstd2[:, s:s + 1], ve2[:, s:s + 1], neghalf[:, 0:1], ALU.pow).then_inc(s_rstd2, 1)

        TPB = 4 + 2 * NT

        @block.tensor
        def _(pe):
            pe.sem_inc(s_at, 2)
            pe.wait_ge(s_ident, 2)
            pe.wait_ge(s_wa, 3)
            with pe.Fori(0, B) as b:
                pe.wait_ge(s_xn, b + 1)
                for n in range(4):
                    k, hf = n // 2, n % 2
                    if n < 2:
                        pe.wait_ge(s_prT, b * NT * 2 + 2)
                    else:
                        pe.wait_ge(s_xnT, b * 4 + n - 1)
                    for j in range(4):
                        i = hf * 4 + j
                        last = nc.tensor.transpose(ps_tp[:, n % 2, j * P:j * P + P], xn[:, i, k * P:k * P + P], ident[:, :])
                    last.then_inc(s_tp, 1)
                pe.wait_ge(s_xnT, b * 4 + 4)
                for i in range(NT):
                    pe.wait_ge(s_hsb, b * NT + i + 1)
                    for k in range(KC):
                        last = nc.tensor.matmul(ps_h[:, i % 2, 0:HX], xnT[:, k, i * P:i * P + P], w_sb[:, k, :],
                                                start=(k == 0), stop=(k == KC - 1))
                    last.then_inc(s_h, 1)
                pe.wait_ge(s_z, b * NT + 2)
                for hf in range(2):
                    for k in range(KC):
                        last = nc.tensor.matmul(ps_s2[:, hf * 512:hf * 512 + 512], wa2[:, k, :],
                                                xnT[:, k, hf * 512:hf * 512 + 512], start=(k == 0), stop=(k == KC - 1))
                last.then_inc(s_s2, 1)
                pe.wait_ge(s_hsb, b * NT + NT + 2)
                for i in range(NT + 2):
                    if i < NT:
                        s = i % 2
                        pe.wait_ge(s_pr, b * NT + i + 3)
                        for hf in range(2):
                            pe.wait_ge(s_prT, (b * NT + i) * 2 + hf + 1)
                            for j in range(4):
                                jj = hf * 4 + j
                                last = nc.tensor.transpose(ps_tp[:, hf, j * P:j * P + P],
                                                           pr[:, s, jj * P:jj * P + P], ident[:, :])
                            last.then_inc(s_tp, 1)
                    if 1 <= i < NT + 1:
                        o = i - 1
                        s = o % 2
                        pe.wait_ge(s_prT, (b * NT + o) * 2 + 4)
                        pe.wait_ge(s_t, b * NT + o + 1)
                        for j in range(NT):
                            last = nc.tensor.matmul(ps_a[:, s, 0:C], prT[:, s, j * P:j * P + P], h_sb[:, j, 0:C],
                                                    start=(j == 0), stop=(j == NT - 1))
                        last.then_inc(s_at, 1)
                    if 2 <= i:
                        o = i - 2
                        s = o % 2
                        pe.wait_ge(s_xn2, b * NT + o + 1)
                        for k in range(KC):
                            last = nc.tensor.transpose(ps_h[:, 0, k * P:k * P + P], xn2[:, s, k * P:k * P + P], ident[:, :])
                        last.then_inc(s_g, 1)
                        pe.wait_ge(s_act, b * NT + o + 1)
                        pe.wait_ge(s_lg, b * NT + o + 1)
                        for k in range(KC):
                            last = nc.tensor.matmul(ps_h[:, 1, 0:E], xn2T[:, s, k * P:k * P + P], gw[:, k, :],
                                                    start=(k == 0), stop=(k == KC - 1))
                        last.then_inc(s_g, 1)
                pe.wait_ge(s_lg, b * NT + NT + 1)

        @block.scalar
        def _(act):
            act.sem_inc(s_hsb, 2)
            act.sem_inc(s_z, 2)
            act.sem_inc(s_pr, 2)
            act.sem_inc(s_prT, 2)
            with act.Fori(0, B) as b:
                for n in range(4):
                    act.wait_ge(s_tp, b * TPB + n + 1)
                    nc.scalar.activation(xnT[:, n // 2, (n % 2) * 512:(n % 2) * 512 + 512], ps_tp[:, n % 2, :],
                                         ACT.Copy).then_inc(s_xnT, 1)
                for i in range(NT):
                    act.wait_ge(s_h, b * NT + i + 1)
                    nc.scalar.activation(h_sb[:, i, :], ps_h[:, i % 2, 0:HX], ACT.Copy).then_inc(s_hsb, 1)
                act.wait_ge(s_s2, b + 1)
                act.wait_ge(s_hsb, b * NT + NT + 2)

                def scores(i):
                    act.wait_ge(s_e, b * NT + i + 1)
                    nc.scalar.activation(z[:, i % 2, :], ps_s2[:, :], ACT.Identity, bias=h_sb[:, i, C:C + 1]).then_inc(s_z, 1)

                scores(0)
                scores(1)
                for i in range(NT + 2):
                    if i < NT:
                        s = i % 2
                        act.wait_ge(s_e, b * NT + i + 3)
                        act.wait_ge(s_tp, b * TPB + 4 + 2 * i - 2)
                        nc.scalar.activation(pr[:, s, :], e_sb[:, s, :], ACT.Exp, bias=nmx[:, s:s + 1],
                                             accum_out=rs[:, s:s + 1]).then_inc(s_pr, 1)
                        if i + 2 < NT:
                            scores(i + 2)
                        act.wait_ge(s_at, b * NT + i + 1)
                        for hf in range(2):
                            act.wait_ge(s_tp, b * TPB + 4 + 2 * i + hf + 1)
                            nc.scalar.activation(prT[:, s, hf * 512:hf * 512 + 512], ps_tp[:, hf, :], ACT.Copy).then_inc(s_prT, 1)
                    if 1 <= i < NT + 1:
                        o = i - 1
                        act.wait_ge(s_t, b * NT + o + 3)
                        nc.scalar.activation(ex[:, o % 2, :], mn[:, o % 2, :], ACT.Exp).then_inc(s_ex, 1)
                    if 2 <= i:
                        o = i - 2
                        act.wait_ge(s_g, (b * NT + o) * 2 + 1)
                        nc.scalar.activation(xn2T[:, o % 2, :], ps_h[:, 0, 0:C], ACT.Copy).then_inc(s_act, 1)

        @block.vector
        def _(dve):
            dve.sem_inc(s_e, 2)
            dve.sem_inc(s_t, 2)
            dve.sem_inc(s_lg, 1)
            nc.vector.memset(zero[:, :], 0.0).then_inc(s_zero, 1)
            own = Chain(dve, s_dve)
            dve.wait_ge(s_w, 32)
            for k in range(KC):
                for j in range(2):
                    own(nc.vector.tensor_tensor_reduce(out=scr[:, :], in0=w_sb[:, k, 0:C], in1=a_bc[:, j, :], scale=1.0,
                                                       scalar=0.0, op0=ALU.mult, op1=ALU.add, accum_out=wa[:, k, j:j + 1]))
                    own.wait()
            nc.vector.tensor_copy(w_sb[:, :, C:C + 1], wa[:, :, 0:1]).then_inc(s_wa, 1)
            for k in range(KC):
                nc.vector.tensor_copy(wa2[:, k, :], wa[:, k, 1:2].to_broadcast([P, P])).then_inc(s_wa, 1)
            dve.wait_ge(s_adj, 16)
            own(nc.vector.tensor_reduce(deg[:, :], adj_sb[:, :, :], AX, ALU.add))
            own.wait()
            own(nc.vector.tensor_scalar(dpos[:, :], deg[:, :], 0.0, None, ALU.is_gt))
            own.wait()
            nc.vector.tensor_scalar(deg[:, :], deg[:, :], 1e-37, None, ALU.max).then_inc(s_deg, 1)
            dve.wait_ge(s_dpow, 1)
            own(nc.vector.tensor_tensor(dinv[:, :], dpow[:, :], dpos[:, :], ALU.mult))
            dve.wait_ge(s_cst, 48)
            pre = own.n

            def batch(b, q, steps):
                ch = Chain(dve, s_dve, b * steps + pre)
                dve.wait_ge(s_xl[q], (b - q) * 8 + 16)
                for i in range(NT):
                    ch(nc.vector.bn_stats(st[:, i, :], x_sb[:, q, i, :]))
                ch.wait()
                dve.sem_inc(s_tick, 1)
                for i in range(NT):
                    last = nc.vector.bn_aggr(mv[:, i, :], st[:, i, :])
                last.then_inc(s_mv, 1)
                dve.wait_ge(s_mv, b + 1)
                dve.wait_ge(s_rstd, b + 1)
                dve.wait_ge(s_lg, b * NT + 1)
                for i in range(NT):
                    last = nc.vector.tensor_scalar(xn[:, i, :], x_sb[:, q, i, :], mv[:, i, 0:1], rstd[:, i:i + 1],
                                                   ALU.subtract, ALU.mult)
                last.then_inc(s_xn, 1)

                def leaky(i):
                    s = i % 2
                    dve.wait_ge(s_z, b * NT + i + 3)
                    ch(nc.vector.scalar_tensor_tensor(out=lr[:, :], in0=z[:, s, :], scalar=SLOPE, in1=z[:, s, :],
                                                      op0=ALU.mult, op1=ALU.max))
                    ch.wait()
                    dve.wait_ge(s_pr, b * NT + i + 1)
                    dve.sem_inc(s_tick, 1)
                    ch(nc.vector.tensor_tensor_reduce(out=e_sb[:, s, :], in0=lr[:, :], in1=adj_sb[:, i, :], scale=1.0,
                                                      scalar=-3.0e38, op0=ALU.mult, op1=ALU.max, accum_out=mx[:, s:s + 1]))
                    ch.wait()
                    nc.vector.tensor_scalar(nmx[:, s:s + 1], mx[:, s:s + 1], -1.0, None, ALU.mult).then_inc(s_e, 1)

                leaky(0)
                for i in range(NT + 2):
                    if i + 1 < NT:
                        leaky(i + 1)
                    if 1 <= i < NT + 1:
                        o = i - 1
                        s = o % 2
                        dve.wait_ge(s_pr, b * NT + o + 3)
                        dve.wait_ge(s_hsb, b * NT + NT + 2)
                        ch(nc.vector.reciprocal(rr[:, s:s + 1], rs[:, s:s + 1]))
                        ch(nc.vector.tensor_scalar(bh[:, s, :], h_sb[:, o, 0:C], beta_bc[:, 0:1], None, ALU.mult))
                        ch.wait()
                        dve.wait_ge(s_at, b * NT + o + 3)
                        ch(nc.vector.scalar_tensor_tensor(out=t_sb[:, s, :], in0=ps_a[:, s, 0:C], scalar=rr[:, s:s + 1],
                                                          in1=bh[:, s, :], op0=ALU.mult, op1=ALU.add))
                        ch.wait()
                        nc.vector.tensor_scalar(mn[:, s, :], t_sb[:, s, :], 0.0, None, ALU.min).then_inc(s_t, 1)
                        dve.wait_ge(s_ex, b * NT + o + 1)
                        ch(nc.vector.scalar_tensor_tensor(out=y_sb[:, :], in0=t_sb[:, s, :], scalar=0.0, in1=ex[:, s, :],
                                                          op0=ALU.max, op1=ALU.add))
                        ch.wait()
                        dve.wait_ge(s_st[s], (b * NT + o - s) * 24 + 16)
                        nc.vector.scalar_tensor_tensor(out=x1[:, s, :], in0=y_sb[:, :], scalar=-1.0, in1=x_sb[:, q, o, :],
                                                       op0=ALU.add, op1=ALU.add).then_inc(s_xused, 1)
                        dve.wait_ge(s_xused, b * NT + o + 1)
                        ch(nc.vector.bn_stats(st2[:, s, :], x1[:, s, :]))
                        ch.wait()
                        dve.sem_inc(s_tick, 1)
                        nc.vector.bn_aggr(mv2[:, s, :], st2[:, s, :]).then_inc(s_mv2, 1)
                        dve.wait_ge(s_mv2, b * NT + o + 1)
                        dve.wait_ge(s_rstd2, b * NT + o + 1)
                        nc.vector.tensor_scalar(xn2[:, s, :], x1[:, s, :], mv2[:, s, 0:1], rstd2[:, s:s + 1],
                                                ALU.subtract, ALU.mult).then_inc(s_xn2, 1)
                    if 2 <= i:
                        o = i - 2
                        dve.wait_ge(s_g, (b * NT + o) * 2 + 2)
                        nc.vector.tensor_tensor(lg[:, o % 2, :], ps_h[:, 1, 0:E], gb[:, :], ALU.add).then_inc(s_lg, 1)
                return ch.n

            steps = NT + 2 * NT + 5 * NT
            with dve.Fori(0, B // 2) as pair:
                for q in range(2):
                    assert batch(pair * 2 + q, q, steps) == steps
    return m.named


def routing_phase(nc, life, keep, consts, logit_d, xn2_d, xg_d, CAP):
    gidx, wk = keep
    T, E = logit_d.shape
    C = xn2_d.shape[1]
    NT = T // P
    CH = P // E
    BIG = float(2 * E * CAP)
    EXPS = [float(2.0 ** (2 ** k)) for k in range(6, -1, -1)] + [1.0]
    with ExitStack() as ctx:
        m = Place(nc, ctx, life, "rt")
        rows = m.sb("rows", [P, NT, C])
        cst = m.sb("cst", [P, 2 * P + 3 * E])
        blk, tri, ecap, rev, sel = (cst[:, 0:P], cst[:, P:2 * P], cst[:, 2 * P:2 * P + E], cst[:, 2 * P + E:2 * P + 2 * E],
                                    cst[:, 2 * P + 2 * E:2 * P + 3 * E])
        ones = m.sb("ones", [P, P])
        lg = m.sb("lg", [P, NT, E])
        pb = m.sb("pb", [P, NT, E])
        oh = m.sb("oh", [P, 2, NT, E])
        t0 = m.sb("t0", [P, NT, E])
        t1 = m.sb("t1", [P, NT, E])
        r0 = m.sb("r0", [P, NT])
        p12 = m.sb("p12", [P, 2, NT])
        v = m.sb("v", [P, E, NT])
        vc = m.sb("vc", [P, T // CH])
        cmp = m.sb("cmp", [P, T // CH])
        cnt = m.sb("cnt", [P, 1])
        g = m.sb("g", [P, 1])
        cand = m.sb("cand", [P, 1])
        delta = m.sb("delta", [P, 1])
        thr8 = m.sb("thr8", [P, E])
        thr = m.sb("thr", [P, E])
        gt = m.sb("gt", [P, E, NT])
        eq = m.sb("eq", [P, E, NT])
        inc = m.sb("inc", [P, E, NT])
        zero = m.sb("zero", [P, NT])
        room = m.sb("room", [P, E])
        kp = m.sb("kp", [P, E, NT])
        pos = m.sb("pos", [P, E, NT])
        s_k = m.sb("s_k", [P, 2, NT])
        kept = m.sb("kept", [P, 2, NT])
        sf = m.sb("sf", [P, 2, NT])
        sidx = m.sb("sidx", [P, 2, NT], I32)
        ps_c = m.ps("c", [P, 512])
        ps_g = m.ps("g", [P, 512])
        ps_i = m.ps("i", [P, E * NT])
        ps_t = m.ps("t", [P, E * NT])
        (s_in, s_rows, s_dve, s_act, s_v, s_vc, s_vr, s_cnt, s_tot, s_thr, s_m, s_pm, s_sidx, s_sc, s_sub) = m.sems(
            "in rows dve act v vc vr cnt tot thr m pm sidx sc sub")
        v_d = nc.dram_tensor("rt_v_dram", (E, P, NT), F32, kind="Internal").ap()
        block = ctx.enter_context(nc.Block())
        NI = len(EXPS) - 1
        NM = 23

        @block.sync
        def _(sp):
            sp.dma_start(lg[:, :, :], logit_d.rearrange("(t p) e -> p t e", p=P)).then_inc(s_in, 16)
            sp.dma_start(cst[:, :], consts).then_inc(s_in, 16)
            sp.dma_start(rows[:, :, :], xn2_d.rearrange("(t p) c -> p t c", p=P)).then_inc(s_rows, 16)
            sp.wait_ge(s_v, 1)
            sp.dma_start(v_d.rearrange("e p t -> p e t"), v[:, :, :]).then_inc(s_vc, 16)
            sp.wait_ge(s_vc, 16)
            sp.dma_start(vc[:, :], v_d.rearrange("e (c q) t -> (e c) (q t)", c=CH)).then_inc(s_vr, 16)
            sp.wait_ge(s_vr, 16)

        @block.scalar
        def _(act):
            act.wait_ge(s_sub, 1)
            nc.scalar.activation(t1[:, :, :], t0[:, :, :], ACT.Exp).then_inc(s_act, 1)

        @block.tensor
        def _(pe):
            pe.wait_ge(s_in, 32)
            for n in range(NI):
                pe.wait_ge(s_cnt, n + 1)
                nc.tensor.matmul(ps_c[:, 0:1], blk, cnt[:, :], start=True, stop=True).then_inc(s_tot, 1)
            with pe.Fori(0, NM) as n:
                pe.wait_ge(s_cnt, n + NI + 1)
                nc.tensor.matmul(ps_c[:, 0:1], blk, cnt[:, :], start=True, stop=True).then_inc(s_tot, 1)
            pe.wait_ge(s_thr, 1)
            nc.tensor.matmul(ps_g[:, 0:E], ones[:, :], thr8[:, :], start=True, stop=True).then_inc(s_tot, 1)
            pe.wait_ge(s_m, 1)
            nc.tensor.matmul(ps_c[:, :], ones[:, :], gt[:, :, :].rearrange("p e t -> p (e t)"), start=True, stop=True)
            nc.tensor.matmul(ps_i[:, :], tri, eq[:, :, :].rearrange("p e t -> p (e t)"), start=True, stop=True)
            nc.tensor.matmul(ps_t[:, :], ones[:, :], eq[:, :, :].rearrange("p e t -> p (e t)"), start=True,
                             stop=True).then_inc(s_pm, 1)
            pe.wait_ge(s_m, 2)
            nc.tensor.matmul(ps_i[:, :], tri, kp[:, :, :].rearrange("p e t -> p (e t)"), start=True, stop=True)
            nc.tensor.matmul(ps_t[:, :], ones[:, :], kp[:, :, :].rearrange("p e t -> p (e t)"), start=True,
                             stop=True).then_inc(s_pm, 1)

        @block.gpsimd
        def _(pool):
            pool.wait_ge(s_sidx, 1)
            pool.wait_ge(s_rows, 16)
            for t in range(NT):
                for k in range(2):
                    pool.indirect_dma_start(out=xg_d, out_offset=bass.IndirectOffsetOnAxis(ap=sidx[:, k, t:t + 1], axis=0),
                                            in_=rows[:, t, :], in_offset=None, bounds_check=E * CAP - 1,
                                            oob_is_err=False).then_inc(s_sc, 16)
            pool.wait_ge(s_sc, 16 * 2 * NT)

        @block.vector
        def _(dve):
            own = Chain(dve, s_dve)
            V = nc.vector

            def do(ins):
                own(ins)
                own.wait()

            do(V.memset(ones[:, :], 1.0))
            do(V.memset(zero[:, :], 0.0))
            do(V.memset(cand[:, :], float(2.0 ** -126 * EXPS[0])))
            dve.wait_ge(s_in, 32)
            bc = lambda a: a.unsqueeze(2).broadcast_to([P, NT, E])
            do(V.tensor_reduce(r0[:, :], lg[:, :, :], AX, ALU.max))
            V.tensor_tensor(t0[:, :, :], lg[:, :, :], bc(r0[:, :]), ALU.subtract).then_inc(s_sub, 1)
            dve.wait_ge(s_act, 1)
            do(V.tensor_reduce(r0[:, :], t1[:, :, :], AX, ALU.add))
            do(V.reciprocal(r0[:, :], r0[:, :]))
            do(V.tensor_tensor(pb[:, :, :], t1[:, :, :], bc(r0[:, :]), ALU.mult))
            revb = rev.unsqueeze(1).broadcast_to([P, NT, E])
            for k in range(2):
                src = pb if k == 0 else t1
                do(V.tensor_reduce(p12[:, k, :], src[:, :, :], AX, ALU.max))
                do(V.tensor_tensor(t0[:, :, :], src[:, :, :], bc(p12[:, k, :]), ALU.is_equal))
                do(V.tensor_tensor(t0[:, :, :], t0[:, :, :], revb, ALU.mult))
                do(V.tensor_reduce(r0[:, :], t0[:, :, :], AX, ALU.max))
                do(V.tensor_tensor(oh[:, k], t0[:, :, :], bc(r0[:, :]), ALU.is_equal))
                if k == 0:
                    do(V.scalar_tensor_tensor(out=t1[:, :, :], in0=oh[:, 0], scalar=-2.0, in1=pb[:, :, :],
                                              op0=ALU.mult, op1=ALU.add))
            do(V.tensor_tensor(t0[:, :, :], oh[:, 0], oh[:, 1], ALU.add))
            V.tensor_tensor(v[:, :, :].rearrange("p e t -> p t e"), t0[:, :, :], pb[:, :, :], ALU.mult).then_inc(s_v, 1)
            dve.wait_ge(s_v, 1)
            dve.wait_ge(s_vr, 16)

            def count(tick):
                do(V.tensor_scalar(cmp[:, :], vc[:, :], cand[:, 0:1], None, ALU.is_ge))
                V.tensor_reduce(cnt[:, :], cmp[:, :], AX, ALU.add).then_inc(s_cnt, 1)
                dve.wait_ge(s_tot, tick)

            for n in range(NI):
                nxt, r = EXPS[n + 1], EXPS[n + 1] / EXPS[n]
                count(n + 1)
                do(V.tensor_scalar(g[:, :], ps_c[:, 0:1], float(CAP), nxt - r, ALU.is_ge, ALU.mult))
                do(V.scalar_tensor_tensor(out=cand[:, :], in0=g[:, :], scalar=r, in1=cand[:, :], op0=ALU.add, op1=ALU.mult))
            do(V.tensor_scalar(delta[:, :], cand[:, :], 0.5, None, ALU.mult))
            do(V.tensor_tensor(cand[:, :], cand[:, :], delta[:, :], ALU.add))
            at = own.n
            with dve.Fori(0, NM - 1) as n:
                own = Chain(dve, s_dve, n * 5 + at)
                do(V.tensor_scalar(cmp[:, :], vc[:, :], cand[:, 0:1], None, ALU.is_ge))
                V.tensor_reduce(cnt[:, :], cmp[:, :], AX, ALU.add).then_inc(s_cnt, 1)
                dve.wait_ge(s_tot, n + NI + 1)
                do(V.tensor_scalar(g[:, :], ps_c[:, 0:1], float(CAP), 0.5, ALU.is_ge, ALU.subtract))
                do(V.tensor_tensor(g[:, :], g[:, :], delta[:, :], ALU.mult))
                do(V.tensor_tensor(cand[:, :], cand[:, :], g[:, :], ALU.add))
                do(V.tensor_scalar(delta[:, :], delta[:, :], 0.5, None, ALU.mult))
            own = Chain(dve, s_dve)
            own.n = at + 5 * (NM - 1)
            count(NI + NM)
            do(V.tensor_scalar(g[:, :], ps_c[:, 0:1], float(CAP), 1.0, ALU.is_ge, ALU.subtract))
            do(V.tensor_tensor(g[:, :], g[:, :], delta[:, :], ALU.mult))
            do(V.tensor_tensor(cand[:, :], cand[:, :], g[:, :], ALU.add))
            V.tensor_scalar(thr8[:, :], sel, cand[:, 0:1], None, ALU.mult).then_inc(s_thr, 1)
            dve.wait_ge(s_tot, NI + NM + 1)
            do(V.tensor_copy(thr[:, :], ps_g[:, 0:E]))
            thrb = thr[:, :].unsqueeze(2).broadcast_to([P, E, NT])
            do(V.tensor_tensor(gt[:, :, :], v[:, :, :], thrb, ALU.is_gt))
            V.tensor_tensor(eq[:, :, :], v[:, :, :], thrb, ALU.is_equal).then_inc(s_m, 1)

            def prefix():
                for e in range(E):
                    own(V.tensor_tensor_scan(out=inc[:, e, :], data0=ps_t[:, e * NT:(e + 1) * NT], data1=zero[:, :],
                                             initial=0.0, op0=ALU.add, op1=ALU.add))
                own.wait()
                do(V.tensor_tensor(pos[:, :, :].rearrange("p e t -> p (e t)"), inc[:, :, :].rearrange("p e t -> p (e t)"),
                                   ps_t[:, :], ALU.subtract))
                do(V.tensor_tensor(pos[:, :, :].rearrange("p e t -> p (e t)"), pos[:, :, :].rearrange("p e t -> p (e t)"),
                                   ps_i[:, :], ALU.add))

            dve.wait_ge(s_pm, 1)
            do(V.tensor_reduce(room[:, :], ps_c[:, :].rearrange("p (e t) -> p e t", e=E), AX, ALU.add))
            do(V.tensor_scalar(room[:, :], room[:, :], -1.0, float(CAP), ALU.mult, ALU.add))
            prefix()
            do(V.tensor_tensor(kp[:, :, :], pos[:, :, :], room[:, :].unsqueeze(2).broadcast_to([P, E, NT]), ALU.is_lt))
            do(V.tensor_tensor(kp[:, :, :], kp[:, :, :], eq[:, :, :], ALU.mult))
            V.tensor_tensor(kp[:, :, :], kp[:, :, :], gt[:, :, :], ALU.add).then_inc(s_m, 1)
            dve.wait_ge(s_pm, 2)
            prefix()
            do(V.tensor_tensor(pos[:, :, :], pos[:, :, :], ecap.unsqueeze(2).broadcast_to([P, E, NT]), ALU.add))
            for k in range(2):
                for src, dst in ((pos, s_k), (kp, kept)):
                    do(V.tensor_tensor(t0[:, :, :], oh[:, k], src[:, :, :].rearrange("p e t -> p t e"), ALU.mult))
                    do(V.tensor_reduce(dst[:, k, :], t0[:, :, :], AX, ALU.add))
            own(V.tensor_tensor(wk[:, :, :], kept[:, :, :], p12[:, :, :], ALU.mult))
            own(V.tensor_tensor(gidx[:, :, :], kept[:, :, :], s_k[:, :, :], ALU.mult))
            do(V.tensor_scalar(sf[:, :, :], kept[:, :, :], -BIG, BIG, ALU.mult, ALU.add))
            V.tensor_tensor(sidx[:, :, :], sf[:, :, :], s_k[:, :, :], ALU.add).then_inc(s_sidx, 1)


def experts_phase(nc, life, xg_d, w1, b1T, w2, b2, y_d, CAP):
    E, C, H = w1.shape
    KC, KH = C // P, H // P
    NR = -(-CAP // P)
    FULL = CAP // P
    TAIL = CAP - FULL * P
    NCH = 4
    CW = CAP // NCH
    assert CAP % NCH == 0 and CW <= 512 and TAIL
    with ExitStack() as ctx:
        m = Place(nc, ctx, life, "ex")
        xg = m.sb("xg", [P, 2, NR, C])
        xgT = m.sb("xgT", [P, KC, CAP])
        w1s = m.sb("w1", [P, 2, KC, H])
        w2s = m.sb("w2", [P, 2, KH, C])
        b1s = m.sb("b1", [P, KH, E])
        b1c = m.sb("b1c", [P, KH])
        b2s = m.sb("b2", [P, E, C])
        hT = m.sb("hT", [P, KH, CAP])
        o_sb = m.sb("o", [P, 4, C])
        ident = m.sb("ident", [P, P])
        ps1 = m.ps("1", [P, 4, 512])
        ps2 = m.ps("2", [P, 2, 512])
        ps_tp = m.ps("tp", [P, 2, 512])
        (s_id, s_w0, s_w1, s_b, s_x0, s_x1, s_tp, s_xT, s_p1, s_h, s_p2, s_o, s_y0, s_y1, s_y2, s_y3, s_bc, s_tick) = m.sems(
            "id w0 w1 b x0 x1 tp xT p1 h p2 o y0 y1 y2 y3 bc tick")
        s_w, s_x, s_y = [s_w0, s_w1], [s_x0, s_x1], [s_y0, s_y1, s_y2, s_y3]
        block = ctx.enter_context(nc.Block())
        size = lambda r: P if r < FULL else TAIL
        w1_v = w1.rearrange("e (k p) h -> e p k h", p=P)
        w2_v = w2.rearrange("e (k p) d -> e p k d", p=P)
        xg_v = xg_d.rearrange("(e r) c -> e r c", e=E)
        y_v = y_d.rearrange("(e r) c -> e r c", e=E)
        one = "o a b c -> a (o b) c"

        @block.sync
        def _(sp):
            for q in range(4):
                sp.sem_inc(s_y[q], 16)
            sp.dma_start(b1s[:, :, :], b1T.rearrange("(j p) e -> p j e", p=P)).then_inc(s_b, 16)
            sp.dma_start(b2s[:, :, :], b2.rearrange("(o e) d -> o e d", o=1).broadcast_to([P, E, C])).then_inc(s_b, 16)

            def load(e, q):
                sp.dma_start(xg[:, q, 0:FULL, :], xg_v[bass.ds(e, 1), 0:FULL * P].rearrange("o (r p) c -> p (o r) c", p=P)).then_inc(s_x[q], 16)
                sp.dma_start(xg[0:TAIL, q, FULL, :], xg_v[bass.ds(e, 1), FULL * P:CAP].rearrange("o r c -> r (o c)")).then_inc(s_x[q], 16)
                sp.dma_start(w1s[:, q], w1_v[bass.ds(e, 1)].rearrange("o p k h -> p (o k) h")).then_inc(s_w[q], 16)
                sp.dma_start(w2s[:, q], w2_v[bass.ds(e, 1)].rearrange("o p k h -> p (o k) h")).then_inc(s_w[q], 16)

            load(0, 0)
            load(1, 1)

            def expert(e, q, more):
                for r in range(NR):
                    sp.wait_ge(s_o, e * NR + r + 3)
                    sp.dma_start(y_v[bass.ds(e, 1), r * P:r * P + size(r)].rearrange("o r c -> r (o c)"),
                                 o_sb[0:size(r), (q * NR + r) % 4, :]).then_inc(s_y[(q * NR + r) % 4], 16)
                if more:
                    sp.wait_ge(s_p2, e * NR + NR)
                    load(e + 2, q)
            with sp.Fori(0, E // 2 - 1) as pair:
                for q in range(2):
                    expert(pair * 2 + q, q, True)
            for q in range(2):
                expert(E - 2 + q, q, False)
            for q in range(4):
                sp.wait_ge(s_y[q], 16 + 16 * (E * NR // 4))

        @block.gpsimd
        def _(pool):
            identity(nc, pool, ident, s_id)

        @block.tensor
        def _(pe):
            pe.wait_ge(s_id, 2)

            def turn(e, q):
                pe.wait_ge(s_x[q], (e - q) * 16 + 32)
                for r in range(NR):
                    n = size(r)
                    pe.wait_ge(s_xT, e * NR + r + 1)
                    for k in range(KC):
                        last = nc.tensor.transpose(ps_tp[:, r % 2, k * P:k * P + n], xg[0:n, q, r, k * P:k * P + P], ident[0:n, 0:n])
                    last.then_inc(s_tp, 1)

            def first(e, q):
                pe.wait_ge(s_w[q], (e - q) * 16 + 32)
                pe.wait_ge(s_xT, e * NR + NR + 2)
                for j in range(KH):
                    for n in range(NCH):
                        pe.wait_ge(s_h, (e * KH + j) * NCH + n + 1)
                        for k in range(KC):
                            last = nc.tensor.matmul(ps1[:, n, 0:CW], w1s[:, q, k, j * P:j * P + P], xgT[:, k, n * CW:(n + 1) * CW],
                                                    start=(k == 0), stop=(k == KC - 1))
                        last.then_inc(s_p1, 1)

            def second(e, q):
                pe.wait_ge(s_h, (e * KH + KH) * NCH + 4)
                for r in range(NR):
                    n = size(r)
                    pe.wait_ge(s_o, e * NR + r + 1)
                    for j in range(KH):
                        last = nc.tensor.matmul(ps2[0:n, r % 2, 0:C], hT[:, j, r * P:r * P + n], w2s[:, q, j, :],
                                                start=(j == 0), stop=(j == KH - 1))
                    last.then_inc(s_p2, 1)

            turn(0, 0)
            with pe.Fori(0, E // 2 - 1) as pair:
                for q in range(2):
                    first(pair * 2 + q, q)
                    turn(pair * 2 + q + 1, 1 - q)
                    second(pair * 2 + q, q)
            first(E - 2, 0)
            turn(E - 1, 1)
            second(E - 2, 0)
            first(E - 1, 1)
            second(E - 1, 1)

        @block.scalar
        def _(act):
            act.sem_inc(s_h, 4)
            act.wait_ge(s_b, 32)

            with act.Fori(0, E) as e:
                act.wait_ge(s_h, e * KH * NCH + 4)
                act.sem_inc(s_tick, 1)
                nc.scalar.activation(b1c[:, :], b1s[:, :, bass.ds(e, 1)].rearrange("p j o -> p (j o)"), ACT.Copy).then_inc(s_bc, 1)
                act.wait_ge(s_bc, e + 1)
                for j in range(KH):
                    for n in range(NCH):
                        act.wait_ge(s_p1, (e * KH + j) * NCH + n + 1)
                        nc.scalar.activation(hT[:, j, n * CW:(n + 1) * CW], ps1[:, n, 0:CW], ACT.Gelu,
                                             bias=b1c[:, j:j + 1]).then_inc(s_h, 1)

        @block.vector
        def _(dve):
            dve.sem_inc(s_xT, 2)
            dve.sem_inc(s_o, 2)

            def turned(e):
                for r in range(NR):
                    n = size(r)
                    dve.wait_ge(s_tp, e * NR + r + 1)
                    nc.vector.tensor_copy(xgT[:, :, r * P:r * P + n],
                                          ps_tp[:, r % 2, 0:KC * P].rearrange("p (k n) -> p k n", k=KC)[:, :, 0:n]).then_inc(s_xT, 1)

            def results(pair, q):
                e = pair * 2 + q
                for r in range(NR):
                    n, i = size(r), q * NR + r
                    dve.wait_ge(s_y[i % 4], pair * (32 * NR // 4) + 16 * (i // 4 + 1))
                    dve.wait_ge(s_p2, e * NR + r + 1)
                    nc.vector.tensor_tensor(o_sb[0:n, i % 4, :], ps2[0:n, r % 2, 0:C],
                                            b2s[0:n, bass.ds(e, 1), :].rearrange("p o d -> p (o d)"), ALU.add).then_inc(s_o, 1)

            dve.wait_ge(s_b, 32)
            turned(0)
            with dve.Fori(0, E // 2 - 1) as pair:
                for q in range(2):
                    turned(pair * 2 + q + 1)
                    results(pair, q)
            turned(E - 1)
            results(E // 2 - 1, 0)
            results(E // 2 - 1, 1)


def graph_phase(nc, life, keep, dinv, x1_d, y_d, adjT, weight, bias, x3_d, xn4T_d):
    gidx, wk = keep
    N = adjT.shape[0]
    T, C = x1_d.shape
    NT = N // P
    KC = C // P
    NP2 = T // N // 2
    TP = 2 * NT
    EPS = 1e-5
    with ExitStack() as ctx:
        m = Place(nc, ctx, life, "gr")
        aT = m.sb("aT", [P, NT, N])
        w_sb = m.sb("w", [P, KC, C])
        bias_bc = m.sb("bias", [P, C])
        ident = m.sb("ident", [P, P])
        neghalf = m.sb("neghalf", [P, 1])
        x1s = m.sb("x1", [P, 2, TP, C])
        gi = m.sb("gi", [P, 2, TP], I32)
        wt = m.sb("wt", [P, 2, TP])
        gat = m.sb("gat", [P, 4, 2, C])
        ta = m.sb("ta", [P, 2, C])
        x2 = m.sb("x2", [P, 2, C])
        x2b = m.sb("x2b", [P, TP, C])
        st = m.sb("st", [P, 2, 6])
        mv = m.sb("mv", [P, 2, 2])
        ve = m.sb("ve", [P, 2])
        rstd = m.sb("rstd", [P, 2])
        xn = m.sb("xn", [P, 2, C])
        xnT = m.sb("xnT", [P, 2, C])
        sup = m.sb("sup", [P, NT, 2, C])
        x3 = m.sb("x3", [P, 2, 2, C])
        xn4 = m.sb("xn4", [P, 2, C])
        xT4 = m.sb("xT4", [P, 4, C])
        ps_tp = m.ps("tp", [P, 2, 512])
        ps_s = m.ps("s", [P, 2, 512])
        ps_o = m.ps("o", [P, 2, 512])
        (s_c, s_id, s_x0, s_x1, s_gi, s_g0, s_g1, s_g2, s_g3, s_x2, s_dve, s_mv, s_rstd, s_xn, s_tp, s_xT, s_sp, s_sup,
         s_x2b, s_po, s_x3, s_st0, s_st1, s_x4, s_s0, s_s1, s_s2, s_s3, s_pt, s_wt, s_pool) = m.sems(
            "c id x0 x1 gi g0 g1 g2 g3 x2 dve mv rstd xn tp xT sp sup x2b po x3 st0 st1 x4 s0 s1 s2 s3 pt wt pool")
        s_x, s_g, s_st, s_s = [s_x0, s_x1], [s_g0, s_g1, s_g2, s_g3], [s_st0, s_st1], [s_s0, s_s1, s_s2, s_s3]
        block = ctx.enter_context(nc.Block())
        x1_v = x1_d.rearrange("(b q t p) c -> b p (q t) c", p=P, q=2, t=NT)
        x3_v = x3_d.rearrange("(b q t p) c -> b t p q c", p=P, q=2, t=NT)
        xT_v = xn4T_d.rearrange("k p (b i n) -> b i p k n", n=P, i=TP)
        J = 2 * TP

        @block.sync
        def _(sp):
            for q in range(4):
                sp.sem_inc(s_s[q], 16)
            for q in range(2):
                sp.sem_inc(s_st[q], 16)
            sp.dma_start(w_sb[:, :, :], weight.rearrange("(k p) f -> p k f", p=P)).then_inc(s_c, 16)
            sp.dma_start(bias_bc[:, :], bias.rearrange("(o e) -> o e", o=1).broadcast_to([P, C])).then_inc(s_c, 16)
            sp.dma_start(x1s[:, 0], x1_v[0]).then_inc(s_x0, 16)
            sp.dma_start(aT[:, :, :], adjT.rearrange("(t p) n -> p t n", p=P)).then_inc(s_c, 16)
            sp.dma_start(x1s[:, 1], x1_v[1]).then_inc(s_x1, 16)

            def two(b, q, more):
                if more:
                    sp.wait_ge(s_x2, b * TP + TP)
                    sp.dma_start(x1s[:, q], x1_v[bass.ds(b + 2, 1)].rearrange("o p t c -> p (o t) c")).then_inc(s_x[q], 16)
                for n in range(NT):
                    sp.wait_ge(s_x3, b * TP + 2 * n + 6)
                    sp.dma_start(x3_v[bass.ds(b, 1), n].rearrange("o p q c -> p (o q) c"), x3[:, n % 2]).then_inc(s_st[n % 2], 16)
                    for r in range(2):
                        i = 2 * n + r
                        sp.wait_ge(s_xT, b * J + TP + i + 3)
                        sp.dma_start(xT_v[bass.ds(b, 1), r * NT + n].rearrange("o p k n -> p (o k) n"),
                                     xT4[:, i % 4, :].rearrange("p (k n) -> p k n", k=KC)).then_inc(s_s[i % 4], 16)
            with sp.Fori(0, NP2 // 2 - 1) as pp:
                for q in range(2):
                    two(pp * 2 + q, q, True)
            for q in range(2):
                two(NP2 - 2 + q, q, False)
            for q in range(2):
                sp.wait_ge(s_st[q], 16 + 16 * NP2 * NT // 2)
            for q in range(4):
                sp.wait_ge(s_s[q], 16 + 16 * NP2 * TP // 4)

        @block.gpsimd
        def _(pool):
            pool.sem_inc(s_x2b, 2)
            identity(nc, pool, ident, s_id)
            nc.gpsimd.memset(neghalf[:, :], -0.5).then_inc(s_id, 1)
            pool.wait_ge(s_id, 3)
            pool.wait_ge(s_c, 48)

            def norm(j, n):
                s = n % 2
                pool.wait_ge(s_mv, j + 1)
                pool.sem_inc(s_pt, 1)
                nc.gpsimd.tensor_scalar(ve[:, s:s + 1], mv[:, s, 1:2], EPS, None, ALU.add).then_inc(s_pool, 1)
                pool.wait_ge(s_pool, j + 1)
                nc.gpsimd.tensor_tensor(rstd[:, s:s + 1], ve[:, s:s + 1], neghalf[:, :], ALU.pow).then_inc(s_rstd, 1)

            def gather(b, i):
                for k in range(2):
                    pool.indirect_dma_start(out=gat[:, i % 4, k, :], out_offset=None, in_=y_d,
                                            in_offset=bass.IndirectOffsetOnAxis(ap=gi[:, k, i:i + 1], axis=0)).then_inc(s_g[i % 4], 16)
            with pool.Fori(0, NP2) as b:
                nc.gpsimd.tensor_copy(gi[:, :, :], gidx[:, :, bass.ds(b * TP, TP)]).then_inc(s_gi, 1)
                pool.wait_ge(s_gi, b + 1)
                pool.sem_inc(s_pt, 1)
                for i in range(3):
                    gather(b, i)
                for i in range(TP):
                    if i + 3 < TP:
                        if i >= 1:
                            pool.wait_ge(s_x2, b * TP + i)
                            pool.sem_inc(s_pt, 1)
                        gather(b, i + 3)
                    norm(b * J + i, i)
                    pool.wait_ge(s_xn, b * J + i + 1)
                    pool.sem_inc(s_pt, 1)
                    nc.gpsimd.tensor_tensor(x2b[:, i, :], x2[:, i % 2, :], bias_bc[:, :], ALU.add).then_inc(s_x2b, 1)
                for i in range(TP):
                    norm(b * J + TP + i, i)
                pool.wait_ge(s_x3, b * TP + TP + 4)

        @block.tensor
        def _(pe):
            pe.sem_inc(s_tp, 2)
            pe.wait_ge(s_id, 2)
            pe.wait_ge(s_c, 48)
            with pe.Fori(0, NP2) as b:
                for i in range(TP + 1):
                    if i < TP:
                        pe.wait_ge(s_xn, b * J + i + 1)
                        pe.wait_ge(s_xT, b * J + i + 1)
                        for k in range(KC):
                            last = nc.tensor.transpose(ps_tp[:, i % 2, k * P:k * P + P], xn[:, i % 2, k * P:k * P + P], ident[:, :])
                        last.then_inc(s_tp, 1)
                    if i >= 1:
                        o = i - 1
                        pe.wait_ge(s_xT, b * J + o + 3)
                        pe.wait_ge(s_sup, b * TP + o + 1)
                        for k in range(KC):
                            last = nc.tensor.matmul(ps_s[:, o % 2, 0:C], xnT[:, o % 2, k * P:k * P + P], w_sb[:, k, :],
                                                    start=(k == 0), stop=(k == KC - 1))
                        last.then_inc(s_sp, 1)
                pe.wait_ge(s_sup, b * TP + TP + 2)
                for n in range(NT + 1):
                    if n < NT:
                        pe.wait_ge(s_x3, b * TP + 2 * n + 2)
                        for mt in range(NT):
                            last = nc.tensor.matmul(ps_o[:, n % 2, :], aT[:, mt, n * P:n * P + P],
                                                    sup[:, mt, :, :].rearrange("p q c -> p (q c)"), start=(mt == 0), stop=(mt == NT - 1))
                        last.then_inc(s_po, 1)
                    if n >= 1:
                        for r in range(2):
                            i = 2 * (n - 1) + r
                            pe.wait_ge(s_xn, b * J + TP + i + 1)
                            pe.wait_ge(s_xT, b * J + TP + i + 1)
                            for k in range(KC):
                                last = nc.tensor.transpose(ps_tp[:, i % 2, k * P:k * P + P], xn4[:, i % 2, k * P:k * P + P], ident[:, :])
                            last.then_inc(s_tp, 1)

        @block.scalar
        def _(act):
            act.sem_inc(s_xT, 2)
            act.sem_inc(s_sup, 2)
            act.wait_ge(s_c, 48)
            with act.Fori(0, NP2) as b:
                for i in range(TP + 1):
                    if i < TP:
                        act.wait_ge(s_tp, b * J + i + 3)
                        nc.scalar.activation(xnT[:, i % 2, :], ps_tp[:, i % 2, 0:C], ACT.Copy).then_inc(s_xT, 1)
                    if i >= 1:
                        o = i - 1
                        act.wait_ge(s_sp, b * TP + o + 1)
                        nc.scalar.activation(sup[:, o % NT, o // NT, :], ps_s[:, o % 2, 0:C], ACT.Copy,
                                             scale=dinv[:, o % NT:o % NT + 1]).then_inc(s_sup, 1)
                for i in range(TP):
                    act.wait_ge(s_tp, b * J + TP + i + 3)
                    act.wait_ge(s_s[i % 4], b * (16 * TP // 4) + 16 * (i // 4 + 1))
                    nc.scalar.activation(xT4[:, i % 4, :], ps_tp[:, i % 2, 0:C], ACT.Copy).then_inc(s_xT, 1)

        @block.vector
        def _(dve):
            V = nc.vector
            dve.sem_inc(s_x3, 4)
            dve.wait_ge(s_c, 48)
            PRE = 0

            def pair(b, q, steps):
                ch = Chain(dve, s_dve, b * steps + PRE)
                dve.wait_ge(s_x[q], (b - q) * 8 + 16)
                ch(V.tensor_copy(wt[:, :, :], wk[:, :, bass.ds(b * TP, TP)]))
                ch.wait()

                def normalise(src, dst, j, n):
                    s = n % 2
                    ch(V.bn_stats(st[:, s, :], src))
                    ch.wait()
                    dve.sem_inc(s_wt, 1)
                    V.bn_aggr(mv[:, s, :], st[:, s, :]).then_inc(s_mv, 1)
                    dve.wait_ge(s_mv, j + 1)
                    dve.wait_ge(s_rstd, j + 1)
                    V.tensor_scalar(dst, src, mv[:, s, 0:1], rstd[:, s:s + 1], ALU.subtract, ALU.mult).then_inc(s_xn, 1)

                for i in range(TP):
                    s = i % 2
                    dve.wait_ge(s_g[i % 4], b * (8 * TP) + 32 * (i // 4 + 1))
                    ch(V.scalar_tensor_tensor(out=ta[:, s, :], in0=gat[:, i % 4, 0, :], scalar=wt[:, 0, i:i + 1], in1=x1s[:, q, i, :],
                                              op0=ALU.mult, op1=ALU.add))
                    ch.wait()
                    dve.wait_ge(s_x2b, b * TP + i + 1)
                    V.scalar_tensor_tensor(out=x2[:, s, :], in0=gat[:, i % 4, 1, :], scalar=wt[:, 1, i:i + 1], in1=ta[:, s, :],
                                           op0=ALU.mult, op1=ALU.add).then_inc(s_x2, 1)
                    dve.wait_ge(s_x2, b * TP + i + 1)
                    dve.wait_ge(s_tp, b * J + i + 1)
                    normalise(x2[:, s, :], xn[:, s, :], b * J + i, i)
                for n in range(NT):
                    dve.wait_ge(s_po, b * NT + n + 1)
                    dve.wait_ge(s_st[n % 2], b * (8 * NT) + 16 * (n // 2 + 1))
                    dve.wait_ge(s_x2b, b * TP + TP + 2)
                    for r in range(2):
                        i = 2 * n + r
                        V.scalar_tensor_tensor(out=x3[:, n % 2, r, :], in0=ps_o[:, n % 2, r * C:r * C + C], scalar=dinv[:, n:n + 1],
                                               in1=x2b[:, r * NT + n, :], op0=ALU.mult, op1=ALU.add).then_inc(s_x3, 1)
                        dve.wait_ge(s_x3, b * TP + i + 5)
                        dve.wait_ge(s_tp, b * J + TP + i + 1)
                        normalise(x3[:, n % 2, r, :], xn4[:, i % 2, :], b * J + TP + i, i)
                return ch.n

            steps = 1 + 2 * TP + TP
            with dve.Fori(0, NP2 // 2) as pp:
                for q in range(2):
                    assert pair(pp * 2 + q, q, steps) == steps


def weights_phase(nc, life, keep, W_inT, W_fc1, b_fc1, W_out, W_fc2T):
    wf, buz, wc = keep
    M, E2 = W_inT.shape
    C = W_fc1.shape[1]
    DI = W_out.shape[1]
    O = W_fc2T.shape[1]
    KM, KC, KD, KE = M // P, C // P, DI // P, E2 // P
    with ExitStack() as ctx:
        m = Place(nc, ctx, life, "wt")
        wi = m.sb("wi", [P, KM, E2])
        f1 = m.sb("f1", [P, KM, C])
        b1 = m.sb("b1", [P, KM])
        wo = m.sb("wo", [P, KM, DI])
        f2 = m.sb("f2", [P, KM, O])
        ps = m.ps("p", [P, 4, 512])
        ps_b = m.ps("b", [P, KE])
        s_in, s_bin, s_mm, s_ev, s_b, s_bc = m.sems("in bin mm ev b bc")
        block = ctx.enter_context(nc.Block())
        NF = KC * (E2 // 512)
        NO = KD // 2

        @block.sync
        def _(sp):
            sp.dma_start(wi[:, :, :], W_inT.rearrange("(k p) e -> p k e", p=P)).then_inc(s_in, 16)
            sp.dma_start(f1[:, :, :], W_fc1.rearrange("(k p) c -> p k c", p=P)).then_inc(s_in, 16)
            sp.dma_start(wo[:, :, :], W_out.rearrange("(k p) d -> p k d", p=P)).then_inc(s_in, 16)
            sp.dma_start(f2[:, :, :], W_fc2T.rearrange("(k p) o -> p k o", p=P)).then_inc(s_in, 16)
            sp.dma_start(b1[:, :], b_fc1.rearrange("(k p) -> p k", p=P), allow_slow_non_contiguous=True).then_inc(s_bin, 16)

        @block.tensor
        def _(pe):
            pe.wait_ge(s_in, 64)
            for n in range(NF + NO):
                if n >= 4:
                    pe.wait_ge(s_ev, n - 3)
                if n < NF:
                    c, e = n % KC, n // KC
                    for k in range(KM):
                        last = nc.tensor.matmul(ps[:, n % 4, :], f1[:, k, c * P:c * P + P], wi[:, k, e * 512:e * 512 + 512],
                                                start=(k == 0), stop=(k == KM - 1))
                else:
                    for r in range(2):
                        d = 2 * (n - NF) + r
                        for k in range(KM):
                            last = nc.tensor.matmul(ps[:, n % 4, r * O:r * O + O], wo[:, k, d * P:d * P + P], f2[:, k, :],
                                                    start=(k == 0), stop=(k == KM - 1))
                last.then_inc(s_mm, 1)
            pe.wait_ge(s_bin, 16)
            for e in range(KE):
                for k in range(KM):
                    last = nc.tensor.matmul(ps_b[:, e:e + 1], wi[:, k, e * P:e * P + P], b1[:, k:k + 1], start=(k == 0), stop=(k == KM - 1))
            last.then_inc(s_b, 1)

        @block.scalar
        def _(act):
            for n in range(NF + NO):
                act.wait_ge(s_mm, n + 1)
                dst = wf[:, n % KC, (n // KC) * 512:(n // KC) * 512 + 512] if n < NF else wc[:, 2 * (n - NF):2 * (n - NF) + 2, :]
                src = ps[:, n % 4, :] if n < NF else ps[:, n % 4, :].rearrange("p (r o) -> p r o", r=2)
                nc.scalar.activation(dst, src, ACT.Copy).then_inc(s_ev, 1)
            act.wait_ge(s_b, 1)
            nc.scalar.activation(buz[:, :], ps_b[:, :], ACT.Copy).then_inc(s_bc, 1)


def mamba_phase(nc, life, keep, tmask, xn4T_d, x3_d, conv_w, conv_b, W_xprojT, W_dtT, b_dt, A_log, D, b_fc2, out, L):
    wf, buz, wc = keep
    T, C = x3_d.shape
    DI, NS = A_log.shape
    R = W_dtT.shape[0]
    KC, KD = C // P, DI // P
    F = 512
    NCH = T // F
    HF = L // F
    KW = conv_w.shape[1]
    G8 = P // NS
    NG = F // G8
    NQ = NG // 4
    NT = F // P
    XR = R + 2 * NS
    NDA = 4
    BY_DVE = (15,)
    EV_DVE = (3, 7, 11, 15)
    with ExitStack() as ctx:
        m = Place(nc, ctx, life, "mb")
        xp = m.sb("xp", [P, KD, XR])
        wdt = m.sb("wdt", [R, DI])
        A = m.sb("A", [P, KD, NS])
        cw = m.sb("cw", [P, KD, KW])
        cb = m.sb("cb", [P, KD])
        bdt = m.sb("bdt", [P, KD])
        Dp = m.sb("Dp", [P, KD])
        bo = m.sb("bo", [P, C])
        tm = m.sb("tm", [P, G8])
        ident = m.sb("ident", [P, P])
        xT = m.sb("xT", [P, KC, F])
        carry = m.sb("carry", [P, KD, KW - 1])
        u = m.sb("u", [P, KD, F])
        z = m.sb("z", [P, KD, F])
        dbc = m.sb("dbc", [XR, F])
        Bb = m.sb("Bb", [P, NS, F])
        csb = m.sb("csb", [P, NT, NS])
        cg = m.sb("cg", [NG, P])
        cblk = m.sb("cblk", [P, NG, G8])
        xm = m.sb("xm", [P, F])
        ln = m.sb("ln", [P, F])
        delta = m.sb("delta", [P, 2, F])
        du = m.sb("du", [P, 2, F])
        dA = m.sb("dA", [P, NDA, F])
        dBu = m.sb("dBu", [P, NDA, F])
        h = m.sb("h", [P, 2, F, NS])
        hl = m.sb("hl", [P, KD, NS])
        hT = m.sb("hT", [P, 2, 512])
        yt = m.sb("yt", [P, 2, F])
        uraw = dA[:, :, :].rearrange("p n f -> p (n f)")[:, 0:2 * (F + KW - 1)].rearrange("p (n f) -> p n f", n=2)
        x3s = xT[:, 0, :].rearrange("p (n c) -> p n c", n=2)
        o_sb = m.sb("o", [P, 2, C])
        ps_p = m.ps("p", [P, 2, 512])
        ps_d = m.ps("d", [P, 512])
        ps_tp = m.ps("tp", [P, 3, 512])
        ps_y = m.ps("y", [P, 512])
        ps_m = m.ps("m", [P, 512])
        (s_w, s_ws, s_A, s_id, s_dve, s_x, s_pp, s_pf, s_cv, s_u, s_xp, s_db, s_dt, s_cs, s_ct, s_cb, s_Bst, s_B0, s_B1, s_B2,
         s_B3, s_Cst, s_Cld, s_dp, s_xm, s_e1, s_ln, s_de, s_du, s_da, s_bm, s_sc) = m.sems(
            "w ws A id dve x pp pf cv u xp db dt cs ct cb Bst B0 B1 B2 B3 Cst Cld dp xm e1 ln de du da bm sc")
        (s_tp, s_eva, s_evd, s_y4, s_yf, s_zf, s_om, s_ov, s_x30, s_x31, s_o0, s_o1, s_tick, s_ptick, s_petick) = m.sems(
            "tp eva evd y4 yf zf om ov x30 x31 o0 o1 tick ptick petick")
        s_B, s_x3, s_o = [s_B0, s_B1, s_B2, s_B3], [s_x30, s_x31], [s_o0, s_o1]
        B_d = nc.dram_tensor("mb_B_dram", (NS, F), F32, kind="Internal").ap()
        C_d = nc.dram_tensor("mb_C_dram", (F, NS), F32, kind="Internal").ap()
        block = ctx.enter_context(nc.Block())
        xT_v = xn4T_d.rearrange("k p (c t) -> c p k t", t=F)
        x3_v = x3_d.rearrange("(c t p) d -> c t p d", t=NT, p=P)
        out_v = out.rearrange("b n d -> (b n) d").rearrange("(c t p) d -> c t p d", t=NT, p=P)
        NPOOL = NS - len(BY_DVE)
        NEA, NED = NQ - len(EV_DVE), len(EV_DVE)

        def pool_count(s):
            return sum(1 for r in range(s + 1) if r not in BY_DVE)

        def copied(eng, U, j, q):
            if q in EV_DVE:
                eng.wait_ge(s_evd, (U + j) * NED + sum(1 for r in range(q + 1) if r in EV_DVE))
            else:
                eng.wait_ge(s_eva, (U + j) * NEA + sum(1 for r in range(q + 1) if r not in EV_DVE))

        def chunks(eng, body):
            with eng.Fori(0, NCH // HF) as b:
                for hf in range(HF):
                    body(b * HF + hf, hf)

        @block.sync
        def _(sp):
            for q in range(2):
                sp.sem_inc(s_o[q], 16)
            sp.dma_start(xp[:, :, :], W_xprojT.rearrange("(k p) r -> p k r", p=P)).then_inc(s_w, 16)
            sp.dma_start(wdt[:, :], W_dtT).then_inc(s_w, 16)
            sp.dma_start(A[:, :, :], A_log.rearrange("(k p) s -> p k s", p=P)).then_inc(s_w, 16)
            sp.dma_start(cw[:, :, :], conv_w.rearrange("(k p) w -> p k w", p=P)).then_inc(s_w, 16)
            sp.dma_start(bo[:, :], b_fc2.rearrange("(o e) -> o e", o=1).broadcast_to([P, C])).then_inc(s_w, 16)
            sp.dma_start(tm[:, :], tmask).then_inc(s_w, 16)
            for dst, src in ((cb, conv_b), (bdt, b_dt), (Dp, D)):
                sp.dma_start(dst[:, :], src.rearrange("(k p) -> p k", p=P), allow_slow_non_contiguous=True).then_inc(s_w, 16)

            def chunk(c, hf):
                sp.wait_ge(s_pp, c * (2 * KD) + 1)
                sp.dma_start(xT[:, :, :], xT_v[bass.ds(c, 1)].rearrange("o p k t -> p (o k) t")).then_inc(s_x, 16)
                sp.wait_ge(s_cs, c + 1)
                sp.dma_start(C_d.rearrange("(t p) s -> p t s", p=P), csb[:, :, :]).then_inc(s_Cst, 16)
                sp.dma_start(B_d, dbc[R:R + NS, :]).then_inc(s_Bst, 16)
                sp.wait_ge(s_Cst, c * 16 + 16)
                sp.dma_start(cg[:, :], C_d.rearrange("(g t) s -> g (t s)", t=G8)).then_inc(s_Cld, 16)
                sp.wait_ge(s_Bst, c * 16 + 16)
                for k in range(4):
                    sp.dma_start(Bb[:, 4 * k:4 * k + 4, :],
                                 B_d.rearrange("(o s) t -> o s t", o=1)[:, 4 * k:4 * k + 4, :].broadcast_to([P, 4, F])).then_inc(s_B[k], 16)
                for t in range(NT):
                    sp.wait_ge(s_ov, c * NT + t + 3)
                    sp.dma_start(x3s[:, t % 2, :], x3_v[bass.ds(c, 1), t].rearrange("o p d -> p (o d)")).then_inc(s_x3[t % 2], 16)
                    if t >= 1:
                        store(c, t - 1)
                store(c, NT - 1)

            def store(c, t):
                sp.wait_ge(s_ov, c * NT + t + 5)
                sp.dma_start(out_v[bass.ds(c, 1), t].rearrange("o p d -> p (o d)"), o_sb[:, t % 2, :]).then_inc(s_o[t % 2], 16)
            chunks(sp, chunk)
            for q in range(2):
                sp.wait_ge(s_o[q], 16 + 16 * NCH * NT // 2)

        @block.tensor
        def _(pe):
            pe.sem_inc(s_pp, 1)
            pe.sem_inc(s_y4, 2)
            pe.sem_inc(s_om, NT)
            pe.sem_inc(s_tp, 2 * NQ)
            pe.wait_ge(s_id, 2)
            pe.wait_ge(s_w, 16 * 9)

            def dt_product(c, j):
                pe.wait_ge(s_de, c * KD + j + 1)
                nc.tensor.matmul(ps_d[:, :], wdt[:, j * P:j * P + P], dbc[0:R, :], start=True, stop=True).then_inc(s_dp, 1)

            def readout(c, j):
                U = c * KD
                pe.wait_ge(s_sc, (U + j) * NS + NS + NDA)
                for q in range(NQ + 1):
                    if q < NQ:
                        if q >= 3:
                            copied(pe, U, j, q - 3)
                        elif j == 0:
                            pe.wait_ge(s_cb, c + 1)
                        if q < 3:
                            pe.wait_ge(s_y4, (U + j) * NQ + 2)
                        for k in range(4):
                            g = q * 4 + k
                            last = nc.tensor.transpose(ps_tp[:, q % 3, k * P:k * P + P],
                                                       h[:, j % 2, g * G8:(g + 1) * G8, :].rearrange("p t s -> p (t s)"), ident[:, :])
                        last.then_inc(s_tp, 1)
                    if q >= 1:
                        o = q - 1
                        copied(pe, U, j, o)
                        if o == 0:
                            pe.wait_ge(s_yf, U + j + 1)
                        for k in range(4):
                            g = o * 4 + k
                            last = nc.tensor.matmul(ps_y[:, g * G8:(g + 1) * G8], hT[:, o % 2, k * P:k * P + P], cblk[:, g, :],
                                                    start=True, stop=True)
                        last.then_inc(s_y4, 1)

            def chunk(c, hf):
                pe.wait_ge(s_x, c * 16 + 16)
                for n in range(2 * KD):
                    pe.wait_ge(s_pf, c * (2 * KD) + n + 1)
                    for k in range(KC):
                        last = nc.tensor.matmul(ps_p[:, n % 2, :], wf[:, k, n * P:n * P + P], xT[:, k, :], start=(k == 0), stop=(k == KC - 1))
                    last.then_inc(s_pp, 1)
                pe.wait_ge(s_u, c * KD + KD)
                pe.wait_ge(s_ov, c * NT + NT)
                for k in range(KD):
                    last = nc.tensor.matmul(ps_m[0:XR, :], xp[:, k, :], u[:, k, :], start=(k == 0), stop=(k == KD - 1))
                last.then_inc(s_xp, 1)
                pe.wait_ge(s_db, c + 1)
                pe.sem_inc(s_petick, 1)
                for t in range(NT):
                    last = nc.tensor.transpose(ps_m[:, t * XR:(t + 1) * XR], dbc[:, t * P:t * P + P], ident[0:XR, 0:XR])
                last.then_inc(s_dt, 1)
                dt_product(c, 0)
                pe.wait_ge(s_Cld, c * 16 + 16)
                pe.sem_inc(s_petick, 1)
                nc.tensor.transpose(ps_m[:, NT * XR:NT * XR + NG], cg[:, :], ident[0:NG, 0:NG]).then_inc(s_ct, 1)
                for j in range(KD):
                    if j + 1 < KD:
                        dt_product(c, j + 1)
                    if j >= 1:
                        readout(c, j - 1)
                readout(c, KD - 1)
                pe.wait_ge(s_zf, c * KD + KD + 2)
                for t in range(NT):
                    pe.wait_ge(s_ov, c * NT + t + 3)
                    for k in range(KD):
                        last = nc.tensor.matmul((ps_m, ps_d)[t % 2][:, 0:C], z[:, k, t * P:t * P + P], wc[:, k, :],
                                                start=(k == 0), stop=(k == KD - 1))
                    last.then_inc(s_om, 1)
            chunks(pe, chunk)

        @block.gpsimd
        def _(pool):
            pool.sem_inc(s_zf, 2)
            identity(nc, pool, ident, s_id)

            def gate(c, j):
                pool.wait_ge(s_yf, c * KD + j + 2)
                nc.gpsimd.tensor_tensor(z[:, j, :], yt[:, j % 2, :], z[:, j, :], ALU.mult).then_inc(s_zf, 1)

            def chunk(c, hf):
                U = c * KD
                for j in range(KD):
                    pool.wait_ge(s_du, U + j + 1)
                    for s in range(NS):
                        if s in BY_DVE:
                            continue
                        if j == 0 and s % 4 == 0:
                            pool.wait_ge(s_B[s // 4], c * 16 + 16)
                        n = (U + j) * NS + s
                        pool.wait_ge(s_sc, n + 1)
                        nc.gpsimd.tensor_tensor(dBu[:, s % NDA, :], du[:, j % 2, :], Bb[:, s, :], ALU.mult).then_inc(s_bm, 1)
                        if s == 8 and j >= 2:
                            gate(c, j - 2)
                gate(c, KD - 2)
                gate(c, KD - 1)
            chunks(pool, chunk)

        @block.scalar
        def _(act):
            act.sem_inc(s_pf, 2)
            act.wait_ge(s_w, 16 * 9)
            nc.scalar.activation(A[:, :, :], A[:, :, :], ACT.Exp).then_inc(s_A, 1)
            act.wait_ge(s_A, 1)
            nc.scalar.activation(A[:, :, :], A[:, :, :], ACT.Copy, scale=-1.0).then_inc(s_A, 1)
            act.wait_ge(s_A, 2)

            def softplus(c, j):
                act.wait_ge(s_xm, c * KD + j + 1)
                nc.scalar.activation(xm[:, :], xm[:, :], ACT.Exp).then_inc(s_e1, 1)
                act.wait_ge(s_e1, c * KD + j + 1)
                nc.scalar.activation(ln[:, :], xm[:, :], ACT.Ln, bias=1.0).then_inc(s_ln, 1)

            def chunk(c, hf):
                U = c * KD

                def silu_u(j):
                    act.wait_ge(s_cv, U + j + 3)
                    nc.scalar.activation(u[:, j, :], u[:, j, :], ACT.Silu, bias=cb[:, j:j + 1]).then_inc(s_u, 1)
                act.wait_ge(s_om, c * NT + NT)
                for j in range(KD):
                    act.wait_ge(s_pp, c * (2 * KD) + j + 2)
                    act.wait_ge(s_cv, U + j + 1)
                    nc.scalar.activation(uraw[:, j % 2, KW - 1:], ps_p[:, j % 2, :], ACT.Identity, bias=buz[:, j:j + 1]).then_inc(s_pf, 1)
                    if j >= 1:
                        silu_u(j - 1)
                silu_u(KD - 1)
                for j in range(KD):
                    n = KD + j
                    act.wait_ge(s_pp, c * (2 * KD) + n + 2)
                    nc.scalar.activation(z[:, j, :], ps_p[:, n % 2, :], ACT.Silu, bias=buz[:, n:n + 1]).then_inc(s_pf, 1)
                act.wait_ge(s_xp, c + 1)
                nc.scalar.activation(dbc[:, :], ps_m[0:XR, :], ACT.Copy).then_inc(s_db, 1)
                act.wait_ge(s_dt, c + 1)
                nc.scalar.activation(csb[:, :, :], ps_m[:, 0:NT * XR].rearrange("p (t r) -> p t r", t=NT)[:, :, R + NS:], ACT.Copy).then_inc(s_cs, 1)
                softplus(c, 0)
                for j in range(KD + 1):
                    if j < KD:
                        act.wait_ge(s_de, U + j + 2)
                    for s in range(NS):
                        if j < KD:
                            n = (U + j) * NS + s
                            act.wait_ge(s_sc, n + 1)
                            nc.scalar.activation(dA[:, s % NDA, :], delta[:, j % 2, :], ACT.Exp, scale=A[:, j, s:s + 1]).then_inc(s_da, 1)
                        if j >= 1 and s not in EV_DVE:
                            n = (U + j - 1) * NQ + s
                            act.wait_ge(s_tp, n + 1 + 2 * NQ)
                            act.wait_ge(s_y4, n + 1)
                            nc.scalar.activation(hT[:, s % 2, :], ps_tp[:, s % 3, :], ACT.Copy).then_inc(s_eva, 1)
                        if s == 7 and j + 1 < KD:
                            softplus(c, j + 1)
            chunks(act, chunk)

        @block.vector
        def _(dve):
            V = nc.vector
            dve.sem_inc(s_cv, 2)
            dve.sem_inc(s_de, 1)
            dve.sem_inc(s_sc, NDA)
            dve.sem_inc(s_yf, 1)
            dve.sem_inc(s_ov, NT)
            dve.wait_ge(s_w, 16 * 9)

            def chunk(c, hf, steps, before):
                U = c * KD
                ch = Chain(dve, s_dve, before)

                def guard(j):
                    dve.wait_ge(s_dp, U + j + 1)
                    V.tensor_scalar(xm[:, :], ps_d[:, :], bdt[:, j:j + 1], 40.0, ALU.add, ALU.min).then_inc(s_xm, 1)

                def step_size(j):
                    dve.wait_ge(s_ln, U + j + 1)
                    V.scalar_tensor_tensor(out=delta[:, j % 2, :], in0=ps_d[:, :], scalar=bdt[:, j:j + 1], in1=ln[:, :],
                                           op0=ALU.add, op1=ALU.max).then_inc(s_de, 1)
                    dve.wait_ge(s_de, U + j + 2)
                    V.tensor_tensor(du[:, j % 2, :], delta[:, j % 2, :], u[:, j, :], ALU.mult).then_inc(s_du, 1)

                def read_sums(j):
                    dve.wait_ge(s_y4, (U + j + 1) * NQ + 2)
                    dve.wait_ge(s_zf, U + j + 1)
                    V.scalar_tensor_tensor(out=yt[:, j % 2, :], in0=u[:, j, :], scalar=Dp[:, j:j + 1], in1=ps_y[:, :],
                                           op0=ALU.mult, op1=ALU.add).then_inc(s_yf, 1)
                for j in range(KD):
                    s = j % 2
                    dve.wait_ge(s_pf, c * (2 * KD) + j + 3)
                    if hf == 0:
                        ch(V.memset(uraw[:, s, 0:KW - 1], 0.0))
                    else:
                        ch(V.tensor_copy(uraw[:, s, 0:KW - 1], carry[:, j, :]))
                    ch.wait()
                    ch(V.tensor_copy(carry[:, j, :], uraw[:, s, F:F + KW - 1]))
                    ch(V.tensor_scalar(u[:, j, :], uraw[:, s, 0:F], cw[:, j, 0:1], None, ALU.mult))
                    for k in range(1, KW):
                        ch.wait()
                        ins = V.scalar_tensor_tensor(out=u[:, j, :], in0=uraw[:, s, k:k + F], scalar=cw[:, j, k:k + 1], in1=u[:, j, :],
                                                     op0=ALU.mult, op1=ALU.add)
                        if k < KW - 1:
                            ch(ins)
                        else:
                            ins.then_inc(s_cv, 1)
                guard(0)
                step_size(0)
                dve.wait_ge(s_ct, c + 1)
                V.tensor_tensor(cblk[:, :, :], ps_m[:, NT * XR:NT * XR + NG].unsqueeze(2).broadcast_to([P, NG, G8]),
                                tm[:, :].unsqueeze(1).broadcast_to([P, NG, G8]), ALU.mult).then_inc(s_cb, 1)
                for j in range(KD + 1):
                    for s in range(NS):
                        if j < KD:
                            n = (U + j) * NS + s
                            if s in BY_DVE:
                                if j == 0:
                                    dve.wait_ge(s_B[s // 4], c * 16 + 16)
                                ch(V.tensor_tensor(dBu[:, s % NDA, :], du[:, j % 2, :], Bb[:, s, :], ALU.mult))
                                ch.wait()
                            else:
                                dve.wait_ge(s_bm, (U + j) * NPOOL + pool_count(s))
                            if s == 0:
                                dve.wait_ge(s_tp, (U + j + 1) * NQ)
                            dve.wait_ge(s_da, n + 1)
                            V.tensor_tensor_scan(out=h[:, j % 2, :, s], data0=dA[:, s % NDA, :], data1=dBu[:, s % NDA, :],
                                                 initial=0.0 if hf == 0 else hl[:, j, s:s + 1], op0=ALU.mult, op1=ALU.add).then_inc(s_sc, 1)
                        if j >= 1 and s in EV_DVE:
                            n = (U + j - 1) * NQ + s
                            dve.wait_ge(s_tp, n + 1 + 2 * NQ)
                            dve.wait_ge(s_y4, n + 1)
                            V.tensor_copy(hT[:, s % 2, :], ps_tp[:, s % 3, :]).then_inc(s_evd, 1)
                        if s == 5 and j + 1 < KD:
                            guard(j + 1)
                        if s == 11 and j + 1 < KD:
                            step_size(j + 1)
                    if j < KD and hf == 0:
                        dve.wait_ge(s_sc, (U + j) * NS + NS + NDA)
                        V.tensor_copy(hl[:, j, :], h[:, j % 2, F - 1, :])
                    if j >= 1:
                        read_sums(j - 1)
                for t in range(NT):
                    dve.wait_ge(s_x3[t % 2], c * (16 * NT // 2) + 16 * (t // 2 + 1))
                    dve.wait_ge(s_om, c * NT + t + 1 + NT)
                    ch(V.tensor_tensor(yt[:, t % 2, 0:C], (ps_m, ps_d)[t % 2][:, 0:C], x3s[:, t % 2, :], ALU.add))
                    ch.wait()
                    dve.wait_ge(s_o[t % 2], c * (16 * NT // 2) + 16 * (t // 2 + 1))
                    V.tensor_tensor(o_sb[:, t % 2, :], yt[:, t % 2, 0:C], bo[:, :], ALU.add).then_inc(s_ov, 1)
                return ch.n

            steps = KD * (2 + KW - 1) + KD * len(BY_DVE) + NT
            with dve.Fori(0, NCH // HF) as b:
                for hf in range(HF):
                    assert chunk(b * HF + hf, hf, steps, b * (HF * steps) + hf * steps) == steps


def network(nc, consts, tmask, x, adj, adjT, gnn_W, gnn_a, gnn_beta, gate_wT, gate_b, w1, b1T, w2, b2, weight, bias,
            W_fc1, b_fc1, W_inT, conv_w, conv_b, W_xprojT, W_dtT, b_dt, A_log, D, W_out, W_fc2T, b_fc2, out):
    B, N, C = x.shape
    T = B * N
    E = w2.shape[0]
    CAP = int(1.2 * T / E)
    NT = T // P
    KC, E2, DI = C // P, W_inT.shape[1], A_log.shape[0]

    def dram(name, shape):
        return nc.dram_tensor(f"{name}_dram", shape, F32, kind="Internal").ap()

    x1_d, xn2_d, logit_d, x3_d, xn4T_d = (dram("x1", (T, C)), dram("xn2", (T, C)), dram("logit", (T, E)), dram("x3", (T, C)),
                                          dram("xn4T", (KC, P, T)))
    xg_d, y_d = dram("xg", (E * CAP, C)), dram("y", (E * CAP, C))
    with ExitStack() as life:
        with ExitStack() as ctx:
            m = Place(nc, ctx, life, "keep")
            gidx = m.sb("gidx", [P, 2, NT], I32)
            wk = m.sb("wk", [P, 2, NT])
            dinv = m.sb("dinv", [P, N // P])
            with ExitStack() as first:
                used = attention_phase(nc, first, dinv, x, adj, gnn_W, gnn_a, gnn_beta, gate_wT, gate_b, x1_d, xn2_d, logit_d, xg_d)
                clear(nc, used)
            routing_phase(nc, life, (gidx, wk), consts, logit_d, xn2_d, xg_d, CAP)
            experts_phase(nc, life, xg_d, w1, b1T, w2, b2, y_d, CAP)
            graph_phase(nc, life, (gidx, wk), dinv, x1_d, y_d, adjT, weight, bias, x3_d, xn4T_d)
        with ExitStack() as ctx:
            m = Place(nc, ctx, life, "fused")
            fused = (m.sb("wf", [P, KC, E2]), m.sb("buz", [P, E2 // P]), m.sb("wc", [P, DI // P, C]))
            weights_phase(nc, life, fused, W_inT, W_fc1, b_fc1, W_out, W_fc2T)
            mamba_phase(nc, life, fused, tmask, xn4T_d, x3_d, conv_w, conv_b, W_xprojT, W_dtT, b_dt, A_log, D, b_fc2, out, N)


_INS = ['consts', 'tmask', 'x', 'adj', 'adjT', 'L0_gnn_W', 'L0_gnn_a', 'L0_gnn_beta', 'L0_ffn_gate_wT', 'L0_ffn_gate_b',
        'L0_ffn_w1', 'L0_ffn_b1T', 'L0_ffn_w2', 'L0_ffn_b2', 'L1_gnn_weight', 'L1_gnn_bias', 'L1_ffn_W_fc1', 'L1_ffn_b_fc1',
        'L1_ffn_W_inT', 'L1_ffn_conv_w', 'L1_ffn_conv_b', 'L1_ffn_W_xprojT', 'L1_ffn_W_dtT', 'L1_ffn_b_dt', 'L1_ffn_A_log',
        'L1_ffn_D', 'L1_ffn_W_out', 'L1_ffn_W_fc2T', 'L1_ffn_b_fc2']
_OUTS = [((8, 1024, 256), 'float32')]


def constants(E, CAP):
    import numpy as _np
    p = _np.arange(128)
    e = _np.arange(E)
    blk = p[:, None] // (128 // E) == p[None, :] // (128 // E)
    tri = p[:, None] < p[None, :]
    first_slot = _np.tile(e * CAP, (128, 1))
    rank = _np.tile(E - e, (128, 1))
    sel = p[:, None] == e[None, :] * (128 // E)
    return _np.concatenate([blk, tri, first_slot, rank, sel], axis=1).astype(_np.float32)


def token_mask(states):
    import numpy as _np
    return (_np.arange(128)[:, None] // states == _np.arange(128 // states)[None, :]).astype(_np.float32)


def kernel(**inputs):
    import numpy as _np
    import concourse.bacc as _bacc
    from concourse import mybir as _mybir
    from concourse.bass_utils import run_bass_kernel_spmd as _run
    E = inputs["L0_ffn_w1"].shape[0]
    T = inputs["x"].shape[0] * inputs["x"].shape[1]
    nc = _bacc.Bacc("TRN2", target_bir_lowering=False, num_devices=1)
    arrays, args = {}, []
    for name in _INS:
        if name == "consts":
            a = constants(E, int(1.2 * T / E))
        elif name == "tmask":
            a = token_mask(inputs["L1_ffn_A_log"].shape[1])
        elif name.endswith("T"):
            a = inputs[name[:-1]].T
        else:
            a = inputs[name]
        a = _np.ascontiguousarray(a)
        arrays[f"in_{name}_dram"] = a
        args.append(nc.dram_tensor(f"in_{name}_dram", a.shape, _mybir.dt.from_np(a.dtype), kind="ExternalInput").ap())
    for i, (shape, dtype) in enumerate(_OUTS):
        dt = _mybir.dt.from_np(_np.dtype(dtype))
        args.append(nc.dram_tensor(f"out_{i}_dram", shape, dt, kind="ExternalOutput").ap())
    network(nc, *args)
    r = _run(nc, [arrays], core_ids=[0])
    return r.results[0]["out_0_dram"]
```

```python
from contextlib import ExitStack

import concourse.bass as bass
from concourse import mybir

F32 = mybir.dt.float32
BF16 = mybir.dt.bfloat16
I32 = mybir.dt.int32
U32 = mybir.dt.uint32
ACT = mybir.ActivationFunctionType
ALU = mybir.AluOpType
AX = mybir.AxisListType.X
P = 128


class Place:

    def __init__(self, nc, ctx, life, tag):
        self.nc, self.ctx, self.life, self.tag = nc, ctx, life, tag
        self.named = []

    def sb(self, name, shape, dt=F32):
        return self.ctx.enter_context(self.nc.sbuf_tensor(f"{self.tag}_{name}", shape, dt))

    def ps(self, name, shape, dt=F32):
        return self.ctx.enter_context(self.nc.psum_tensor(f"{self.tag}_ps_{name}", shape, dt))

    def sems(self, names):
        new = [self.life.enter_context(self.nc.semaphore(f"{self.tag}_{n}")) for n in names.split()]
        self.named += new
        return new


def clear(nc, sems):
    with nc.Block() as block:
        @block.sync
        def _(sp):
            for s in sems:
                sp.sem_clear(s)


class Chain:

    def __init__(self, eng, sem, base=0):
        self.eng, self.sem, self.base, self.n = eng, sem, base, 0

    def __call__(self, ins):
        ins.then_inc(self.sem, 1)
        self.n += 1

    def wait(self, back=0):
        if self.n > back:
            self.eng.wait_ge(self.sem, self.base + (self.n - back))


def identity(nc, pool, ident, s_ident):
    nc.gpsimd.memset(ident[:, :], 0.0).then_inc(s_ident, 1)
    pool.wait_ge(s_ident, 1)
    nc.gpsimd.affine_select(out=ident[:, :], in_=ident[:, :], compare_op=ALU.not_equal, fill=1.0, base=0,
                            pattern=[[-1, P]], channel_multiplier=1).then_inc(s_ident, 1)


def attention_phase(nc, life, dinv, x, adj, W, a, beta, gate_wT, gate_b, x1_d, xn2_d, logit_d, xg_d):
    B, N, C = x.shape
    NT = N // P
    KC = C // P
    E = gate_wT.shape[1]
    EPS = 1e-5
    SLOPE = 0.2
    ZN = 4
    ZW = xg_d.shape[0] * xg_d.shape[1] // P // ZN
    HX = C + 1
    with ExitStack() as ctx:
        m = Place(nc, ctx, life, "att")
        adj_sb = m.sb("adj", [P, NT, N])
        x_sb = m.sb("x", [P, 2, NT, C])
        w_sb = m.sb("w", [P, KC, HX])
        a_bc = m.sb("a_bc", [P, 2, C])
        wa = m.sb("wa", [P, KC, 2])
        wa2 = m.sb("wa2", [P, KC, P])
        scr = m.sb("scr", [P, C])
        beta_bc = m.sb("beta", [P, 1])
        gw = m.sb("gw", [P, KC, E])
        gb = m.sb("gb", [P, E])
        ident = m.sb("ident", [P, P])
        neghalf = m.sb("neghalf", [P, NT])
        st = m.sb("st", [P, NT, 6])
        mv = m.sb("mv", [P, NT, 2])
        ve = m.sb("ve", [P, NT])
        rstd = m.sb("rstd", [P, NT])
        xn = m.sb("xn", [P, NT, C])
        xnT = m.sb("xnT", [P, KC, N])
        h_sb = m.sb("h", [P, NT, HX])
        z = m.sb("z", [P, 2, N])
        lr = m.sb("lr", [P, N])
        e_sb = m.sb("e", [P, 2, N])
        mx = m.sb("mx", [P, 2])
        nmx = m.sb("nmx", [P, 2])
        rs = m.sb("rs", [P, 2])
        rr = m.sb("rr", [P, 2])
        pr = m.sb("pr", [P, 2, N])
        prT = m.sb("prT", [P, 2, N])
        bh = m.sb("bh", [P, 2, C])
        t_sb = m.sb("t", [P, 2, C])
        mn = m.sb("mn", [P, 2, C])
        ex = m.sb("ex", [P, 2, C])
        y_sb = m.sb("y", [P, C])
        x1 = m.sb("x1", [P, 2, C])
        st2 = m.sb("st2", [P, 2, 6])
        mv2 = m.sb("mv2", [P, 2, 2])
        ve2 = m.sb("ve2", [P, 2])
        rstd2 = m.sb("rstd2", [P, 2])
        xn2 = m.sb("xn2", [P, 2, C])
        xn2T = m.sb("xn2T", [P, 2, C])
        lg = m.sb("lg", [P, 2, E])
        deg = m.sb("deg", [P, NT])
        dpos = m.sb("dpos", [P, NT])
        dpow = m.sb("dpow", [P, NT])
        zero = m.sb("zero", [P, ZW])
        ps_s2 = m.ps("s2", [P, N])
        ps_tp = m.ps("tp", [P, 2, 512])
        ps_h = m.ps("h", [P, 2, 512])
        ps_a = m.ps("a", [P, 2, 512])

        (s_adj, s_w, s_cst, s_x0, s_x1, s_ident, s_half, s_pool, s_dve, s_act) = m.sems(
            "adj w cst x0 x1 ident half pool dve act")
        (s_wa, s_mv, s_rstd, s_xn, s_tp, s_xnT, s_h, s_hsb, s_s2) = m.sems("wa mv rstd xn tp xnT hps hsb s2ps")
        (s_z, s_e, s_pr, s_prT, s_at, s_bh, s_t, s_ex, s_x1r, s_mv2, s_rstd2, s_xn2, s_g, s_lg, s_xused) = m.sems(
            "z e pr prT at bh t ex x1r mv2 rstd2 xn2 g lg xused")
        (s_st0, s_st1, s_tick, s_ptick, s_deg, s_dpow, s_zero, s_zst) = m.sems("st0 st1 tick ptick deg dpow zero zst")
        s_xl = [s_x0, s_x1]
        s_st = [s_st0, s_st1]
        x_v = x.rearrange("b (t p) c -> b p t c", p=P)
        x1_v = x1_d.rearrange("(b t p) c -> b t p c", p=P, t=NT)
        xn2_v = xn2_d.rearrange("(b t p) c -> b t p c", p=P, t=NT)
        lg_v = logit_d.rearrange("(b t p) e -> b t p e", p=P, t=NT)
        block = ctx.enter_context(nc.Block())

        @block.sync
        def _(sp):
            sp.sem_inc(s_st0, 16)
            sp.sem_inc(s_st1, 16)
            sp.dma_start(w_sb[:, :, 0:C], W.rearrange("(k p) f -> p k f", p=P)).then_inc(s_w, 16)
            sp.dma_start(a_bc[:, :, :], a.rearrange("(h f) o -> o h f", h=2).broadcast_to([P, 2, C])).then_inc(s_w, 16)
            sp.dma_start(x_sb[:, 0], x_v[0]).then_inc(s_x0, 16)
            sp.dma_start(adj_sb[:, :, :], adj.rearrange("(t p) m -> p t m", p=P)).then_inc(s_adj, 16)
            sp.dma_start(x_sb[:, 1], x_v[1]).then_inc(s_x1, 16)
            sp.dma_start(gw[:, :, :], gate_wT.rearrange("(k p) e -> p k e", p=P)).then_inc(s_cst, 16)
            sp.dma_start(gb[:, :], gate_b.rearrange("(o e) -> o e", o=1).broadcast_to([P, E])).then_inc(s_cst, 16)
            sp.dma_start(beta_bc[:, :], beta.rearrange("(o e) -> o e", o=1).broadcast_to([P, 1])).then_inc(s_cst, 16)

            sp.wait_ge(s_zero, 1)
            for n in range(ZN):
                sp.dma_start(xg_d.rearrange("r c -> (r c)").rearrange("(n p w) -> n p w", n=ZN, p=P)[n], zero[:, :]).then_inc(s_zst, 16)

            def batch(b, pair, q, more):
                for i in range(NT):
                    sp.wait_ge(s_lg, b * NT + i + 2)
                    sp.dma_start(x1_v[bass.ds(b, 1), i].rearrange("o p c -> p (o c)"), x1[:, i % 2]).then_inc(s_st[i % 2], 16)
                    sp.dma_start(xn2_v[bass.ds(b, 1), i].rearrange("o p c -> p (o c)"), xn2[:, i % 2]).then_inc(s_st[i % 2], 16)
                    sp.dma_start(lg_v[bass.ds(b, 1), i].rearrange("o p c -> p (o c)"), lg[:, i % 2]).then_inc(s_st[i % 2], 16)
                if more:
                    sp.wait_ge(s_xused, b * NT + NT)
                    sp.dma_start(x_sb[:, q], x_v[bass.ds(b + 2, 1)].rearrange("o p t c -> p (o t) c")).then_inc(s_xl[q], 16)
            with sp.Fori(0, B // 2 - 1) as pair:
                for q in range(2):
                    batch(pair * 2 + q, pair, q, True)
            for q in range(2):
                batch(B - 2 + q, B // 2 - 1, q, False)
            sp.wait_ge(s_zst, 16 * ZN)
            for q in range(2):
                sp.wait_ge(s_st[q], 48 * B * NT // 2 + 16)

        @block.gpsimd
        def _(pool):
            identity(nc, pool, ident, s_ident)
            nc.gpsimd.memset(neghalf[:, :], -0.5).then_inc(s_half, 1)
            pool.wait_ge(s_half, 1)
            pool.wait_ge(s_deg, 1)
            nc.gpsimd.tensor_tensor(dpow[:, :], deg[:, :], neghalf[:, :], ALU.pow).then_inc(s_dpow, 1)
            with pool.Fori(0, B) as b:
                pool.wait_ge(s_mv, b + 1)
                pool.sem_inc(s_ptick, 1)
                nc.gpsimd.tensor_scalar(ve[:, :], mv[:, :, 1], EPS, None, ALU.add).then_inc(s_pool, 1)
                pool.wait_ge(s_pool, b * (NT + 1) + 1)
                nc.gpsimd.tensor_tensor(rstd[:, :], ve[:, :], neghalf[:, :], ALU.pow).then_inc(s_rstd, 1)
                for i in range(NT):
                    s = i % 2
                    pool.wait_ge(s_mv2, b * NT + i + 1)
                    pool.sem_inc(s_ptick, 1)
                    nc.gpsimd.tensor_scalar(ve2[:, s:s + 1], mv2[:, s, 1:2], EPS, None, ALU.add).then_inc(s_pool, 1)
                    pool.wait_ge(s_pool, b * (NT + 1) + i + 2)
                    nc.gpsimd.tensor_tensor(rstd2[:, s:s + 1], ve2[:, s:s + 1], neghalf[:, 0:1], ALU.pow).then_inc(s_rstd2, 1)

        TPB = 4 + 2 * NT

        @block.tensor
        def _(pe):
            pe.sem_inc(s_at, 2)
            pe.wait_ge(s_ident, 2)
            pe.wait_ge(s_wa, 3)
            with pe.Fori(0, B) as b:
                pe.wait_ge(s_xn, b + 1)
                for n in range(4):
                    k, hf = n // 2, n % 2
                    if n < 2:
                        pe.wait_ge(s_prT, b * NT * 2 + 2)
                    else:
                        pe.wait_ge(s_xnT, b * 4 + n - 1)
                    for j in range(4):
                        i = hf * 4 + j
                        last = nc.tensor.transpose(ps_tp[:, n % 2, j * P:j * P + P], xn[:, i, k * P:k * P + P], ident[:, :])
                    last.then_inc(s_tp, 1)
                pe.wait_ge(s_xnT, b * 4 + 4)
                for i in range(NT):
                    pe.wait_ge(s_hsb, b * NT + i + 1)
                    for k in range(KC):
                        last = nc.tensor.matmul(ps_h[:, i % 2, 0:HX], xnT[:, k, i * P:i * P + P], w_sb[:, k, :],
                                                start=(k == 0), stop=(k == KC - 1))
                    last.then_inc(s_h, 1)
                pe.wait_ge(s_z, b * NT + 2)
                for hf in range(2):
                    for k in range(KC):
                        last = nc.tensor.matmul(ps_s2[:, hf * 512:hf * 512 + 512], wa2[:, k, :],
                                                xnT[:, k, hf * 512:hf * 512 + 512], start=(k == 0), stop=(k == KC - 1))
                last.then_inc(s_s2, 1)
                pe.wait_ge(s_hsb, b * NT + NT + 2)
                for i in range(NT + 2):
                    if i < NT:
                        s = i % 2
                        pe.wait_ge(s_pr, b * NT + i + 3)
                        for hf in range(2):
                            pe.wait_ge(s_prT, (b * NT + i) * 2 + hf + 1)
                            for j in range(4):
                                jj = hf * 4 + j
                                last = nc.tensor.transpose(ps_tp[:, hf, j * P:j * P + P],
                                                           pr[:, s, jj * P:jj * P + P], ident[:, :])
                            last.then_inc(s_tp, 1)
                    if 1 <= i < NT + 1:
                        o = i - 1
                        s = o % 2
                        pe.wait_ge(s_prT, (b * NT + o) * 2 + 4)
                        pe.wait_ge(s_t, b * NT + o + 1)
                        for j in range(NT):
                            last = nc.tensor.matmul(ps_a[:, s, 0:C], prT[:, s, j * P:j * P + P], h_sb[:, j, 0:C],
                                                    start=(j == 0), stop=(j == NT - 1))
                        last.then_inc(s_at, 1)
                    if 2 <= i:
                        o = i - 2
                        s = o % 2
                        pe.wait_ge(s_xn2, b * NT + o + 1)
                        for k in range(KC):
                            last = nc.tensor.transpose(ps_h[:, 0, k * P:k * P + P], xn2[:, s, k * P:k * P + P], ident[:, :])
                        last.then_inc(s_g, 1)
                        pe.wait_ge(s_act, b * NT + o + 1)
                        pe.wait_ge(s_lg, b * NT + o + 1)
                        for k in range(KC):
                            last = nc.tensor.matmul(ps_h[:, 1, 0:E], xn2T[:, s, k * P:k * P + P], gw[:, k, :],
                                                    start=(k == 0), stop=(k == KC - 1))
                        last.then_inc(s_g, 1)
                pe.wait_ge(s_lg, b * NT + NT + 1)

        @block.scalar
        def _(act):
            act.sem_inc(s_hsb, 2)
            act.sem_inc(s_z, 2)
            act.sem_inc(s_pr, 2)
            act.sem_inc(s_prT, 2)
            with act.Fori(0, B) as b:
                for n in range(4):
                    act.wait_ge(s_tp, b * TPB + n + 1)
                    nc.scalar.activation(xnT[:, n // 2, (n % 2) * 512:(n % 2) * 512 + 512], ps_tp[:, n % 2, :],
                                         ACT.Copy).then_inc(s_xnT, 1)
                for i in range(NT):
                    act.wait_ge(s_h, b * NT + i + 1)
                    nc.scalar.activation(h_sb[:, i, :], ps_h[:, i % 2, 0:HX], ACT.Copy).then_inc(s_hsb, 1)
                act.wait_ge(s_s2, b + 1)
                act.wait_ge(s_hsb, b * NT + NT + 2)

                def scores(i):
                    act.wait_ge(s_e, b * NT + i + 1)
                    nc.scalar.activation(z[:, i % 2, :], ps_s2[:, :], ACT.Identity, bias=h_sb[:, i, C:C + 1]).then_inc(s_z, 1)

                scores(0)
                scores(1)
                for i in range(NT + 2):
                    if i < NT:
                        s = i % 2
                        act.wait_ge(s_e, b * NT + i + 3)
                        act.wait_ge(s_tp, b * TPB + 4 + 2 * i - 2)
                        nc.scalar.activation(pr[:, s, :], e_sb[:, s, :], ACT.Exp, bias=nmx[:, s:s + 1],
                                             accum_out=rs[:, s:s + 1]).then_inc(s_pr, 1)
                        if i + 2 < NT:
                            scores(i + 2)
                        act.wait_ge(s_at, b * NT + i + 1)
                        for hf in range(2):
                            act.wait_ge(s_tp, b * TPB + 4 + 2 * i + hf + 1)
                            nc.scalar.activation(prT[:, s, hf * 512:hf * 512 + 512], ps_tp[:, hf, :], ACT.Copy).then_inc(s_prT, 1)
                    if 1 <= i < NT + 1:
                        o = i - 1
                        act.wait_ge(s_t, b * NT + o + 3)
                        nc.scalar.activation(ex[:, o % 2, :], mn[:, o % 2, :], ACT.Exp).then_inc(s_ex, 1)
                    if 2 <= i:
                        o = i - 2
                        act.wait_ge(s_g, (b * NT + o) * 2 + 1)
                        nc.scalar.activation(xn2T[:, o % 2, :], ps_h[:, 0, 0:C], ACT.Copy).then_inc(s_act, 1)

        @block.vector
        def _(dve):
            dve.sem_inc(s_e, 2)
            dve.sem_inc(s_t, 2)
            dve.sem_inc(s_lg, 1)
            nc.vector.memset(zero[:, :], 0.0).then_inc(s_zero, 1)
            own = Chain(dve, s_dve)
            dve.wait_ge(s_w, 32)
            for k in range(KC):
                for j in range(2):
                    own(nc.vector.tensor_tensor_reduce(out=scr[:, :], in0=w_sb[:, k, 0:C], in1=a_bc[:, j, :], scale=1.0,
                                                       scalar=0.0, op0=ALU.mult, op1=ALU.add, accum_out=wa[:, k, j:j + 1]))
                    own.wait()
            nc.vector.tensor_copy(w_sb[:, :, C:C + 1], wa[:, :, 0:1]).then_inc(s_wa, 1)
            for k in range(KC):
                nc.vector.tensor_copy(wa2[:, k, :], wa[:, k, 1:2].to_broadcast([P, P])).then_inc(s_wa, 1)
            dve.wait_ge(s_adj, 16)
            own(nc.vector.tensor_reduce(deg[:, :], adj_sb[:, :, :], AX, ALU.add))
            own.wait()
            own(nc.vector.tensor_scalar(dpos[:, :], deg[:, :], 0.0, None, ALU.is_gt))
            own.wait()
            nc.vector.tensor_scalar(deg[:, :], deg[:, :], 1e-37, None, ALU.max).then_inc(s_deg, 1)
            dve.wait_ge(s_dpow, 1)
            own(nc.vector.tensor_tensor(dinv[:, :], dpow[:, :], dpos[:, :], ALU.mult))
            dve.wait_ge(s_cst, 48)
            pre = own.n

            def batch(b, q, steps):
                ch = Chain(dve, s_dve, b * steps + pre)
                dve.wait_ge(s_xl[q], (b - q) * 8 + 16)
                for i in range(NT):
                    ch(nc.vector.bn_stats(st[:, i, :], x_sb[:, q, i, :]))
                ch.wait()
                dve.sem_inc(s_tick, 1)
                for i in range(NT):
                    last = nc.vector.bn_aggr(mv[:, i, :], st[:, i, :])
                last.then_inc(s_mv, 1)
                dve.wait_ge(s_mv, b + 1)
                dve.wait_ge(s_rstd, b + 1)
                dve.wait_ge(s_lg, b * NT + 1)
                for i in range(NT):
                    last = nc.vector.tensor_scalar(xn[:, i, :], x_sb[:, q, i, :], mv[:, i, 0:1], rstd[:, i:i + 1],
                                                   ALU.subtract, ALU.mult)
                last.then_inc(s_xn, 1)

                def leaky(i):
                    s = i % 2
                    dve.wait_ge(s_z, b * NT + i + 3)
                    ch(nc.vector.scalar_tensor_tensor(out=lr[:, :], in0=z[:, s, :], scalar=SLOPE, in1=z[:, s, :],
                                                      op0=ALU.mult, op1=ALU.max))
                    ch.wait()
                    dve.wait_ge(s_pr, b * NT + i + 1)
                    dve.sem_inc(s_tick, 1)
                    ch(nc.vector.tensor_tensor_reduce(out=e_sb[:, s, :], in0=lr[:, :], in1=adj_sb[:, i, :], scale=1.0,
                                                      scalar=-3.0e38, op0=ALU.mult, op1=ALU.max, accum_out=mx[:, s:s + 1]))
                    ch.wait()
                    nc.vector.tensor_scalar(nmx[:, s:s + 1], mx[:, s:s + 1], -1.0, None, ALU.mult).then_inc(s_e, 1)

                leaky(0)
                for i in range(NT + 2):
                    if i + 1 < NT:
                        leaky(i + 1)
                    if 1 <= i < NT + 1:
                        o = i - 1
                        s = o % 2
                        dve.wait_ge(s_pr, b * NT + o + 3)
                        dve.wait_ge(s_hsb, b * NT + NT + 2)
                        ch(nc.vector.reciprocal(rr[:, s:s + 1], rs[:, s:s + 1]))
                        ch(nc.vector.tensor_scalar(bh[:, s, :], h_sb[:, o, 0:C], beta_bc[:, 0:1], None, ALU.mult))
                        ch.wait()
                        dve.wait_ge(s_at, b * NT + o + 3)
                        ch(nc.vector.scalar_tensor_tensor(out=t_sb[:, s, :], in0=ps_a[:, s, 0:C], scalar=rr[:, s:s + 1],
                                                          in1=bh[:, s, :], op0=ALU.mult, op1=ALU.add))
                        ch.wait()
                        nc.vector.tensor_scalar(mn[:, s, :], t_sb[:, s, :], 0.0, None, ALU.min).then_inc(s_t, 1)
                        dve.wait_ge(s_ex, b * NT + o + 1)
                        ch(nc.vector.scalar_tensor_tensor(out=y_sb[:, :], in0=t_sb[:, s, :], scalar=0.0, in1=ex[:, s, :],
                                                          op0=ALU.max, op1=ALU.add))
                        ch.wait()
                        dve.wait_ge(s_st[s], (b * NT + o - s) * 24 + 16)
                        nc.vector.scalar_tensor_tensor(out=x1[:, s, :], in0=y_sb[:, :], scalar=-1.0, in1=x_sb[:, q, o, :],
                                                       op0=ALU.add, op1=ALU.add).then_inc(s_xused, 1)
                        dve.wait_ge(s_xused, b * NT + o + 1)
                        ch(nc.vector.bn_stats(st2[:, s, :], x1[:, s, :]))
                        ch.wait()
                        dve.sem_inc(s_tick, 1)
                        nc.vector.bn_aggr(mv2[:, s, :], st2[:, s, :]).then_inc(s_mv2, 1)
                        dve.wait_ge(s_mv2, b * NT + o + 1)
                        dve.wait_ge(s_rstd2, b * NT + o + 1)
                        nc.vector.tensor_scalar(xn2[:, s, :], x1[:, s, :], mv2[:, s, 0:1], rstd2[:, s:s + 1],
                                                ALU.subtract, ALU.mult).then_inc(s_xn2, 1)
                    if 2 <= i:
                        o = i - 2
                        dve.wait_ge(s_g, (b * NT + o) * 2 + 2)
                        nc.vector.tensor_tensor(lg[:, o % 2, :], ps_h[:, 1, 0:E], gb[:, :], ALU.add).then_inc(s_lg, 1)
                return ch.n

            steps = NT + 2 * NT + 5 * NT
            with dve.Fori(0, B // 2) as pair:
                for q in range(2):
                    assert batch(pair * 2 + q, q, steps) == steps
    return m.named


def routing_phase(nc, life, keep, consts, logit_d, xn2_d, xg_d, CAP):
    gidx, wk = keep
    T, E = logit_d.shape
    C = xn2_d.shape[1]
    NT = T // P
    CH = P // E
    BIG = float(2 * E * CAP)
    EXPS = [float(2.0 ** (2 ** k)) for k in range(6, -1, -1)] + [1.0]
    with ExitStack() as ctx:
        m = Place(nc, ctx, life, "rt")
        rows = m.sb("rows", [P, NT, C])
        cst = m.sb("cst", [P, 2 * P + 3 * E])
        blk, tri, ecap, rev, sel = (cst[:, 0:P], cst[:, P:2 * P], cst[:, 2 * P:2 * P + E], cst[:, 2 * P + E:2 * P + 2 * E],
                                    cst[:, 2 * P + 2 * E:2 * P + 3 * E])
        ones = m.sb("ones", [P, P])
        lg = m.sb("lg", [P, NT, E])
        pb = m.sb("pb", [P, NT, E])
        oh = m.sb("oh", [P, 2, NT, E])
        t0 = m.sb("t0", [P, NT, E])
        t1 = m.sb("t1", [P, NT, E])
        r0 = m.sb("r0", [P, NT])
        p12 = m.sb("p12", [P, 2, NT])
        v = m.sb("v", [P, E, NT])
        vc = m.sb("vc", [P, T // CH])
        cmp = m.sb("cmp", [P, T // CH])
        cnt = m.sb("cnt", [P, 1])
        g = m.sb("g", [P, 1])
        cand = m.sb("cand", [P, 1])
        delta = m.sb("delta", [P, 1])
        thr8 = m.sb("thr8", [P, E])
        thr = m.sb("thr", [P, E])
        gt = m.sb("gt", [P, E, NT])
        eq = m.sb("eq", [P, E, NT])
        inc = m.sb("inc", [P, E, NT])
        zero = m.sb("zero", [P, NT])
        room = m.sb("room", [P, E])
        kp = m.sb("kp", [P, E, NT])
        pos = m.sb("pos", [P, E, NT])
        s_k = m.sb("s_k", [P, 2, NT])
        kept = m.sb("kept", [P, 2, NT])
        sf = m.sb("sf", [P, 2, NT])
        sidx = m.sb("sidx", [P, 2, NT], I32)
        ps_c = m.ps("c", [P, 512])
        ps_g = m.ps("g", [P, 512])
        ps_i = m.ps("i", [P, E * NT])
        ps_t = m.ps("t", [P, E * NT])
        (s_in, s_rows, s_dve, s_act, s_v, s_vc, s_vr, s_cnt, s_tot, s_thr, s_m, s_pm, s_sidx, s_sc, s_sub) = m.sems(
            "in rows dve act v vc vr cnt tot thr m pm sidx sc sub")
        v_d = nc.dram_tensor("rt_v_dram", (E, P, NT), F32, kind="Internal").ap()
        block = ctx.enter_context(nc.Block())
        NI = len(EXPS) - 1
        NM = 23

        @block.sync
        def _(sp):
            sp.dma_start(lg[:, :, :], logit_d.rearrange("(t p) e -> p t e", p=P)).then_inc(s_in, 16)
            sp.dma_start(cst[:, :], consts).then_inc(s_in, 16)
            sp.dma_start(rows[:, :, :], xn2_d.rearrange("(t p) c -> p t c", p=P)).then_inc(s_rows, 16)
            sp.wait_ge(s_v, 1)
            sp.dma_start(v_d.rearrange("e p t -> p e t"), v[:, :, :]).then_inc(s_vc, 16)
            sp.wait_ge(s_vc, 16)
            sp.dma_start(vc[:, :], v_d.rearrange("e (c q) t -> (e c) (q t)", c=CH)).then_inc(s_vr, 16)
            sp.wait_ge(s_vr, 16)

        @block.scalar
        def _(act):
            act.wait_ge(s_sub, 1)
            nc.scalar.activation(t1[:, :, :], t0[:, :, :], ACT.Exp).then_inc(s_act, 1)

        @block.tensor
        def _(pe):
            pe.wait_ge(s_in, 32)
            for n in range(NI):
                pe.wait_ge(s_cnt, n + 1)
                nc.tensor.matmul(ps_c[:, 0:1], blk, cnt[:, :], start=True, stop=True).then_inc(s_tot, 1)
            with pe.Fori(0, NM) as n:
                pe.wait_ge(s_cnt, n + NI + 1)
                nc.tensor.matmul(ps_c[:, 0:1], blk, cnt[:, :], start=True, stop=True).then_inc(s_tot, 1)
            pe.wait_ge(s_thr, 1)
            nc.tensor.matmul(ps_g[:, 0:E], ones[:, :], thr8[:, :], start=True, stop=True).then_inc(s_tot, 1)
            pe.wait_ge(s_m, 1)
            nc.tensor.matmul(ps_c[:, :], ones[:, :], gt[:, :, :].rearrange("p e t -> p (e t)"), start=True, stop=True)
            nc.tensor.matmul(ps_i[:, :], tri, eq[:, :, :].rearrange("p e t -> p (e t)"), start=True, stop=True)
            nc.tensor.matmul(ps_t[:, :], ones[:, :], eq[:, :, :].rearrange("p e t -> p (e t)"), start=True,
                             stop=True).then_inc(s_pm, 1)
            pe.wait_ge(s_m, 2)
            nc.tensor.matmul(ps_i[:, :], tri, kp[:, :, :].rearrange("p e t -> p (e t)"), start=True, stop=True)
            nc.tensor.matmul(ps_t[:, :], ones[:, :], kp[:, :, :].rearrange("p e t -> p (e t)"), start=True,
                             stop=True).then_inc(s_pm, 1)

        @block.gpsimd
        def _(pool):
            pool.wait_ge(s_sidx, 1)
            pool.wait_ge(s_rows, 16)
            for t in range(NT):
                for k in range(2):
                    pool.indirect_dma_start(out=xg_d, out_offset=bass.IndirectOffsetOnAxis(ap=sidx[:, k, t:t + 1], axis=0),
                                            in_=rows[:, t, :], in_offset=None, bounds_check=E * CAP - 1,
                                            oob_is_err=False).then_inc(s_sc, 16)
            pool.wait_ge(s_sc, 16 * 2 * NT)

        @block.vector
        def _(dve):
            own = Chain(dve, s_dve)
            V = nc.vector

            def do(ins):
                own(ins)
                own.wait()

            do(V.memset(ones[:, :], 1.0))
            do(V.memset(zero[:, :], 0.0))
            do(V.memset(cand[:, :], float(2.0 ** -126 * EXPS[0])))
            dve.wait_ge(s_in, 32)
            bc = lambda a: a.unsqueeze(2).broadcast_to([P, NT, E])
            do(V.tensor_reduce(r0[:, :], lg[:, :, :], AX, ALU.max))
            V.tensor_tensor(t0[:, :, :], lg[:, :, :], bc(r0[:, :]), ALU.subtract).then_inc(s_sub, 1)
            dve.wait_ge(s_act, 1)
            do(V.tensor_reduce(r0[:, :], t1[:, :, :], AX, ALU.add))
            do(V.reciprocal(r0[:, :], r0[:, :]))
            do(V.tensor_tensor(pb[:, :, :], t1[:, :, :], bc(r0[:, :]), ALU.mult))
            revb = rev.unsqueeze(1).broadcast_to([P, NT, E])
            for k in range(2):
                src = pb if k == 0 else t1
                do(V.tensor_reduce(p12[:, k, :], src[:, :, :], AX, ALU.max))
                do(V.tensor_tensor(t0[:, :, :], src[:, :, :], bc(p12[:, k, :]), ALU.is_equal))
                do(V.tensor_tensor(t0[:, :, :], t0[:, :, :], revb, ALU.mult))
                do(V.tensor_reduce(r0[:, :], t0[:, :, :], AX, ALU.max))
                do(V.tensor_tensor(oh[:, k], t0[:, :, :], bc(r0[:, :]), ALU.is_equal))
                if k == 0:
                    do(V.scalar_tensor_tensor(out=t1[:, :, :], in0=oh[:, 0], scalar=-2.0, in1=pb[:, :, :],
                                              op0=ALU.mult, op1=ALU.add))
            do(V.tensor_tensor(t0[:, :, :], oh[:, 0], oh[:, 1], ALU.add))
            V.tensor_tensor(v[:, :, :].rearrange("p e t -> p t e"), t0[:, :, :], pb[:, :, :], ALU.mult).then_inc(s_v, 1)
            dve.wait_ge(s_v, 1)
            dve.wait_ge(s_vr, 16)

            def count(tick):
                do(V.tensor_scalar(cmp[:, :], vc[:, :], cand[:, 0:1], None, ALU.is_ge))
                V.tensor_reduce(cnt[:, :], cmp[:, :], AX, ALU.add).then_inc(s_cnt, 1)
                dve.wait_ge(s_tot, tick)

            for n in range(NI):
                nxt, r = EXPS[n + 1], EXPS[n + 1] / EXPS[n]
                count(n + 1)
                do(V.tensor_scalar(g[:, :], ps_c[:, 0:1], float(CAP), nxt - r, ALU.is_ge, ALU.mult))
                do(V.scalar_tensor_tensor(out=cand[:, :], in0=g[:, :], scalar=r, in1=cand[:, :], op0=ALU.add, op1=ALU.mult))
            do(V.tensor_scalar(delta[:, :], cand[:, :], 0.5, None, ALU.mult))
            do(V.tensor_tensor(cand[:, :], cand[:, :], delta[:, :], ALU.add))
            at = own.n
            with dve.Fori(0, NM - 1) as n:
                own = Chain(dve, s_dve, n * 5 + at)
                do(V.tensor_scalar(cmp[:, :], vc[:, :], cand[:, 0:1], None, ALU.is_ge))
                V.tensor_reduce(cnt[:, :], cmp[:, :], AX, ALU.add).then_inc(s_cnt, 1)
                dve.wait_ge(s_tot, n + NI + 1)
                do(V.tensor_scalar(g[:, :], ps_c[:, 0:1], float(CAP), 0.5, ALU.is_ge, ALU.subtract))
                do(V.tensor_tensor(g[:, :], g[:, :], delta[:, :], ALU.mult))
                do(V.tensor_tensor(cand[:, :], cand[:, :], g[:, :], ALU.add))
                do(V.tensor_scalar(delta[:, :], delta[:, :], 0.5, None, ALU.mult))
            own = Chain(dve, s_dve)
            own.n = at + 5 * (NM - 1)
            count(NI + NM)
            do(V.tensor_scalar(g[:, :], ps_c[:, 0:1], float(CAP), 1.0, ALU.is_ge, ALU.subtract))
            do(V.tensor_tensor(g[:, :], g[:, :], delta[:, :], ALU.mult))
            do(V.tensor_tensor(cand[:, :], cand[:, :], g[:, :], ALU.add))
            V.tensor_scalar(thr8[:, :], sel, cand[:, 0:1], None, ALU.mult).then_inc(s_thr, 1)
            dve.wait_ge(s_tot, NI + NM + 1)
            do(V.tensor_copy(thr[:, :], ps_g[:, 0:E]))
            thrb = thr[:, :].unsqueeze(2).broadcast_to([P, E, NT])
            do(V.tensor_tensor(gt[:, :, :], v[:, :, :], thrb, ALU.is_gt))
            V.tensor_tensor(eq[:, :, :], v[:, :, :], thrb, ALU.is_equal).then_inc(s_m, 1)

            def prefix():
                for e in range(E):
                    own(V.tensor_tensor_scan(out=inc[:, e, :], data0=ps_t[:, e * NT:(e + 1) * NT], data1=zero[:, :],
                                             initial=0.0, op0=ALU.add, op1=ALU.add))
                own.wait()
                do(V.tensor_tensor(pos[:, :, :].rearrange("p e t -> p (e t)"), inc[:, :, :].rearrange("p e t -> p (e t)"),
                                   ps_t[:, :], ALU.subtract))
                do(V.tensor_tensor(pos[:, :, :].rearrange("p e t -> p (e t)"), pos[:, :, :].rearrange("p e t -> p (e t)"),
                                   ps_i[:, :], ALU.add))

            dve.wait_ge(s_pm, 1)
            do(V.tensor_reduce(room[:, :], ps_c[:, :].rearrange("p (e t) -> p e t", e=E), AX, ALU.add))
            do(V.tensor_scalar(room[:, :], room[:, :], -1.0, float(CAP), ALU.mult, ALU.add))
            prefix()
            do(V.tensor_tensor(kp[:, :, :], pos[:, :, :], room[:, :].unsqueeze(2).broadcast_to([P, E, NT]), ALU.is_lt))
            do(V.tensor_tensor(kp[:, :, :], kp[:, :, :], eq[:, :, :], ALU.mult))
            V.tensor_tensor(kp[:, :, :], kp[:, :, :], gt[:, :, :], ALU.add).then_inc(s_m, 1)
            dve.wait_ge(s_pm, 2)
            prefix()
            do(V.tensor_tensor(pos[:, :, :], pos[:, :, :], ecap.unsqueeze(2).broadcast_to([P, E, NT]), ALU.add))
            for k in range(2):
                for src, dst in ((pos, s_k), (kp, kept)):
                    do(V.tensor_tensor(t0[:, :, :], oh[:, k], src[:, :, :].rearrange("p e t -> p t e"), ALU.mult))
                    do(V.tensor_reduce(dst[:, k, :], t0[:, :, :], AX, ALU.add))
            own(V.tensor_tensor(wk[:, :, :], kept[:, :, :], p12[:, :, :], ALU.mult))
            own(V.tensor_tensor(gidx[:, :, :], kept[:, :, :], s_k[:, :, :], ALU.mult))
            do(V.tensor_scalar(sf[:, :, :], kept[:, :, :], -BIG, BIG, ALU.mult, ALU.add))
            V.tensor_tensor(sidx[:, :, :], sf[:, :, :], s_k[:, :, :], ALU.add).then_inc(s_sidx, 1)


def experts_phase(nc, life, xg_d, w1, b1T, w2, b2, y_d, CAP):
    E, C, H = w1.shape
    KC, KH = C // P, H // P
    NR = -(-CAP // P)
    FULL = CAP // P
    TAIL = CAP - FULL * P
    NCH = 4
    CW = CAP // NCH
    assert CAP % NCH == 0 and CW <= 512 and TAIL
    with ExitStack() as ctx:
        m = Place(nc, ctx, life, "ex")
        xg = m.sb("xg", [P, 2, NR, C])
        xgT = m.sb("xgT", [P, KC, CAP])
        w1s = m.sb("w1", [P, 2, KC, H])
        w2s = m.sb("w2", [P, 2, KH, C])
        b1s = m.sb("b1", [P, KH, E])
        b1c = m.sb("b1c", [P, KH])
        b2s = m.sb("b2", [P, E, C])
        hT = m.sb("hT", [P, KH, CAP])
        o_sb = m.sb("o", [P, 4, C])
        ident = m.sb("ident", [P, P])
        ps1 = m.ps("1", [P, 4, 512])
        ps2 = m.ps("2", [P, 2, 512])
        ps_tp = m.ps("tp", [P, 2, 512])
        (s_id, s_w0, s_w1, s_b, s_x0, s_x1, s_tp, s_xT, s_p1, s_h, s_p2, s_o, s_y0, s_y1, s_y2, s_y3, s_bc, s_tick) = m.sems(
            "id w0 w1 b x0 x1 tp xT p1 h p2 o y0 y1 y2 y3 bc tick")
        s_w, s_x, s_y = [s_w0, s_w1], [s_x0, s_x1], [s_y0, s_y1, s_y2, s_y3]
        block = ctx.enter_context(nc.Block())
        size = lambda r: P if r < FULL else TAIL
        w1_v = w1.rearrange("e (k p) h -> e p k h", p=P)
        w2_v = w2.rearrange("e (k p) d -> e p k d", p=P)
        xg_v = xg_d.rearrange("(e r) c -> e r c", e=E)
        y_v = y_d.rearrange("(e r) c -> e r c", e=E)
        one = "o a b c -> a (o b) c"

        @block.sync
        def _(sp):
            for q in range(4):
                sp.sem_inc(s_y[q], 16)
            sp.dma_start(b1s[:, :, :], b1T.rearrange("(j p) e -> p j e", p=P)).then_inc(s_b, 16)
            sp.dma_start(b2s[:, :, :], b2.rearrange("(o e) d -> o e d", o=1).broadcast_to([P, E, C])).then_inc(s_b, 16)

            def load(e, q):
                sp.dma_start(xg[:, q, 0:FULL, :], xg_v[bass.ds(e, 1), 0:FULL * P].rearrange("o (r p) c -> p (o r) c", p=P)).then_inc(s_x[q], 16)
                sp.dma_start(xg[0:TAIL, q, FULL, :], xg_v[bass.ds(e, 1), FULL * P:CAP].rearrange("o r c -> r (o c)")).then_inc(s_x[q], 16)
                sp.dma_start(w1s[:, q], w1_v[bass.ds(e, 1)].rearrange("o p k h -> p (o k) h")).then_inc(s_w[q], 16)
                sp.dma_start(w2s[:, q], w2_v[bass.ds(e, 1)].rearrange("o p k h -> p (o k) h")).then_inc(s_w[q], 16)

            load(0, 0)
            load(1, 1)

            def expert(e, q, more):
                for r in range(NR):
                    sp.wait_ge(s_o, e * NR + r + 3)
                    sp.dma_start(y_v[bass.ds(e, 1), r * P:r * P + size(r)].rearrange("o r c -> r (o c)"),
                                 o_sb[0:size(r), (q * NR + r) % 4, :]).then_inc(s_y[(q * NR + r) % 4], 16)
                if more:
                    sp.wait_ge(s_p2, e * NR + NR)
                    load(e + 2, q)
            with sp.Fori(0, E // 2 - 1) as pair:
                for q in range(2):
                    expert(pair * 2 + q, q, True)
            for q in range(2):
                expert(E - 2 + q, q, False)
            for q in range(4):
                sp.wait_ge(s_y[q], 16 + 16 * (E * NR // 4))

        @block.gpsimd
        def _(pool):
            identity(nc, pool, ident, s_id)

        @block.tensor
        def _(pe):
            pe.wait_ge(s_id, 2)

            def turn(e, q):
                pe.wait_ge(s_x[q], (e - q) * 16 + 32)
                for r in range(NR):
                    n = size(r)
                    pe.wait_ge(s_xT, e * NR + r + 1)
                    for k in range(KC):
                        last = nc.tensor.transpose(ps_tp[:, r % 2, k * P:k * P + n], xg[0:n, q, r, k * P:k * P + P], ident[0:n, 0:n])
                    last.then_inc(s_tp, 1)

            def first(e, q):
                pe.wait_ge(s_w[q], (e - q) * 16 + 32)
                pe.wait_ge(s_xT, e * NR + NR + 2)
                for j in range(KH):
                    for n in range(NCH):
                        pe.wait_ge(s_h, (e * KH + j) * NCH + n + 1)
                        for k in range(KC):
                            last = nc.tensor.matmul(ps1[:, n, 0:CW], w1s[:, q, k, j * P:j * P + P], xgT[:, k, n * CW:(n + 1) * CW],
                                                    start=(k == 0), stop=(k == KC - 1))
                        last.then_inc(s_p1, 1)

            def second(e, q):
                pe.wait_ge(s_h, (e * KH + KH) * NCH + 4)
                for r in range(NR):
                    n = size(r)
                    pe.wait_ge(s_o, e * NR + r + 1)
                    for j in range(KH):
                        last = nc.tensor.matmul(ps2[0:n, r % 2, 0:C], hT[:, j, r * P:r * P + n], w2s[:, q, j, :],
                                                start=(j == 0), stop=(j == KH - 1))
                    last.then_inc(s_p2, 1)

            turn(0, 0)
            with pe.Fori(0, E // 2 - 1) as pair:
                for q in range(2):
                    first(pair * 2 + q, q)
                    turn(pair * 2 + q + 1, 1 - q)
                    second(pair * 2 + q, q)
            first(E - 2, 0)
            turn(E - 1, 1)
            second(E - 2, 0)
            first(E - 1, 1)
            second(E - 1, 1)

        @block.scalar
        def _(act):
            act.sem_inc(s_h, 4)
            act.wait_ge(s_b, 32)

            with act.Fori(0, E) as e:
                act.wait_ge(s_h, e * KH * NCH + 4)
                act.sem_inc(s_tick, 1)
                nc.scalar.activation(b1c[:, :], b1s[:, :, bass.ds(e, 1)].rearrange("p j o -> p (j o)"), ACT.Copy).then_inc(s_bc, 1)
                act.wait_ge(s_bc, e + 1)
                for j in range(KH):
                    for n in range(NCH):
                        act.wait_ge(s_p1, (e * KH + j) * NCH + n + 1)
                        nc.scalar.activation(hT[:, j, n * CW:(n + 1) * CW], ps1[:, n, 0:CW], ACT.Gelu,
                                             bias=b1c[:, j:j + 1]).then_inc(s_h, 1)

        @block.vector
        def _(dve):
            dve.sem_inc(s_xT, 2)
            dve.sem_inc(s_o, 2)

            def turned(e):
                for r in range(NR):
                    n = size(r)
                    dve.wait_ge(s_tp, e * NR + r + 1)
                    nc.vector.tensor_copy(xgT[:, :, r * P:r * P + n],
                                          ps_tp[:, r % 2, 0:KC * P].rearrange("p (k n) -> p k n", k=KC)[:, :, 0:n]).then_inc(s_xT, 1)

            def results(pair, q):
                e = pair * 2 + q
                for r in range(NR):
                    n, i = size(r), q * NR + r
                    dve.wait_ge(s_y[i % 4], pair * (32 * NR // 4) + 16 * (i // 4 + 1))
                    dve.wait_ge(s_p2, e * NR + r + 1)
                    nc.vector.tensor_tensor(o_sb[0:n, i % 4, :], ps2[0:n, r % 2, 0:C],
                                            b2s[0:n, bass.ds(e, 1), :].rearrange("p o d -> p (o d)"), ALU.add).then_inc(s_o, 1)

            dve.wait_ge(s_b, 32)
            turned(0)
            with dve.Fori(0, E // 2 - 1) as pair:
                for q in range(2):
                    turned(pair * 2 + q + 1)
                    results(pair, q)
            turned(E - 1)
            results(E // 2 - 1, 0)
            results(E // 2 - 1, 1)


def graph_phase(nc, life, keep, dinv, x1_d, y_d, adjT, weight, bias, x3_d, xn4T_d):
    gidx, wk = keep
    N = adjT.shape[0]
    T, C = x1_d.shape
    NT = N // P
    KC = C // P
    NP2 = T // N // 2
    TP = 2 * NT
    EPS = 1e-5
    with ExitStack() as ctx:
        m = Place(nc, ctx, life, "gr")
        aT = m.sb("aT", [P, NT, N])
        w_sb = m.sb("w", [P, KC, C])
        bias_bc = m.sb("bias", [P, C])
        ident = m.sb("ident", [P, P])
        neghalf = m.sb("neghalf", [P, 1])
        x1s = m.sb("x1", [P, 2, TP, C])
        gi = m.sb("gi", [P, 2, TP], I32)
        wt = m.sb("wt", [P, 2, TP])
        gat = m.sb("gat", [P, 4, 2, C])
        ta = m.sb("ta", [P, 2, C])
        x2 = m.sb("x2", [P, 2, C])
        x2b = m.sb("x2b", [P, TP, C])
        st = m.sb("st", [P, 2, 6])
        mv = m.sb("mv", [P, 2, 2])
        ve = m.sb("ve", [P, 2])
        rstd = m.sb("rstd", [P, 2])
        xn = m.sb("xn", [P, 2, C])
        xnT = m.sb("xnT", [P, 2, C])
        sup = m.sb("sup", [P, NT, 2, C])
        x3 = m.sb("x3", [P, 2, 2, C])
        xn4 = m.sb("xn4", [P, 2, C])
        xT4 = m.sb("xT4", [P, 4, C])
        ps_tp = m.ps("tp", [P, 2, 512])
        ps_s = m.ps("s", [P, 2, 512])
        ps_o = m.ps("o", [P, 2, 512])
        (s_c, s_id, s_x0, s_x1, s_gi, s_g0, s_g1, s_g2, s_g3, s_x2, s_dve, s_mv, s_rstd, s_xn, s_tp, s_xT, s_sp, s_sup,
         s_x2b, s_po, s_x3, s_st0, s_st1, s_x4, s_s0, s_s1, s_s2, s_s3, s_pt, s_wt, s_pool) = m.sems(
            "c id x0 x1 gi g0 g1 g2 g3 x2 dve mv rstd xn tp xT sp sup x2b po x3 st0 st1 x4 s0 s1 s2 s3 pt wt pool")
        s_x, s_g, s_st, s_s = [s_x0, s_x1], [s_g0, s_g1, s_g2, s_g3], [s_st0, s_st1], [s_s0, s_s1, s_s2, s_s3]
        block = ctx.enter_context(nc.Block())
        x1_v = x1_d.rearrange("(b q t p) c -> b p (q t) c", p=P, q=2, t=NT)
        x3_v = x3_d.rearrange("(b q t p) c -> b t p q c", p=P, q=2, t=NT)
        xT_v = xn4T_d.rearrange("k p (b i n) -> b i p k n", n=P, i=TP)
        J = 2 * TP

        @block.sync
        def _(sp):
            for q in range(4):
                sp.sem_inc(s_s[q], 16)
            for q in range(2):
                sp.sem_inc(s_st[q], 16)
            sp.dma_start(w_sb[:, :, :], weight.rearrange("(k p) f -> p k f", p=P)).then_inc(s_c, 16)
            sp.dma_start(bias_bc[:, :], bias.rearrange("(o e) -> o e", o=1).broadcast_to([P, C])).then_inc(s_c, 16)
            sp.dma_start(x1s[:, 0], x1_v[0]).then_inc(s_x0, 16)
            sp.dma_start(aT[:, :, :], adjT.rearrange("(t p) n -> p t n", p=P)).then_inc(s_c, 16)
            sp.dma_start(x1s[:, 1], x1_v[1]).then_inc(s_x1, 16)

            def two(b, q, more):
                if more:
                    sp.wait_ge(s_x2, b * TP + TP)
                    sp.dma_start(x1s[:, q], x1_v[bass.ds(b + 2, 1)].rearrange("o p t c -> p (o t) c")).then_inc(s_x[q], 16)
                for n in range(NT):
                    sp.wait_ge(s_x3, b * TP + 2 * n + 6)
                    sp.dma_start(x3_v[bass.ds(b, 1), n].rearrange("o p q c -> p (o q) c"), x3[:, n % 2]).then_inc(s_st[n % 2], 16)
                    for r in range(2):
                        i = 2 * n + r
                        sp.wait_ge(s_xT, b * J + TP + i + 3)
                        sp.dma_start(xT_v[bass.ds(b, 1), r * NT + n].rearrange("o p k n -> p (o k) n"),
                                     xT4[:, i % 4, :].rearrange("p (k n) -> p k n", k=KC)).then_inc(s_s[i % 4], 16)
            with sp.Fori(0, NP2 // 2 - 1) as pp:
                for q in range(2):
                    two(pp * 2 + q, q, True)
            for q in range(2):
                two(NP2 - 2 + q, q, False)
            for q in range(2):
                sp.wait_ge(s_st[q], 16 + 16 * NP2 * NT // 2)
            for q in range(4):
                sp.wait_ge(s_s[q], 16 + 16 * NP2 * TP // 4)

        @block.gpsimd
        def _(pool):
            pool.sem_inc(s_x2b, 2)
            identity(nc, pool, ident, s_id)
            nc.gpsimd.memset(neghalf[:, :], -0.5).then_inc(s_id, 1)
            pool.wait_ge(s_id, 3)
            pool.wait_ge(s_c, 48)

            def norm(j, n):
                s = n % 2
                pool.wait_ge(s_mv, j + 1)
                pool.sem_inc(s_pt, 1)
                nc.gpsimd.tensor_scalar(ve[:, s:s + 1], mv[:, s, 1:2], EPS, None, ALU.add).then_inc(s_pool, 1)
                pool.wait_ge(s_pool, j + 1)
                nc.gpsimd.tensor_tensor(rstd[:, s:s + 1], ve[:, s:s + 1], neghalf[:, :], ALU.pow).then_inc(s_rstd, 1)

            def gather(b, i):
                for k in range(2):
                    pool.indirect_dma_start(out=gat[:, i % 4, k, :], out_offset=None, in_=y_d,
                                            in_offset=bass.IndirectOffsetOnAxis(ap=gi[:, k, i:i + 1], axis=0)).then_inc(s_g[i % 4], 16)
            with pool.Fori(0, NP2) as b:
                nc.gpsimd.tensor_copy(gi[:, :, :], gidx[:, :, bass.ds(b * TP, TP)]).then_inc(s_gi, 1)
                pool.wait_ge(s_gi, b + 1)
                pool.sem_inc(s_pt, 1)
                for i in range(3):
                    gather(b, i)
                for i in range(TP):
                    if i + 3 < TP:
                        if i >= 1:
                            pool.wait_ge(s_x2, b * TP + i)
                            pool.sem_inc(s_pt, 1)
                        gather(b, i + 3)
                    norm(b * J + i, i)
                    pool.wait_ge(s_xn, b * J + i + 1)
                    pool.sem_inc(s_pt, 1)
                    nc.gpsimd.tensor_tensor(x2b[:, i, :], x2[:, i % 2, :], bias_bc[:, :], ALU.add).then_inc(s_x2b, 1)
                for i in range(TP):
                    norm(b * J + TP + i, i)
                pool.wait_ge(s_x3, b * TP + TP + 4)

        @block.tensor
        def _(pe):
            pe.sem_inc(s_tp, 2)
            pe.wait_ge(s_id, 2)
            pe.wait_ge(s_c, 48)
            with pe.Fori(0, NP2) as b:
                for i in range(TP + 1):
                    if i < TP:
                        pe.wait_ge(s_xn, b * J + i + 1)
                        pe.wait_ge(s_xT, b * J + i + 1)
                        for k in range(KC):
                            last = nc.tensor.transpose(ps_tp[:, i % 2, k * P:k * P + P], xn[:, i % 2, k * P:k * P + P], ident[:, :])
                        last.then_inc(s_tp, 1)
                    if i >= 1:
                        o = i - 1
                        pe.wait_ge(s_xT, b * J + o + 3)
                        pe.wait_ge(s_sup, b * TP + o + 1)
                        for k in range(KC):
                            last = nc.tensor.matmul(ps_s[:, o % 2, 0:C], xnT[:, o % 2, k * P:k * P + P], w_sb[:, k, :],
                                                    start=(k == 0), stop=(k == KC - 1))
                        last.then_inc(s_sp, 1)
                pe.wait_ge(s_sup, b * TP + TP + 2)
                for n in range(NT + 1):
                    if n < NT:
                        pe.wait_ge(s_x3, b * TP + 2 * n + 2)
                        for mt in range(NT):
                            last = nc.tensor.matmul(ps_o[:, n % 2, :], aT[:, mt, n * P:n * P + P],
                                                    sup[:, mt, :, :].rearrange("p q c -> p (q c)"), start=(mt == 0), stop=(mt == NT - 1))
                        last.then_inc(s_po, 1)
                    if n >= 1:
                        for r in range(2):
                            i = 2 * (n - 1) + r
                            pe.wait_ge(s_xn, b * J + TP + i + 1)
                            pe.wait_ge(s_xT, b * J + TP + i + 1)
                            for k in range(KC):
                                last = nc.tensor.transpose(ps_tp[:, i % 2, k * P:k * P + P], xn4[:, i % 2, k * P:k * P + P], ident[:, :])
                            last.then_inc(s_tp, 1)

        @block.scalar
        def _(act):
            act.sem_inc(s_xT, 2)
            act.sem_inc(s_sup, 2)
            act.wait_ge(s_c, 48)
            with act.Fori(0, NP2) as b:
                for i in range(TP + 1):
                    if i < TP:
                        act.wait_ge(s_tp, b * J + i + 3)
                        nc.scalar.activation(xnT[:, i % 2, :], ps_tp[:, i % 2, 0:C], ACT.Copy).then_inc(s_xT, 1)
                    if i >= 1:
                        o = i - 1
                        act.wait_ge(s_sp, b * TP + o + 1)
                        nc.scalar.activation(sup[:, o % NT, o // NT, :], ps_s[:, o % 2, 0:C], ACT.Copy,
                                             scale=dinv[:, o % NT:o % NT + 1]).then_inc(s_sup, 1)
                for i in range(TP):
                    act.wait_ge(s_tp, b * J + TP + i + 3)
                    act.wait_ge(s_s[i % 4], b * (16 * TP // 4) + 16 * (i // 4 + 1))
                    nc.scalar.activation(xT4[:, i % 4, :], ps_tp[:, i % 2, 0:C], ACT.Copy).then_inc(s_xT, 1)

        @block.vector
        def _(dve):
            V = nc.vector
            dve.sem_inc(s_x3, 4)
            dve.wait_ge(s_c, 48)
            PRE = 0

            def pair(b, q, steps):
                ch = Chain(dve, s_dve, b * steps + PRE)
                dve.wait_ge(s_x[q], (b - q) * 8 + 16)
                ch(V.tensor_copy(wt[:, :, :], wk[:, :, bass.ds(b * TP, TP)]))
                ch.wait()

                def normalise(src, dst, j, n):
                    s = n % 2
                    ch(V.bn_stats(st[:, s, :], src))
                    ch.wait()
                    dve.sem_inc(s_wt, 1)
                    V.bn_aggr(mv[:, s, :], st[:, s, :]).then_inc(s_mv, 1)
                    dve.wait_ge(s_mv, j + 1)
                    dve.wait_ge(s_rstd, j + 1)
                    V.tensor_scalar(dst, src, mv[:, s, 0:1], rstd[:, s:s + 1], ALU.subtract, ALU.mult).then_inc(s_xn, 1)

                for i in range(TP):
                    s = i % 2
                    dve.wait_ge(s_g[i % 4], b * (8 * TP) + 32 * (i // 4 + 1))
                    ch(V.scalar_tensor_tensor(out=ta[:, s, :], in0=gat[:, i % 4, 0, :], scalar=wt[:, 0, i:i + 1], in1=x1s[:, q, i, :],
                                              op0=ALU.mult, op1=ALU.add))
                    ch.wait()
                    dve.wait_ge(s_x2b, b * TP + i + 1)
                    V.scalar_tensor_tensor(out=x2[:, s, :], in0=gat[:, i % 4, 1, :], scalar=wt[:, 1, i:i + 1], in1=ta[:, s, :],
                                           op0=ALU.mult, op1=ALU.add).then_inc(s_x2, 1)
                    dve.wait_ge(s_x2, b * TP + i + 1)
                    dve.wait_ge(s_tp, b * J + i + 1)
                    normalise(x2[:, s, :], xn[:, s, :], b * J + i, i)
                for n in range(NT):
                    dve.wait_ge(s_po, b * NT + n + 1)
                    dve.wait_ge(s_st[n % 2], b * (8 * NT) + 16 * (n // 2 + 1))
                    dve.wait_ge(s_x2b, b * TP + TP + 2)
                    for r in range(2):
                        i = 2 * n + r
                        V.scalar_tensor_tensor(out=x3[:, n % 2, r, :], in0=ps_o[:, n % 2, r * C:r * C + C], scalar=dinv[:, n:n + 1],
                                               in1=x2b[:, r * NT + n, :], op0=ALU.mult, op1=ALU.add).then_inc(s_x3, 1)
                        dve.wait_ge(s_x3, b * TP + i + 5)
                        dve.wait_ge(s_tp, b * J + TP + i + 1)
                        normalise(x3[:, n % 2, r, :], xn4[:, i % 2, :], b * J + TP + i, i)
                return ch.n

            steps = 1 + 2 * TP + TP
            with dve.Fori(0, NP2 // 2) as pp:
                for q in range(2):
                    assert pair(pp * 2 + q, q, steps) == steps


def weights_phase(nc, life, keep, W_inT, W_fc1, b_fc1, W_out, W_fc2T):
    wf, buz, wc = keep
    M, E2 = W_inT.shape
    C = W_fc1.shape[1]
    DI = W_out.shape[1]
    O = W_fc2T.shape[1]
    KM, KC, KD, KE = M // P, C // P, DI // P, E2 // P
    with ExitStack() as ctx:
        m = Place(nc, ctx, life, "wt")
        wi = m.sb("wi", [P, KM, E2])
        f1 = m.sb("f1", [P, KM, C])
        b1 = m.sb("b1", [P, KM])
        wo = m.sb("wo", [P, KM, DI])
        f2 = m.sb("f2", [P, KM, O])
        ps = m.ps("p", [P, 4, 512])
        ps_b = m.ps("b", [P, KE])
        s_in, s_bin, s_mm, s_ev, s_b, s_bc = m.sems("in bin mm ev b bc")
        block = ctx.enter_context(nc.Block())
        NF = KC * (E2 // 512)
        NO = KD // 2

        @block.sync
        def _(sp):
            sp.dma_start(wi[:, :, :], W_inT.rearrange("(k p) e -> p k e", p=P)).then_inc(s_in, 16)
            sp.dma_start(f1[:, :, :], W_fc1.rearrange("(k p) c -> p k c", p=P)).then_inc(s_in, 16)
            sp.dma_start(wo[:, :, :], W_out.rearrange("(k p) d -> p k d", p=P)).then_inc(s_in, 16)
            sp.dma_start(f2[:, :, :], W_fc2T.rearrange("(k p) o -> p k o", p=P)).then_inc(s_in, 16)
            sp.dma_start(b1[:, :], b_fc1.rearrange("(k p) -> p k", p=P), allow_slow_non_contiguous=True).then_inc(s_bin, 16)

        @block.tensor
        def _(pe):
            pe.wait_ge(s_in, 64)
            for n in range(NF + NO):
                if n >= 4:
                    pe.wait_ge(s_ev, n - 3)
                if n < NF:
                    c, e = n % KC, n // KC
                    for k in range(KM):
                        last = nc.tensor.matmul(ps[:, n % 4, :], f1[:, k, c * P:c * P + P], wi[:, k, e * 512:e * 512 + 512],
                                                start=(k == 0), stop=(k == KM - 1))
                else:
                    for r in range(2):
                        d = 2 * (n - NF) + r
                        for k in range(KM):
                            last = nc.tensor.matmul(ps[:, n % 4, r * O:r * O + O], wo[:, k, d * P:d * P + P], f2[:, k, :],
                                                    start=(k == 0), stop=(k == KM - 1))
                last.then_inc(s_mm, 1)
            pe.wait_ge(s_bin, 16)
            for e in range(KE):
                for k in range(KM):
                    last = nc.tensor.matmul(ps_b[:, e:e + 1], wi[:, k, e * P:e * P + P], b1[:, k:k + 1], start=(k == 0), stop=(k == KM - 1))
            last.then_inc(s_b, 1)

        @block.scalar
        def _(act):
            for n in range(NF + NO):
                act.wait_ge(s_mm, n + 1)
                dst = wf[:, n % KC, (n // KC) * 512:(n // KC) * 512 + 512] if n < NF else wc[:, 2 * (n - NF):2 * (n - NF) + 2, :]
                src = ps[:, n % 4, :] if n < NF else ps[:, n % 4, :].rearrange("p (r o) -> p r o", r=2)
                nc.scalar.activation(dst, src, ACT.Copy).then_inc(s_ev, 1)
            act.wait_ge(s_b, 1)
            nc.scalar.activation(buz[:, :], ps_b[:, :], ACT.Copy).then_inc(s_bc, 1)


def mamba_phase(nc, life, keep, xn4T_d, x3_d, conv_w, conv_b, W_xprojT, W_dtT, b_dt, A_log, D, b_fc2, out, L):
    wf, buz, wc = keep
    T, C = x3_d.shape
    DI, NS = A_log.shape
    R = W_dtT.shape[0]
    KC, KD = C // P, DI // P
    F = 512
    NCH = T // F
    assert L == 2 * F
    KW = conv_w.shape[1]
    NT = F // P
    XR = R + 2 * NS
    NI = KD // 2
    NM = NS * NI
    RING = 4
    RG = 4
    SKEW = 2
    CONV = KW
    LIMIT = 40.0
    U_PE, U_ACT, U_DVE = ((2, 6), (2, 4)), ((12, 6), (12, 4)), ((11, 6), (11, 4))
    SILU_U = (35, 30)
    X_PE, DBC_ACT = ((18, 2), (26, 1)), 36
    DT_PE, DT_ACT = ((22, 7), (31, 4)), ((31, 7), (40, 4))
    LN_ACT, DE_DVE = 53, 54
    Z_PE, Z_ACT, SILU_Z = ((32, 6), (32, 6)), ((42, 6), (42, 6)), 62
    OUT_PE, OUT_PART, OUT_DVE = (6, 8), 2, (17, 8)
    DIAG_ACT = 40

    def b_dve(m):
        return m % NI == 3 or m % (2 * NI) == 1

    def c_dve(m):
        return m % NI in (1, 3)

    def turn(m, steps, later=0):
        i, off = divmod(m - later - steps[0], steps[1])
        return i if off == 0 and 0 <= i < NI else -1

    def upto(own, m):
        return sum(1 for r in range(m + 1) if own(r))

    NBV, NCV = upto(b_dve, NM - 1), upto(c_dve, NM - 1)
    NBP, NCP = NM - NBV, NM - NCV
    with ExitStack() as ctx:
        m_ = Place(nc, ctx, life, "mb")
        xp = m_.sb("xp", [P, KD, XR])
        wdt = m_.sb("wdt", [R, DI])
        A = m_.sb("A", [P, KD, NS])
        cw = m_.sb("cw", [P, KD, KW])
        cb = m_.sb("cb", [P, KD])
        bdt = m_.sb("bdt", [P, KD])
        Dp = m_.sb("Dp", [P, KD])
        bo = m_.sb("bo", [P, C])
        ident = m_.sb("ident", [P, P])
        diagD = m_.sb("diagD", [P, NI, P])
        xT = m_.sb("xT", [P, 2, KC, F])
        carry = m_.sb("carry", [P, KD, KW - 1])
        u = m_.sb("u", [P, KD, F])
        z = m_.sb("z", [P, KD, F])
        delta = m_.sb("delta", [P, KD, F])
        du = m_.sb("du", [P, KD, F])
        dbc = m_.sb("dbc", [XR, F])
        BC = m_.sb("BC", [P, 2, NS, F])
        dA = m_.sb("dA", [P, RING, F])
        dBu = m_.sb("dBu", [P, RING, F])
        h = m_.sb("h", [P, RING, F])
        hC = m_.sb("hC", [P, RG, F])
        hl = m_.sb("hl", [P, KD, NS])
        o_sb = m_.sb("o", [P, 2, C])
        bt3 = m_.sb("bt3", [P, KD])
        spare = [delta[:, NI * (1 - g):NI * (2 - g), :].rearrange("p i t -> p (i t)") for g in range(2)]
        uraw = [spare[g][:, 0:2 * (F + KW - 1)].rearrange("p (n t) -> p n t", n=2) for g in range(2)]
        ps_y = m_.ps("y", [P, NI, 512])
        ps_p = m_.ps("p", [P, 2, 512])
        ps_x = m_.ps("x", [P, 512])
        ps_o = m_.ps("o", [P, 512])
        (s_w, s_bt, s_A, s_id, s_diag, s_x0, s_x1, s_pu, s_fu, s_pz, s_fz, s_zs, s_conv, s_cv, s_u, s_xp, s_db, s_st, s_dp, s_df, s_ln) = m_.sems(
            "w bt A id diag x0 x1 pu fu pz fz zs conv cv u xp db st dp df ln")
        (s_dm, s_de, s_du, s_da, s_bp, s_bv, s_sc, s_hl, s_cp, s_cd, s_D, s_y, s_yr, s_om, s_oa, s_ov, s_x30, s_x31, s_o0, s_o1) = m_.sems(
            "dm de du da bp bv sc hl cp cd D y yr om oa ov x30 x31 o0 o1")
        s_B = m_.sems("B0 B1 B2 B3")
        s_tick, = m_.sems("tick")
        s_x, s_x3, s_o = [s_x0, s_x1], [s_x30, s_x31], [s_o0, s_o1]
        BC_d = nc.dram_tensor("mb_BC_dram", (2 * NS, F), F32, kind="Internal").ap()
        block = ctx.enter_context(nc.Block())
        xT_v = xn4T_d.rearrange("k p (c t) -> c p k t", t=F)
        x3_v = x3_d.rearrange("(c t p) d -> c t p d", t=NT, p=P)
        out_v = out.rearrange("b n d -> (b n) d").rearrange("(c t p) d -> c t p d", t=NT, p=P)

        def chunks(eng, body):
            body(0, 0, 0, True, False)
            with eng.Fori(0, NCH // 2 - 1) as b:
                body(b * 2 + 1, b, 1, False, False)
                body(b * 2 + 2, b + 1, 0, False, False)
            body(NCH - 1, NCH // 2 - 1, 1, False, True)

        def one(view, c):
            return view[bass.ds(c, 1)]

        @block.sync
        def _(sp):
            for q in range(2):
                sp.sem_inc(s_o[q], 16)
            sp.dma_start(xp[:, :, :], W_xprojT.rearrange("(k p) r -> p k r", p=P)).then_inc(s_w, 16)
            sp.dma_start(wdt[:, :], W_dtT).then_inc(s_w, 16)
            sp.dma_start(A[:, :, :], A_log.rearrange("(k p) s -> p k s", p=P)).then_inc(s_w, 16)
            sp.dma_start(cw[:, :, :], conv_w.rearrange("(k p) w -> p k w", p=P)).then_inc(s_w, 16)
            sp.dma_start(bo[:, :], b_fc2.rearrange("(o e) -> o e", o=1).broadcast_to([P, C])).then_inc(s_w, 16)
            for dst, src in ((cb, conv_b), (bdt, b_dt), (Dp, D)):
                sp.dma_start(dst[:, :], src.rearrange("(k p) -> p k", p=P), allow_slow_non_contiguous=True).then_inc(s_w, 16)

            def load_x(c, slot):
                sp.dma_start(xT[:, slot, :, :], one(xT_v, c).rearrange("o p k t -> p (o k) t")).then_inc(s_x[slot], 16)

            def share_bc(c, H, groups):
                if 0 in groups:
                    sp.wait_ge(s_db, c + 2)
                    sp.dma_start(BC_d, dbc[R:XR, :]).then_inc(s_st, 16)
                    sp.wait_ge(s_st, c * 16 + 16)
                for k in groups:
                    if H is not None:
                        sp.wait_ge(s_y, H * NM + (4 * k + 4) * NI + RG)
                        sp.sem_inc(s_tick, 1)
                    for r in range(2):
                        sp.dma_start(BC[:, r, 4 * k:4 * k + 4, :], BC_d.rearrange("(o r s) t -> o r s t", o=1, r=2)[:, r, 4 * k:4 * k + 4, :]
                                     .broadcast_to([P, 4, F])).then_inc(s_B[k], 16)

            def output(c):
                for t in range(NT):
                    sp.wait_ge(s_o[t % 2], c * (16 * NT // 2) + 16 * (t // 2 + 1))
                    sp.dma_start(o_sb[:, t % 2, :], one(x3_v, c)[:, t].rearrange("o p d -> p (o d)")).then_inc(s_x3[t % 2], 16)
                    if t >= 1:
                        store(c, t - 1)
                store(c, NT - 1)

            def store(c, t):
                sp.wait_ge(s_ov, c * NT + t + 1)
                sp.dma_start(one(out_v, c)[:, t].rearrange("o p d -> p (o d)"), o_sb[:, t % 2, :]).then_inc(s_o[t % 2], 16)

            def chunk(c, bt, hf, first, last):
                if not last:
                    if not first:
                        sp.wait_ge(s_pz, c * KD)
                    load_x(c + 1, 1 - hf)
                if not first:
                    share_bc(c, 2 * c - 1, [3])
                    output(c - 1)
                if not last:
                    for k in range(4):
                        sp.wait_ge(s_B[k], c * 32 + 32)
                        sp.sem_inc(s_tick, 1)
                    share_bc(c + 1, 2 * c + 1, [0, 1, 2])
            load_x(0, 0)
            share_bc(0, None, range(4))
            chunks(sp, chunk)
            output(NCH - 1)
            for q in range(2):
                sp.wait_ge(s_o[q], 16 + 16 * NCH * NT // 2)

        @block.tensor
        def _(pe):
            pe.sem_inc(s_y, RG)
            pe.wait_ge(s_id, 2)
            pe.wait_ge(s_w, 16 * 8)

            def project(bank, slot, n, k):
                return nc.tensor.matmul(ps_p[:, bank, :], wf[:, k, n * P:n * P + P], xT[:, slot, k, :], start=(k == 0), stop=(k == KC - 1))

            def x_product(c, k):
                pe.wait_ge(s_u, c * KD + k + 1)
                if k == 0:
                    pe.wait_ge(s_db, c + 1)
                last = nc.tensor.matmul(ps_x[0:XR, :], xp[:, k, :], u[:, k, :], start=(k == 0), stop=(k == KD - 1))
                if k == KD - 1:
                    last.then_inc(s_xp, 1)

            def dt_product(c, H, g, i):
                if i == 0:
                    pe.wait_ge(s_db, c + 2)
                pe.wait_ge(s_df, H * NI + i + 1)
                j = g * NI + i
                nc.tensor.matmul(ps_x[:, :], wdt[:, j * P:j * P + P], dbc[0:R, :], start=True, stop=True).then_inc(s_dp, 1)

            def out_product(c, t, part):
                if t == 0 and part == 0:
                    pe.wait_ge(s_yr, (c + 1) * KD + NI)
                if part == 0:
                    pe.wait_ge(s_oa, c * NT + t + 1)
                for k in range(part * KD // 4, (part + 1) * KD // 4):
                    last = nc.tensor.matmul(ps_o[:, 0:C], z[:, k, t * P:t * P + P], wc[:, k, :], start=(k == 0), stop=(k == KD - 1))
                if part == 3:
                    last.then_inc(s_om, 1)

            def chunk(c, bt, hf, first, last):
                for g in range(2):
                    H = c * 2 + g
                    for s in range(NS):
                        for i in range(NI):
                            m = s * NI + i
                            j = g * NI + i
                            if s == 0:
                                pe.wait_ge(s_yr, H * NI + i + 1)
                                pe.wait_ge(s_diag, H * NI + i + 1)
                                if first:
                                    pe.wait_ge(s_u, j + 1)
                                nc.tensor.matmul(ps_y[:, i, :], diagD[:, i, :], u[:, j, :], start=True, stop=False).then_inc(s_D, 1)
                            if c_dve(m):
                                pe.wait_ge(s_cd, H * NCV + upto(c_dve, m) + NCV)
                            else:
                                pe.wait_ge(s_cp, H * NCP + (m + 1 - upto(c_dve, m)) + NCP)
                            nc.tensor.matmul(ps_y[:, i, :], ident[:, :], hC[:, m % RG, :], start=False, stop=(s == NS - 1)).then_inc(s_y, 1)
                            for part in range(KC):
                                k = turn(m, U_PE[g], part)
                                if last or k < 0:
                                    continue
                                if part == 0:
                                    if k == 0 and g == 0:
                                        pe.wait_ge(s_x[1 - hf], (bt + 1) * 16 if hf == 0 else (bt + 2) * 16)
                                    if k < 2:
                                        pe.wait_ge(s_fz, H * NI + k + 3)
                                    else:
                                        pe.wait_ge(s_fu, (c + 1) * KD + g * NI + k - 1)
                                ins = project(k % 2, 1 - hf, g * NI + k, part)
                                if part == KC - 1:
                                    ins.then_inc(s_pu, 1)
                            for part in range(4):
                                k = turn(m, OUT_PE, part * OUT_PART)
                                if g == 0 and not first and k >= 0:
                                    out_product(c - 1, k, part)
                            for part in range(2):
                                k = turn(m, X_PE[part])
                                if g == 1 and k >= 0 and not last:
                                    if part == 0 and k == 0:
                                        pe.wait_ge(s_df, H * NI + NI + 1)
                                    x_product(c + 1, part * NI + k)
                            for part in range(KC):
                                k = turn(m, Z_PE[g], part)
                                if k < 0:
                                    continue
                                if part == 0:
                                    if k < 2 and not last:
                                        pe.wait_ge(s_fu, (c + 1) * KD + g * NI + k + 3)
                                    else:
                                        pe.wait_ge(s_fz, H * NI + k + 3)
                                ins = project(k % 2, hf, KD + g * NI + k, part)
                                if part == KC - 1:
                                    ins.then_inc(s_pz, 1)
                            k = turn(m, DT_PE[g])
                            if k >= 0 and not (last and g == 1):
                                dt_product(c + g, H + 1, 1 - g, k)
            pe.wait_ge(s_x[0], 16)
            for j in range(KD):
                if j >= 2:
                    pe.wait_ge(s_fu, j - 1)
                project(j % 2, 0, j, 0)
                project(j % 2, 0, j, 1).then_inc(s_pu, 1)
            for k in range(KD):
                x_product(0, k)
            for i in range(NI):
                dt_product(0, 0, 0, i)
            chunks(pe, chunk)
            for t in range(NT):
                for part in range(4):
                    out_product(NCH - 1, t, part)

        @block.gpsimd
        def _(pool):
            pool.sem_inc(s_cp, NCP)
            identity(nc, pool, ident, s_id)

            def times_C(H, g, m):
                if c_dve(m):
                    return
                pool.wait_ge(s_sc, H * NM + m + 1 + RING)
                pool.wait_ge(s_y, H * NM + m + 1)
                nc.gpsimd.tensor_tensor(hC[:, m % RG, :], h[:, m % RING, :], BC[:, 1, m // NI, :], ALU.mult).then_inc(s_cp, 1)

            def chunk(c, bt, hf, first, last):
                for g in range(2):
                    H = c * 2 + g
                    for m in range(NM):
                        s, i = m // NI, m % NI
                        if g == 0 and m % (4 * NI) == 0:
                            pool.wait_ge(s_B[s // 4], c * 32 + 32)
                        if not b_dve(m):
                            if s == 0:
                                pool.wait_ge(s_du, H * NI + i + 1)
                            pool.wait_ge(s_sc, H * NM + m + 1)
                            nc.gpsimd.tensor_tensor(dBu[:, m % RING, :], du[:, g * NI + i, :], BC[:, 0, s, :], ALU.mult).then_inc(s_bp, 1)
                        if m >= SKEW:
                            times_C(H, g, m - SKEW)
                        elif not (first and g == 0):
                            times_C(H - 1, 1 - g, m - SKEW + NM)
            chunks(pool, chunk)
            for m in range(NM - SKEW, NM):
                times_C(2 * NCH - 1, 1, m)

        @block.scalar
        def _(act):
            act.sem_inc(s_fz, NI)
            act.sem_inc(s_db, 1)
            act.sem_inc(s_df, 1)
            act.wait_ge(s_w, 16 * 8)
            nc.scalar.activation(A[:, :, :], A[:, :, :], ACT.Exp).then_inc(s_A, 1)
            act.wait_ge(s_A, 1)
            nc.scalar.activation(A[:, :, :], A[:, :, :], ACT.Copy, scale=-1.0).then_inc(s_A, 1)
            act.wait_ge(s_A, 2)
            act.wait_ge(s_id, 2)

            def diagonals(g):
                for i in range(NI):
                    nc.scalar.activation(diagD[:, i, :], ident[:, :], ACT.Copy, scale=Dp[:, g * NI + i:g * NI + i + 1]).then_inc(s_diag, 1)

            def copy_u(U, j):
                act.wait_ge(s_pu, U + 1)
                act.wait_ge(s_cv, U + 1)
                nc.scalar.activation(uraw[j // NI][:, j % 2, KW - 1:], ps_p[:, j % 2, :], ACT.Identity, bias=buz[:, j:j + 1])
                nc.scalar.activation(u[:, j, :], ps_p[:, j % 2, :], ACT.Identity, bias=bt3[:, j:j + 1],
                                     scale=cw[:, j, KW - 1:KW]).then_inc(s_fu, 1)

            def silu_u(U, j):
                act.wait_ge(s_cv, U + 3)
                nc.scalar.activation(u[:, j, :], u[:, j, :], ACT.Silu, bias=cb[:, j:j + 1]).then_inc(s_u, 1)

            def copy_dbc(c):
                act.wait_ge(s_xp, c + 1)
                nc.scalar.activation(dbc[:, :], ps_x[0:XR, :], ACT.Copy).then_inc(s_db, 1)

            def exp_dt(H, g, i):
                j = g * NI + i
                act.wait_ge(s_dp, H * NI + i + 1)
                nc.scalar.activation(delta[:, j, :], ps_x[:, :], ACT.Identity, bias=bdt[:, j:j + 1])
                nc.scalar.activation(du[:, j, :], ps_x[:, :], ACT.Exp, bias=bdt[:, j:j + 1]).then_inc(s_df, 1)

            def keep_last(H, g, m):
                act.wait_ge(s_sc, H * NM + m + 1 + RING)
                nc.scalar.activation(hl[:, g * NI + m % NI, m // NI:m // NI + 1], h[:, m % RING, F - 1:F], ACT.Copy).then_inc(s_hl, 1)

            def ln_dt(H, g, i):
                act.wait_ge(s_df, H * NI + i + 2)
                j = g * NI + i
                nc.scalar.activation(du[:, j, :], du[:, j, :], ACT.Ln, bias=1.0).then_inc(s_ln, 1)

            def chunk(c, bt, hf, first, last):
                for g in range(2):
                    H = c * 2 + g
                    for s in range(NS):
                        for i in range(NI):
                            m = s * NI + i
                            if s == 0:
                                act.wait_ge(s_de, H * NI + i + 1)
                            act.wait_ge(s_sc, H * NM + m + 1)
                            nc.scalar.activation(dA[:, m % RING, :], delta[:, g * NI + i, :], ACT.Exp,
                                                 scale=A[:, g * NI + i, s:s + 1]).then_inc(s_da, 1)
                            if hf == 0 and m > RING:
                                keep_last(H, g, m - RING - 1)
                            if (hf == 0) == (g == 1) and m <= RING and not (first and g == 0):
                                keep_last(H - 1, 1 - g, m - RING - 1 + NM)
                            k = turn(m, U_ACT[g])
                            if k >= 0 and not last:
                                act.wait_ge(s_D, H * NI + k + 1)
                                copy_u((c + 1) * KD + g * NI + k, g * NI + k)
                            if m == SILU_U[g] and not last:
                                for k in range(NI):
                                    silu_u((c + 1) * KD + g * NI + k, g * NI + k)
                            if m == DIAG_ACT and not (last and g == 1):
                                act.wait_ge(s_D, H * NI + NI)
                                diagonals(1 - g)
                            if m == DBC_ACT and g == 1 and not last:
                                act.wait_ge(s_st, c * 16 + 16)
                                copy_dbc(c + 1)
                            k = turn(m, DT_ACT[g])
                            if k >= 0 and not (last and g == 1):
                                exp_dt(H + 1, 1 - g, k)
                            k = turn(m, Z_ACT[g])
                            if k >= 0:
                                act.wait_ge(s_pz, H * NI + k + 1)
                                if g == 0 and k == 0 and not first:
                                    act.wait_ge(s_om, c * NT)
                                nc.scalar.activation(z[:, g * NI + k, :], ps_p[:, k % 2, :], ACT.Identity,
                                                     bias=buz[:, KD + g * NI + k:KD + g * NI + k + 1]).then_inc(s_fz, 1)
                            if m == LN_ACT and not (last and g == 1):
                                for k in range(NI):
                                    ln_dt(H + 1, 1 - g, k)
                            if m == SILU_Z:
                                for k in range(NI):
                                    act.wait_ge(s_fz, H * NI + k + 1 + NI)
                                    nc.scalar.activation(z[:, g * NI + k, :], z[:, g * NI + k, :], ACT.Silu).then_inc(s_zs, 1)
            diagonals(0)
            act.wait_ge(s_bt, 1)
            for j in range(KD):
                copy_u(j, j)
            for j in range(KD):
                silu_u(j, j)
            copy_dbc(0)
            for i in range(NI):
                exp_dt(0, 0, i)
            for i in range(NI):
                ln_dt(0, 0, i)
            chunks(act, chunk)

        @block.vector
        def _(dve):
            V = nc.vector
            dve.sem_inc(s_cv, 2)
            dve.sem_inc(s_sc, RING)
            dve.sem_inc(s_yr, NI)
            dve.sem_inc(s_oa, 1)
            dve.sem_inc(s_cd, NCV)
            dve.wait_ge(s_w, 16 * 8)
            V.tensor_tensor(bt3[:, :], buz[:, 0:KD], cw[:, :, KW - 1], ALU.mult).then_inc(s_bt, 1)

            def conv(c, j, hf, k):
                raw, U = uraw[j // NI][:, j % 2, :], c * KD + j
                if k == 0:
                    dve.wait_ge(s_fu, U + 1)
                    if hf == 0:
                        V.memset(raw[:, 0:KW - 1], 0.0).then_inc(s_conv, 1)
                    else:
                        V.tensor_copy(raw[:, 0:KW - 1], carry[:, j, :]).then_inc(s_conv, 1)
                    dve.wait_ge(s_conv, U * CONV + 1)
                    V.tensor_copy(carry[:, j, :], raw[:, F:F + KW - 1]).then_inc(s_conv, 1)
                else:
                    dve.wait_ge(s_conv, U * CONV + 2 + k)
                V.scalar_tensor_tensor(out=u[:, j, :], in0=raw[:, k:k + F], scalar=cw[:, j, k:k + 1], in1=u[:, j, :],
                                       op0=ALU.mult, op1=ALU.add).then_inc(s_cv if k == KW - 2 else s_conv, 1)

            def step_size(H, g, i):
                j = g * NI + i
                dve.wait_ge(s_ln, H * NI + i + 1)
                V.scalar_tensor_tensor(out=delta[:, j, :], in0=du[:, j, :], scalar=LIMIT, in1=delta[:, j, :],
                                       op0=ALU.min, op1=ALU.max).then_inc(s_de, 1)

            def step_u(H, g, i):
                j = g * NI + i
                dve.wait_ge(s_de, H * NI + i + 1)
                V.tensor_tensor(du[:, j, :], delta[:, j, :], u[:, j, :], ALU.mult).then_inc(s_du, 1)

            def gate(H, g, i):
                dve.wait_ge(s_y, (H + 1) * NM - NI + i + 1 + RG)
                dve.wait_ge(s_zs, H * NI + i + 1)
                V.tensor_tensor(z[:, g * NI + i, :], ps_y[:, i, :], z[:, g * NI + i, :], ALU.mult).then_inc(s_yr, 1)

            def out_sum(c, t, k):
                if k == 1:
                    dve.wait_ge(s_oa, c * NT + t + 2)
                    V.tensor_tensor(o_sb[:, t % 2, :], o_sb[:, t % 2, :], bo[:, :], ALU.add).then_inc(s_ov, 1)
                    return
                dve.wait_ge(s_x3[t % 2], c * (16 * NT // 2) + 16 * (t // 2 + 1))
                dve.wait_ge(s_om, c * NT + t + 1)
                V.tensor_tensor(o_sb[:, t % 2, :], ps_o[:, 0:C], o_sb[:, t % 2, :], ALU.add).then_inc(s_oa, 1)

            def times_B(c, H, g, m):
                if not b_dve(m):
                    return
                s, i = m // NI, m % NI
                if g == 0:
                    dve.wait_ge(s_B[s // 4], c * 32 + 32)
                if s == 0:
                    dve.wait_ge(s_du, H * NI + i + 1)
                V.tensor_tensor(dBu[:, m % RING, :], du[:, g * NI + i, :], BC[:, 0, s, :], ALU.mult).then_inc(s_bv, 1)

            def times_C(H, m):
                if c_dve(m):
                    dve.wait_ge(s_sc, H * NM + m + 1 + RING)
                    dve.wait_ge(s_y, H * NM + m + 1)
                    V.tensor_tensor(hC[:, m % RG, :], h[:, m % RING, :], BC[:, 1, m // NI, :], ALU.mult).then_inc(s_cd, 1)

            def scan(bt, H, g, m, hf):
                s, i = m // NI, m % NI
                if b_dve(m):
                    dve.wait_ge(s_bv, H * NBV + upto(b_dve, m))
                else:
                    dve.wait_ge(s_bp, H * NBP + (m + 1 - upto(b_dve, m)))
                dve.wait_ge(s_da, H * NM + m + 1)
                back = (m - RING) % NM
                prior = H if m >= RING else H - 1
                if c_dve(back):
                    dve.wait_ge(s_cd, prior * NCV + upto(c_dve, back) + NCV)
                else:
                    dve.wait_ge(s_cp, prior * NCP + (back + 1 - upto(c_dve, back)) + NCP)
                kept = g * NM + m - RING + 1
                if hf == 0 and kept > 0:
                    dve.wait_ge(s_hl, bt * (2 * NM) + kept)
                if hf == 1 and g == 0 and m < RING:
                    dve.wait_ge(s_hl, bt * (2 * NM) + 2 * NM + kept)
                V.tensor_tensor_scan(out=h[:, m % RING, :], data0=dA[:, m % RING, :], data1=dBu[:, m % RING, :],
                                     initial=0.0 if hf == 0 else hl[:, g * NI + i, s:s + 1], op0=ALU.mult, op1=ALU.add).then_inc(s_sc, 1)

            def chunk(c, bt, hf, first, last):
                for g in range(2):
                    H = c * 2 + g
                    start = first and g == 0
                    end = last and g == 1
                    if start:
                        times_B(c, H, g, 0)
                    for m in range(NM):
                        s, i = m // NI, m % NI
                        if m + 1 < NM:
                            times_B(c, H, g, m + 1)
                        elif not end:
                            times_B(c + g, H + 1, 1 - g, 0)
                        scan(bt, H, g, m, hf)
                        if m >= 1:
                            times_C(H, m - 1)
                        elif not start:
                            times_C(H - 1, NM - 1)
                        if 1 <= m <= NI and not start:
                            gate(H - 1, 1 - g, m - 1)
                        for k in range(KW - 1):
                            unit = turn(m, U_DVE[g], k)
                            if unit >= 0 and not last:
                                conv(c + 1, g * NI + unit, 1 - hf, k)
                        for k in range(2):
                            t = turn(m, OUT_DVE, k)
                            if g == 0 and not first and t >= 0:
                                out_sum(c - 1, t, k)
                        if DE_DVE <= m < DE_DVE + 2 * NI and not end:
                            (step_size, step_u)[(m - DE_DVE) % 2](H + 1, 1 - g, (m - DE_DVE) // 2)
            for j in range(KD):
                for k in range(KW - 1):
                    conv(0, j, 0, k)
            for i in range(NI):
                step_size(0, 0, i)
                step_u(0, 0, i)
            chunks(dve, chunk)
            times_C(2 * NCH - 1, NM - 1)
            for i in range(NI):
                gate(2 * NCH - 1, 1, i)
            for t in range(NT):
                out_sum(NCH - 1, t, 0)
                out_sum(NCH - 1, t, 1)


def network(nc, consts, x, adj, adjT, gnn_W, gnn_a, gnn_beta, gate_wT, gate_b, w1, b1T, w2, b2, weight, bias,
            W_fc1, b_fc1, W_inT, conv_w, conv_b, W_xprojT, W_dtT, b_dt, A_log, D, W_out, W_fc2T, b_fc2, out):
    B, N, C = x.shape
    T = B * N
    E = w2.shape[0]
    CAP = int(1.2 * T / E)
    NT = T // P
    KC, E2, DI = C // P, W_inT.shape[1], A_log.shape[0]

    def dram(name, shape):
        return nc.dram_tensor(f"{name}_dram", shape, F32, kind="Internal").ap()

    x1_d, xn2_d, logit_d, x3_d, xn4T_d = (dram("x1", (T, C)), dram("xn2", (T, C)), dram("logit", (T, E)), dram("x3", (T, C)),
                                          dram("xn4T", (KC, P, T)))
    xg_d, y_d = dram("xg", (E * CAP, C)), dram("y", (E * CAP, C))
    with ExitStack() as life:
        with ExitStack() as ctx:
            m = Place(nc, ctx, life, "keep")
            gidx = m.sb("gidx", [P, 2, NT], I32)
            wk = m.sb("wk", [P, 2, NT])
            dinv = m.sb("dinv", [P, N // P])
            with ExitStack() as first:
                used = attention_phase(nc, first, dinv, x, adj, gnn_W, gnn_a, gnn_beta, gate_wT, gate_b, x1_d, xn2_d, logit_d, xg_d)
                clear(nc, used)
            routing_phase(nc, life, (gidx, wk), consts, logit_d, xn2_d, xg_d, CAP)
            experts_phase(nc, life, xg_d, w1, b1T, w2, b2, y_d, CAP)
            graph_phase(nc, life, (gidx, wk), dinv, x1_d, y_d, adjT, weight, bias, x3_d, xn4T_d)
        with ExitStack() as ctx:
            m = Place(nc, ctx, life, "fused")
            fused = (m.sb("wf", [P, KC, E2]), m.sb("buz", [P, E2 // P]), m.sb("wc", [P, DI // P, C]))
            weights_phase(nc, life, fused, W_inT, W_fc1, b_fc1, W_out, W_fc2T)
            mamba_phase(nc, life, fused, xn4T_d, x3_d, conv_w, conv_b, W_xprojT, W_dtT, b_dt, A_log, D, b_fc2, out, N)


_INS = ['consts', 'x', 'adj', 'adjT', 'L0_gnn_W', 'L0_gnn_a', 'L0_gnn_beta', 'L0_ffn_gate_wT', 'L0_ffn_gate_b',
        'L0_ffn_w1', 'L0_ffn_b1T', 'L0_ffn_w2', 'L0_ffn_b2', 'L1_gnn_weight', 'L1_gnn_bias', 'L1_ffn_W_fc1', 'L1_ffn_b_fc1',
        'L1_ffn_W_inT', 'L1_ffn_conv_w', 'L1_ffn_conv_b', 'L1_ffn_W_xprojT', 'L1_ffn_W_dtT', 'L1_ffn_b_dt', 'L1_ffn_A_log',
        'L1_ffn_D', 'L1_ffn_W_out', 'L1_ffn_W_fc2T', 'L1_ffn_b_fc2']
_OUTS = [((8, 1024, 256), 'float32')]


def constants(E, CAP):
    import numpy as _np
    p = _np.arange(128)
    e = _np.arange(E)
    blk = p[:, None] // (128 // E) == p[None, :] // (128 // E)
    tri = p[:, None] < p[None, :]
    first_slot = _np.tile(e * CAP, (128, 1))
    rank = _np.tile(E - e, (128, 1))
    sel = p[:, None] == e[None, :] * (128 // E)
    return _np.concatenate([blk, tri, first_slot, rank, sel], axis=1).astype(_np.float32)


def kernel(**inputs):
    import numpy as _np
    import concourse.bacc as _bacc
    from concourse import mybir as _mybir
    from concourse.bass_utils import run_bass_kernel_spmd as _run
    E = inputs["L0_ffn_w1"].shape[0]
    T = inputs["x"].shape[0] * inputs["x"].shape[1]
    nc = _bacc.Bacc("TRN2", target_bir_lowering=False, num_devices=1)
    arrays, args = {}, []
    for name in _INS:
        if name == "consts":
            a = constants(E, int(1.2 * T / E))
        elif name.endswith("T"):
            a = inputs[name[:-1]].T
        else:
            a = inputs[name]
        a = _np.ascontiguousarray(a)
        arrays[f"in_{name}_dram"] = a
        args.append(nc.dram_tensor(f"in_{name}_dram", a.shape, _mybir.dt.from_np(a.dtype), kind="ExternalInput").ap())
    for i, (shape, dtype) in enumerate(_OUTS):
        dt = _mybir.dt.from_np(_np.dtype(dtype))
        args.append(nc.dram_tensor(f"out_{i}_dram", shape, dt, kind="ExternalOutput").ap())
    network(nc, *args)
    r = _run(nc, [arrays], core_ids=[0])
    return r.results[0]["out_0_dram"]
```

```python
from contextlib import ExitStack

import concourse.bass as bass
from concourse import mybir

F32 = mybir.dt.float32
I32 = mybir.dt.int32
ACT = mybir.ActivationFunctionType
ALU = mybir.AluOpType
AX = mybir.AxisListType.X
P = 128


class Place:

    def __init__(self, nc, ctx, life, tag):
        self.nc, self.ctx, self.life, self.tag = nc, ctx, life, tag
        self.named = []

    def sb(self, name, shape, dt=F32):
        return self.ctx.enter_context(self.nc.sbuf_tensor(f"{self.tag}_{name}", shape, dt))

    def ps(self, name, shape, dt=F32):
        return self.ctx.enter_context(self.nc.psum_tensor(f"{self.tag}_ps_{name}", shape, dt))

    def sems(self, names):
        new = [self.life.enter_context(self.nc.semaphore(f"{self.tag}_{n}")) for n in names.split()]
        self.named += new
        return new


def clear(nc, sems):
    with nc.Block() as block:
        @block.sync
        def _(sp):
            for s in sems:
                sp.sem_clear(s)


class Chain:

    def __init__(self, eng, sem, base=0):
        self.eng, self.sem, self.base, self.n = eng, sem, base, 0

    def __call__(self, ins):
        ins.then_inc(self.sem, 1)
        self.n += 1

    def wait(self, back=0):
        if self.n > back:
            self.eng.wait_ge(self.sem, self.base + (self.n - back))


def identity(nc, pool, ident, s_ident):
    nc.gpsimd.memset(ident[:, :], 0.0).then_inc(s_ident, 1)
    pool.wait_ge(s_ident, 1)
    nc.gpsimd.affine_select(out=ident[:, :], in_=ident[:, :], compare_op=ALU.not_equal, fill=1.0, base=0,
                            pattern=[[-1, P]], channel_multiplier=1).then_inc(s_ident, 1)


def attention_phase(nc, life, dinv, x, adj, W, a, beta, gate_wT, gate_b, x1_d, xn2_d, logit_d, xg_d):
    B, N, C = x.shape
    NT = N // P
    KC = C // P
    E = gate_wT.shape[1]
    EPS = 1e-5
    SLOPE = 0.2
    ZN = 4
    ZW = xg_d.shape[0] * xg_d.shape[1] // P // ZN
    HX = C + 1
    with ExitStack() as ctx:
        m = Place(nc, ctx, life, "att")
        adj_sb = m.sb("adj", [P, NT, N])
        x_sb = m.sb("x", [P, 2, NT, C])
        w_sb = m.sb("w", [P, KC, HX])
        a_bc = m.sb("a_bc", [P, 2, C])
        wa = m.sb("wa", [P, KC, 2])
        wa2 = m.sb("wa2", [P, KC, P])
        scr = m.sb("scr", [P, C])
        beta_bc = m.sb("beta", [P, 1])
        gw = m.sb("gw", [P, KC, E])
        gb = m.sb("gb", [P, E])
        ident = m.sb("ident", [P, P])
        neghalf = m.sb("neghalf", [P, NT])
        st = m.sb("st", [P, NT, 6])
        mv = m.sb("mv", [P, NT, 2])
        ve = m.sb("ve", [P, NT])
        rstd = m.sb("rstd", [P, NT])
        xn = m.sb("xn", [P, NT, C])
        xnT = m.sb("xnT", [P, KC, N])
        h_sb = m.sb("h", [P, 2, NT, HX])
        s2_sb = m.sb("s2", [P, 2, N])
        z = m.sb("z", [P, 2, N])
        lr = m.sb("lr", [P, N])
        e_sb = m.sb("e", [P, 2, N])
        mx = m.sb("mx", [P, 2])
        nmx = m.sb("nmx", [P, 2])
        rs = m.sb("rs", [P, 4])
        rr = m.sb("rr", [P, 2])
        pr = m.sb("pr", [P, 2, N])
        prT = m.sb("prT", [P, 2, N])
        bh = m.sb("bh", [P, 2, C])
        t_sb = m.sb("t", [P, 2, C])
        mn = m.sb("mn", [P, 2, C])
        ex = m.sb("ex", [P, 2, C])
        y_sb = m.sb("y", [P, C])
        x1 = m.sb("x1", [P, NT, C])
        st2 = m.sb("st2", [P, 2, 6])
        mv2 = m.sb("mv2", [P, 2, 2])
        ve2 = m.sb("ve2", [P, 2])
        rstd2 = m.sb("rstd2", [P, 2])
        xn2 = m.sb("xn2", [P, NT, C])
        xn2T = m.sb("xn2T", [P, 2, C])
        lg = m.sb("lg", [P, NT, E])
        deg = m.sb("deg", [P, NT])
        dpos = m.sb("dpos", [P, NT])
        dpow = m.sb("dpow", [P, NT])
        zero = m.sb("zero", [P, ZW])
        ps_r = m.ps("r", [P, 2, 512])
        ps_tp = m.ps("tp", [P, 2, 512])
        ps_h = m.ps("h", [P, 2, 512])
        ps_a = m.ps("a", [P, 2, 512])

        (s_adj, s_w, s_cst, s_x0, s_x1, s_ident, s_half, s_pool, s_dve, s_act) = m.sems(
            "adj w cst x0 x1 ident half pool dve act")
        s_pool2, = m.sems("pool2")
        (s_wa, s_mv, s_rstd, s_xn, s_tp, s_rp, s_rc) = m.sems("wa mv rstd xn tp rp rc")
        (s_z, s_e, s_pr, s_prT, s_at, s_t, s_ex, s_mv2, s_rstd2, s_xn2, s_gt, s_gm, s_lg, s_xused) = m.sems(
            "z e pr prT at t ex mv2 rstd2 xn2 gt gm lg xused")
        s_tick, s_ptick, s_deg, s_dpow, s_zero, s_zst = m.sems("tick ptick deg dpow zero zst")
        s_xl = [s_x0, s_x1]
        s_st = m.sems(" ".join(f"st{i}" for i in range(NT)))
        x_v = x.rearrange("b (t p) c -> b p t c", p=P)
        x1_v = x1_d.rearrange("(t p) c -> t p c", p=P)
        xn2_v = xn2_d.rearrange("(t p) c -> t p c", p=P)
        lg_v = logit_d.rearrange("(t p) e -> t p e", p=P)
        block = ctx.enter_context(nc.Block())

        LAG_AT, LAG_T, LAG_X1, LAG_XN2, LAG_TURN, LAG_COPY, LAG_GATE, LAG_LG = 1, 2, 3, 4, 5, 6, 7, 8
        NR = 4 + 2 + NT
        READY = {5: (0, 6), 6: (6, 10), 7: (10, 14)}
        assert NT == 8

        def batches(eng, body):
            body(0, 0, True, False)
            with eng.Fori(0, B // 2 - 1) as p:
                body(p * 2 + 1, 1, False, False)
                body(p * 2 + 2, 0, False, False)
            body(B - 1, 1, False, True)

        def later(b, q, i, lag, first):
            if i >= lag:
                return b * NT + (i - lag), i - lag, q
            return None if first else (b * NT + (i - lag), i - lag + NT, 1 - q)

        def drain(step, lag):
            for o in range(NT - lag, NT):
                step((B - 1) * NT + o, o, 1)

        @block.sync
        def _(sp):
            for q in range(NT):
                sp.sem_inc(s_st[q], 16)
            sp.dma_start(w_sb[:, :, 0:C], W.rearrange("(k p) f -> p k f", p=P)).then_inc(s_w, 16)
            sp.dma_start(a_bc[:, :, :], a.rearrange("(h f) o -> o h f", h=2).broadcast_to([P, 2, C])).then_inc(s_w, 16)
            sp.dma_start(x_sb[:, 0], x_v[0]).then_inc(s_x0, 16)
            sp.dma_start(adj_sb[:, :, :], adj.rearrange("(t p) m -> p t m", p=P)).then_inc(s_adj, 16)
            sp.dma_start(x_sb[:, 1], x_v[1]).then_inc(s_x1, 16)
            sp.dma_start(gw[:, :, :], gate_wT.rearrange("(k p) e -> p k e", p=P)).then_inc(s_cst, 16)
            sp.dma_start(gb[:, :], gate_b.rearrange("(o e) -> o e", o=1).broadcast_to([P, E])).then_inc(s_cst, 16)
            sp.dma_start(beta_bc[:, :], beta.rearrange("(o e) -> o e", o=1).broadcast_to([P, 1])).then_inc(s_cst, 16)

            sp.wait_ge(s_zero, 1)
            for n in range(ZN):
                sp.dma_start(xg_d.rearrange("r c -> (r c)").rearrange("(n p w) -> n p w", n=ZN, p=P)[n], zero[:, :]).then_inc(s_zst, 16)

            def store(t, o, q):
                sp.wait_ge(s_lg, t + 2)
                for dst, src in ((x1_v, x1), (xn2_v, xn2), (lg_v, lg)):
                    sp.dma_start(dst[bass.ds(t, 1)].rearrange("o p c -> p (o c)"), src[:, o]).then_inc(s_st[o], 16)

            def batch(b, q, first, last):
                for i in range(NT):
                    if i == 3 and not first and not last:
                        sp.wait_ge(s_xused, b * NT)
                        sp.dma_start(x_sb[:, 1 - q], x_v[bass.ds(b + 1, 1)].rearrange("o p t c -> p (o t) c")).then_inc(s_xl[1 - q], 16)
                    tile = later(b, q, i, LAG_LG, first)
                    if tile:
                        store(*tile)
            batches(sp, batch)
            drain(store, LAG_LG)
            sp.wait_ge(s_zst, 16 * ZN)
            for o in range(NT):
                sp.wait_ge(s_st[o], 48 * B + 16)

        @block.gpsimd
        def _(pool):
            identity(nc, pool, ident, s_ident)
            nc.gpsimd.memset(neghalf[:, :], -0.5).then_inc(s_half, 1)
            pool.wait_ge(s_half, 1)

            def scale_batch(b):
                pool.wait_ge(s_mv, b + 1)
                pool.sem_inc(s_ptick, 1)
                nc.gpsimd.tensor_scalar(ve[:, :], mv[:, :, 1], EPS, None, ALU.add).then_inc(s_pool, 1)
                pool.wait_ge(s_pool, b + 1)
                nc.gpsimd.tensor_tensor(rstd[:, :], ve[:, :], neghalf[:, :], ALU.pow).then_inc(s_rstd, 1)

            def scale_tile(t, o, q):
                s = o % 2
                pool.wait_ge(s_mv2, t + 1)
                pool.sem_inc(s_ptick, 1)
                nc.gpsimd.tensor_scalar(ve2[:, s:s + 1], mv2[:, s, 1:2], EPS, None, ALU.add).then_inc(s_pool2, 1)
                pool.wait_ge(s_pool2, t + 1)
                nc.gpsimd.tensor_tensor(rstd2[:, s:s + 1], ve2[:, s:s + 1], neghalf[:, 0:1], ALU.pow).then_inc(s_rstd2, 1)

            def batch(b, q, first, last):
                for i in range(NT):
                    if i == 4 and not last:
                        scale_batch(b + 1)
                    tile = later(b, q, i, LAG_X1, first)
                    if tile:
                        scale_tile(*tile)
            scale_batch(0)
            pool.wait_ge(s_deg, 1)
            nc.gpsimd.tensor_tensor(dpow[:, :], deg[:, :], neghalf[:, :], ALU.pow).then_inc(s_dpow, 1)
            batches(pool, batch)
            drain(scale_tile, LAG_X1)

        @block.tensor
        def _(pe):
            pe.sem_inc(s_at, 2)
            pe.sem_inc(s_gm, 2)
            pe.wait_ge(s_ident, 2)
            pe.wait_ge(s_wa, 3)

            def ready(b, n, q):
                pe.wait_ge(s_rc, b * NR + n + 1)
                if n < 4:
                    hf, k = n // 2, n % 2
                    pe.wait_ge(s_xn, b * 2 + hf + 1)
                    for j in range(4):
                        last = nc.tensor.transpose(ps_r[:, n % 2, j * P:j * P + P], xn[:, hf * 4 + j, k * P:k * P + P], ident[:, :])
                elif n < 6:
                    hf = n - 4
                    if hf == 0:
                        pe.wait_ge(s_rc, b * NR + 4 + 2)
                    for k in range(KC):
                        last = nc.tensor.matmul(ps_r[:, n % 2, :], wa2[:, k, :], xnT[:, k, hf * 512:hf * 512 + 512],
                                                start=(k == 0), stop=(k == KC - 1))
                else:
                    i = n - 6
                    for k in range(KC):
                        last = nc.tensor.matmul(ps_r[:, n % 2, 0:HX], xnT[:, k, i * P:i * P + P], w_sb[:, k, :],
                                                start=(k == 0), stop=(k == KC - 1))
                last.then_inc(s_rp, 1)

            def turn_probs(t, o, q):
                pe.wait_ge(s_pr, t + 3)
                for hf in range(2):
                    pe.wait_ge(s_prT, t * 2 + hf + 1)
                    for j in range(4):
                        jj = hf * 4 + j
                        last = nc.tensor.transpose(ps_tp[:, hf, j * P:j * P + P], pr[:, o % 2, jj * P:jj * P + P], ident[:, :])
                    last.then_inc(s_tp, 1)

            def attend(t, o, q):
                s = o % 2
                pe.wait_ge(s_prT, t * 2 + 4)
                pe.wait_ge(s_t, t + 1)
                for j in range(NT):
                    last = nc.tensor.matmul(ps_a[:, s, 0:C], prT[:, s, j * P:j * P + P], h_sb[:, q, j, 0:C],
                                            start=(j == 0), stop=(j == NT - 1))
                last.then_inc(s_at, 1)

            def turn_rows(t, o, q):
                pe.wait_ge(s_xn2, t + 1)
                pe.wait_ge(s_act, t + 1)
                for k in range(KC):
                    last = nc.tensor.transpose(ps_h[:, 0, k * P:k * P + P], xn2[:, o, k * P:k * P + P], ident[:, :])
                last.then_inc(s_gt, 1)

            def gate(t, o, q):
                pe.wait_ge(s_act, t + 2)
                pe.wait_ge(s_lg, t + 1)
                for k in range(KC):
                    last = nc.tensor.matmul(ps_h[:, 1, 0:E], xn2T[:, o % 2, k * P:k * P + P], gw[:, k, :],
                                            start=(k == 0), stop=(k == KC - 1))
                last.then_inc(s_gm, 1)

            def batch(b, q, first, last):
                for i in range(NT):
                    turn_probs(b * NT + i, i, q)
                    if i in READY and not last:
                        for n in range(*READY[i]):
                            ready(b + 1, n, 1 - q)
                    if i == 1:
                        pe.wait_ge(s_rc, b * NR + NR + 2)
                    for step, lag in ((attend, LAG_AT), (gate, LAG_GATE), (turn_rows, LAG_TURN)):
                        tile = later(b, q, i, lag, first)
                        if tile:
                            step(*tile)
            for n in range(NR):
                ready(0, n, 0)
            batches(pe, batch)
            drain(attend, LAG_AT)
            for i in range(NT, NT + LAG_GATE):
                for step, lag in ((gate, LAG_GATE), (turn_rows, LAG_TURN)):
                    if i - lag < NT:
                        step((B - 1) * NT + i - lag, i - lag, 1)

        @block.scalar
        def _(act):
            act.sem_inc(s_z, 2)
            act.sem_inc(s_pr, 2)
            act.sem_inc(s_prT, 2)
            act.sem_inc(s_rc, 2)
            act.sem_inc(s_act, 1)

            def ready(b, n, q):
                act.wait_ge(s_rp, b * NR + n + 1)
                if n < 4:
                    hf, k = n // 2, n % 2
                    dst, src = xnT[:, k, hf * 512:hf * 512 + 512], ps_r[:, n % 2, :]
                elif n < 6:
                    dst, src = s2_sb[:, q, (n - 4) * 512:(n - 4) * 512 + 512], ps_r[:, n % 2, :]
                else:
                    dst, src = h_sb[:, q, n - 6, :], ps_r[:, n % 2, 0:HX]
                nc.scalar.activation(dst, src, ACT.Copy).then_inc(s_rc, 1)

            def scores(t, o, q):
                act.wait_ge(s_e, t + 1)
                nc.scalar.activation(z[:, o % 2, :], s2_sb[:, q, :], ACT.Identity, bias=h_sb[:, q, o, C:C + 1]).then_inc(s_z, 1)

            def copy_rows(t, o, q):
                act.wait_ge(s_gt, t + 1)
                act.wait_ge(s_gm, t + 1)
                nc.scalar.activation(xn2T[:, o % 2, :], ps_h[:, 0, 0:C], ACT.Copy).then_inc(s_act, 1)

            def elu(t, o, q):
                act.wait_ge(s_t, t + 3)
                nc.scalar.activation(ex[:, o % 2, :], mn[:, o % 2, :], ACT.Exp).then_inc(s_ex, 1)

            def batch(b, q, first, last):
                for i in range(NT):
                    t = b * NT + i
                    s = i % 2
                    act.wait_ge(s_e, t + 3)
                    if not (first and i < 2):
                        act.wait_ge(s_tp, (t - 1) * 2)
                    nc.scalar.activation(pr[:, s, :], e_sb[:, s, :], ACT.Exp, bias=nmx[:, s:s + 1],
                                         accum_out=rs[:, i % 4:i % 4 + 1]).then_inc(s_pr, 1)
                    act.wait_ge(s_at, t + 1)
                    for hf in range(2):
                        act.wait_ge(s_tp, t * 2 + hf + 1)
                        nc.scalar.activation(prT[:, s, hf * 512:hf * 512 + 512], ps_tp[:, hf, :], ACT.Copy).then_inc(s_prT, 1)
                    if i in READY and not last:
                        for n in range(*READY[i]):
                            ready(b + 1, n, 1 - q)
                    if i + 2 < NT:
                        scores(t + 2, i + 2, q)
                    elif not last:
                        act.wait_ge(s_rc, (b + 1) * NR + 6 + (i + 3 - NT) + 2)
                        scores(t + 2, i + 2 - NT, 1 - q)
                    for step, lag in ((elu, LAG_T), (copy_rows, LAG_COPY)):
                        tile = later(b, q, i, lag, first)
                        if tile:
                            step(*tile)
            for n in range(NR):
                ready(0, n, 0)
            act.wait_ge(s_rc, NR + 2)
            scores(0, 0, 0)
            scores(1, 1, 0)
            batches(act, batch)
            drain(elu, LAG_T)
            drain(copy_rows, LAG_COPY)

        @block.vector
        def _(dve):
            dve.sem_inc(s_e, 2)
            dve.sem_inc(s_t, 2)
            dve.sem_inc(s_lg, 1)
            nc.vector.memset(zero[:, :], 0.0).then_inc(s_zero, 1)
            own = Chain(dve, s_dve)
            dve.wait_ge(s_w, 32)
            for k in range(KC):
                for j in range(2):
                    own(nc.vector.tensor_tensor_reduce(out=scr[:, :], in0=w_sb[:, k, 0:C], in1=a_bc[:, j, :], scale=1.0,
                                                       scalar=0.0, op0=ALU.mult, op1=ALU.add, accum_out=wa[:, k, j:j + 1]))
                    own.wait()
            nc.vector.tensor_copy(w_sb[:, :, C:C + 1], wa[:, :, 0:1]).then_inc(s_wa, 1)
            for k in range(KC):
                nc.vector.tensor_copy(wa2[:, k, :], wa[:, k, 1:2].to_broadcast([P, P])).then_inc(s_wa, 1)
            own_n = own.n

            class state:
                ch = None

            def statistics(b, q):
                ch = state.ch
                dve.wait_ge(s_xl[q], (b - q) * 8 + 16)
                for i in range(NT):
                    ch(nc.vector.bn_stats(st[:, i, :], x_sb[:, q, i, :]))
                ch.wait()
                dve.sem_inc(s_tick, 1)
                for i in range(NT):
                    last = nc.vector.bn_aggr(mv[:, i, :], st[:, i, :])
                last.then_inc(s_mv, 1)

            def normalise(b, q, hf):
                if hf == 0:
                    dve.wait_ge(s_mv, b + 1)
                    dve.wait_ge(s_rstd, b + 1)
                for i in range(hf * 4, hf * 4 + 4):
                    last = nc.vector.tensor_scalar(xn[:, i, :], x_sb[:, q, i, :], mv[:, i, 0:1], rstd[:, i:i + 1],
                                                   ALU.subtract, ALU.mult)
                last.then_inc(s_xn, 1)

            def leaky(t, o):
                ch, s = state.ch, o % 2
                dve.wait_ge(s_z, t + 3)
                ch(nc.vector.scalar_tensor_tensor(out=lr[:, :], in0=z[:, s, :], scalar=SLOPE, in1=z[:, s, :],
                                                  op0=ALU.mult, op1=ALU.max))
                ch.wait()
                dve.wait_ge(s_pr, t + 1)
                dve.sem_inc(s_tick, 1)
                ch(nc.vector.tensor_tensor_reduce(out=e_sb[:, s, :], in0=lr[:, :], in1=adj_sb[:, o, :], scale=1.0,
                                                  scalar=-3.0e38, op0=ALU.mult, op1=ALU.max, accum_out=mx[:, s:s + 1]))
                ch.wait()
                nc.vector.tensor_scalar(nmx[:, s:s + 1], mx[:, s:s + 1], -1.0, None, ALU.mult).then_inc(s_e, 1)

            def mix(t, o, q):
                ch, s = state.ch, o % 2
                dve.wait_ge(s_pr, t + 3)
                ch(nc.vector.reciprocal(rr[:, s:s + 1], rs[:, o % 4:o % 4 + 1]))
                ch(nc.vector.tensor_scalar(bh[:, s, :], h_sb[:, q, o, 0:C], beta_bc[:, 0:1], None, ALU.mult))
                ch.wait()
                dve.wait_ge(s_at, t + 3)
                ch(nc.vector.scalar_tensor_tensor(out=t_sb[:, s, :], in0=ps_a[:, s, 0:C], scalar=rr[:, s:s + 1],
                                                  in1=bh[:, s, :], op0=ALU.mult, op1=ALU.add))
                ch.wait()
                nc.vector.tensor_scalar(mn[:, s, :], t_sb[:, s, :], 0.0, None, ALU.min).then_inc(s_t, 1)

            def residual(t, o, q):
                ch, s = state.ch, o % 2
                dve.wait_ge(s_ex, t + 1)
                ch(nc.vector.scalar_tensor_tensor(out=y_sb[:, :], in0=t_sb[:, s, :], scalar=0.0, in1=ex[:, s, :],
                                                  op0=ALU.max, op1=ALU.add))
                ch.wait()
                dve.wait_ge(s_st[o], (t - o) * 6 + 16)
                nc.vector.scalar_tensor_tensor(out=x1[:, o, :], in0=y_sb[:, :], scalar=-1.0, in1=x_sb[:, q, o, :],
                                               op0=ALU.add, op1=ALU.add).then_inc(s_xused, 1)
                dve.wait_ge(s_xused, t + 1)
                ch(nc.vector.bn_stats(st2[:, s, :], x1[:, o, :]))
                ch.wait()
                dve.sem_inc(s_tick, 1)
                nc.vector.bn_aggr(mv2[:, s, :], st2[:, s, :]).then_inc(s_mv2, 1)

            def normalise_tile(t, o, q):
                s = o % 2
                dve.wait_ge(s_mv2, t + 1)
                dve.wait_ge(s_rstd2, t + 1)
                nc.vector.tensor_scalar(xn2[:, o, :], x1[:, o, :], mv2[:, s, 0:1], rstd2[:, s:s + 1],
                                        ALU.subtract, ALU.mult).then_inc(s_xn2, 1)

            def logits(t, o, q):
                dve.wait_ge(s_gm, t + 3)
                nc.vector.tensor_tensor(lg[:, o, :], ps_h[:, 1, 0:E], gb[:, :], ALU.add).then_inc(s_lg, 1)

            late = ((normalise_tile, LAG_XN2), (mix, LAG_T), (residual, LAG_X1), (logits, LAG_LG))

            def batch(b, q, first, last, base):
                state.ch = Chain(dve, s_dve, base)
                state.ch.n = 0
                for i in range(NT):
                    if i == 4 and not last:
                        statistics(b + 1, 1 - q)
                    if i + 1 < NT:
                        leaky(b * NT + i + 1, i + 1)
                    elif not last:
                        leaky((b + 1) * NT, 0)
                    for step, lag in late:
                        tile = later(b, q, i, lag, first)
                        if tile:
                            step(*tile)
                    if i == 4 and not last:
                        normalise(b + 1, 1 - q, 0)
                        normalise(b + 1, 1 - q, 1)
                return state.ch.n

            state.ch = Chain(dve, s_dve, 0)
            state.ch.n = own_n
            statistics(0, 0)
            normalise(0, 0, 0)
            normalise(0, 0, 1)
            dve.wait_ge(s_adj, 16)
            state.ch(nc.vector.tensor_reduce(deg[:, :], adj_sb[:, :, :], AX, ALU.add))
            state.ch.wait()
            state.ch(nc.vector.tensor_scalar(dpos[:, :], deg[:, :], 0.0, None, ALU.is_gt))
            state.ch.wait()
            nc.vector.tensor_scalar(deg[:, :], deg[:, :], 1e-37, None, ALU.max).then_inc(s_deg, 1)
            dve.wait_ge(s_dpow, 1)
            state.ch(nc.vector.tensor_tensor(dinv[:, :], dpow[:, :], dpos[:, :], ALU.mult))
            dve.wait_ge(s_cst, 48)
            leaky(0, 0)
            start = state.ch.n
            start += batch(0, 0, True, False, start)
            steps = NT + 2 * NT + 5 * NT
            with dve.Fori(0, B // 2 - 1) as p:
                assert batch(p * 2 + 1, 1, False, False, p * (2 * steps) + start) == steps
                assert batch(p * 2 + 2, 0, False, False, p * (2 * steps) + (start + steps)) == steps
            batch(B - 1, 1, False, True, start + (B - 2) * steps)
            for i in range(NT, NT + LAG_LG):
                for step, lag in late:
                    if i - lag < NT:
                        step((B - 1) * NT + i - lag, i - lag, 1)
    return m.named


class WeightProducts:

    def __init__(self, nc, m, keep, W_inT, W_fc1, b_fc1, W_out, W_fc2T):
        self.nc, self.keep, self.weights = nc, keep, (W_inT, W_fc1, b_fc1, W_out, W_fc2T)
        M, E2 = W_inT.shape
        C, DI, O = W_fc1.shape[1], W_out.shape[1], W_fc2T.shape[1]
        self.KM, self.KC, self.KD, self.KE, self.O = M // P, C // P, DI // P, E2 // P, O
        self.wi = m.sb("wi", [P, self.KM, E2])
        self.f1 = m.sb("f1", [P, self.KM, C])
        self.b1 = m.sb("b1", [P, self.KM])
        self.wo = m.sb("wo", [P, self.KM, DI])
        self.f2 = m.sb("f2", [P, self.KM, O])
        self.ps = m.ps("wp", [P, 3, 512])
        self.ps_b = m.ps("wb", [P, self.KE])
        self.s_in, self.s_mm, self.s_ev, self.s_b, self.s_bc = m.sems("win wmm wev wb wbc")
        self.NF = self.KC * (E2 // 512)
        self.NO = self.KD // 2

    def load(self, sp):
        W_inT, W_fc1, b_fc1, W_out, W_fc2T = self.weights
        sp.dma_start(self.wi[:, :, :], W_inT.rearrange("(k p) e -> p k e", p=P)).then_inc(self.s_in, 16)
        sp.dma_start(self.f1[:, :, :], W_fc1.rearrange("(k p) c -> p k c", p=P)).then_inc(self.s_in, 16)
        sp.dma_start(self.wo[:, :, :], W_out.rearrange("(k p) d -> p k d", p=P)).then_inc(self.s_in, 16)
        sp.dma_start(self.f2[:, :, :], W_fc2T.rearrange("(k p) o -> p k o", p=P)).then_inc(self.s_in, 16)
        sp.dma_start(self.b1[:, :], b_fc1.rearrange("(k p) -> p k", p=P), allow_slow_non_contiguous=True).then_inc(self.s_in, 16)

    def multiply(self, pe):
        mm, KM, KC, O, wi, ps = self.nc.tensor.matmul, self.KM, self.KC, self.O, self.wi, self.ps
        pe.wait_ge(self.s_in, 16 * 5)
        for n in range(self.NF + self.NO):
            if n >= 3:
                pe.wait_ge(self.s_ev, n - 2)
            if n < self.NF:
                c, e = n % KC, n // KC
                for k in range(KM):
                    last = mm(ps[:, n % 3, :], self.f1[:, k, c * P:c * P + P], wi[:, k, e * 512:e * 512 + 512],
                              start=(k == 0), stop=(k == KM - 1))
            else:
                for r in range(2):
                    d = 2 * (n - self.NF) + r
                    for k in range(KM):
                        last = mm(ps[:, n % 3, r * O:r * O + O], self.wo[:, k, d * P:d * P + P], self.f2[:, k, :],
                                  start=(k == 0), stop=(k == KM - 1))
            last.then_inc(self.s_mm, 1)
        for e in range(self.KE):
            for k in range(KM):
                last = mm(self.ps_b[:, e:e + 1], wi[:, k, e * P:e * P + P], self.b1[:, k:k + 1], start=(k == 0), stop=(k == KM - 1))
        last.then_inc(self.s_b, 1)

    def copy(self, act):
        wf, buz, wc = self.keep
        nc, ps, KC, NF = self.nc, self.ps, self.KC, self.NF
        for n in range(NF + self.NO):
            act.wait_ge(self.s_mm, n + 1)
            dst = wf[:, n % KC, (n // KC) * 512:(n // KC) * 512 + 512] if n < NF else wc[:, 2 * (n - NF):2 * (n - NF) + 2, :]
            src = ps[:, n % 3, :] if n < NF else ps[:, n % 3, :].rearrange("p (r o) -> p r o", r=2)
            nc.scalar.activation(dst, src, ACT.Copy).then_inc(self.s_ev, 1)
        act.wait_ge(self.s_b, 1)
        nc.scalar.activation(buz[:, :], self.ps_b[:, :], ACT.Copy).then_inc(self.s_bc, 1)




def routing_phase(nc, life, keep, consts, logit_d, xn2_d, xg_d, CAP, fused, weights):
    gidx, wk = keep
    T, E = logit_d.shape
    C = xn2_d.shape[1]
    NT = T // P
    CH = P // E
    BIG = float(2 * E * CAP)
    EXPS = [float(2.0 ** (2 ** k)) for k in range(6, -1, -1)] + [1.0]
    with ExitStack() as ctx:
        m = Place(nc, ctx, life, "rt")
        rows = m.sb("rows", [P, NT, C])
        cst = m.sb("cst", [P, 2 * P + 3 * E])
        blk, tri, ecap, rev, sel = (cst[:, 0:P], cst[:, P:2 * P], cst[:, 2 * P:2 * P + E], cst[:, 2 * P + E:2 * P + 2 * E],
                                    cst[:, 2 * P + 2 * E:2 * P + 3 * E])
        ones = m.sb("ones", [P, P])
        lg = m.sb("lg", [P, NT, E])
        pb = m.sb("pb", [P, NT, E])
        oh = m.sb("oh", [P, 2, NT, E])
        t0 = m.sb("t0", [P, NT, E])
        t1 = m.sb("t1", [P, NT, E])
        r0 = m.sb("r0", [P, NT])
        p12 = m.sb("p12", [P, 2, NT])
        v = m.sb("v", [P, E, NT])
        vc = m.sb("vc", [P, T // CH])
        cmp = m.sb("cmp", [P, T // CH])
        cnt = m.sb("cnt", [P, 1])
        g = m.sb("g", [P, 1])
        cand = m.sb("cand", [P, 1])
        delta = m.sb("delta", [P, 1])
        thr8 = m.sb("thr8", [P, E])
        thr = m.sb("thr", [P, E])
        gt = m.sb("gt", [P, E, NT])
        eq = m.sb("eq", [P, E, NT])
        inc = m.sb("inc", [P, E, NT])
        zero = m.sb("zero", [P, NT])
        room = m.sb("room", [P, E])
        kp = m.sb("kp", [P, E, NT])
        pos = m.sb("pos", [P, E, NT])
        s_k = m.sb("s_k", [P, 2, NT])
        kept = m.sb("kept", [P, 2, NT])
        sf = m.sb("sf", [P, 2, NT])
        sidx = m.sb("sidx", [P, 2, NT], I32)
        ps_c = m.ps("c", [P, 512])
        ps_g = m.ps("g", [P, 512])
        ps_i = m.ps("i", [P, E * NT])
        ps_t = m.ps("t", [P, E * NT])
        (s_in, s_rows, s_dve, s_act, s_v, s_vc, s_vr, s_cnt, s_tot, s_thr, s_m, s_pm, s_sidx, s_sc, s_sub) = m.sems(
            "in rows dve act v vc vr cnt tot thr m pm sidx sc sub")
        v_d = nc.dram_tensor("rt_v_dram", (E, P, NT), F32, kind="Internal").ap()
        block = ctx.enter_context(nc.Block())
        products = WeightProducts(nc, m, fused, *weights)
        NI = len(EXPS) - 1
        NM = 23

        @block.sync
        def _(sp):
            sp.dma_start(lg[:, :, :], logit_d.rearrange("(t p) e -> p t e", p=P)).then_inc(s_in, 16)
            sp.dma_start(cst[:, :], consts).then_inc(s_in, 16)
            sp.dma_start(rows[:, :, :], xn2_d.rearrange("(t p) c -> p t c", p=P)).then_inc(s_rows, 16)
            sp.wait_ge(s_v, 1)
            sp.dma_start(v_d.rearrange("e p t -> p e t"), v[:, :, :]).then_inc(s_vc, 16)
            sp.wait_ge(s_vc, 16)
            sp.dma_start(vc[:, :], v_d.rearrange("e (c q) t -> (e c) (q t)", c=CH)).then_inc(s_vr, 16)
            products.load(sp)
            sp.wait_ge(s_vr, 16)

        @block.scalar
        def _(act):
            act.wait_ge(s_sub, 1)
            nc.scalar.activation(t1[:, :, :], t0[:, :, :], ACT.Exp).then_inc(s_act, 1)
            products.copy(act)

        @block.tensor
        def _(pe):
            pe.wait_ge(s_in, 32)
            for n in range(NI):
                pe.wait_ge(s_cnt, n + 1)
                nc.tensor.matmul(ps_c[:, 0:1], blk, cnt[:, :], start=True, stop=True).then_inc(s_tot, 1)
            with pe.Fori(0, NM) as n:
                pe.wait_ge(s_cnt, n + NI + 1)
                nc.tensor.matmul(ps_c[:, 0:1], blk, cnt[:, :], start=True, stop=True).then_inc(s_tot, 1)
            pe.wait_ge(s_thr, 1)
            nc.tensor.matmul(ps_g[:, 0:E], ones[:, :], thr8[:, :], start=True, stop=True).then_inc(s_tot, 1)
            pe.wait_ge(s_m, 1)
            nc.tensor.matmul(ps_c[:, :], ones[:, :], gt[:, :, :].rearrange("p e t -> p (e t)"), start=True, stop=True)
            nc.tensor.matmul(ps_i[:, :], tri, eq[:, :, :].rearrange("p e t -> p (e t)"), start=True, stop=True)
            nc.tensor.matmul(ps_t[:, :], ones[:, :], eq[:, :, :].rearrange("p e t -> p (e t)"), start=True,
                             stop=True).then_inc(s_pm, 1)
            pe.wait_ge(s_m, 2)
            nc.tensor.matmul(ps_i[:, :], tri, kp[:, :, :].rearrange("p e t -> p (e t)"), start=True, stop=True)
            nc.tensor.matmul(ps_t[:, :], ones[:, :], kp[:, :, :].rearrange("p e t -> p (e t)"), start=True,
                             stop=True).then_inc(s_pm, 1)
            products.multiply(pe)

        @block.gpsimd
        def _(pool):
            pool.wait_ge(s_sidx, 1)
            pool.wait_ge(s_rows, 16)
            for t in range(NT):
                for k in range(2):
                    pool.indirect_dma_start(out=xg_d, out_offset=bass.IndirectOffsetOnAxis(ap=sidx[:, k, t:t + 1], axis=0),
                                            in_=rows[:, t, :], in_offset=None, bounds_check=E * CAP - 1,
                                            oob_is_err=False).then_inc(s_sc, 16)
            pool.wait_ge(s_sc, 16 * 2 * NT)

        @block.vector
        def _(dve):
            own = Chain(dve, s_dve)
            V = nc.vector

            def do(ins):
                own(ins)
                own.wait()

            do(V.memset(ones[:, :], 1.0))
            do(V.memset(zero[:, :], 0.0))
            do(V.memset(cand[:, :], float(2.0 ** -126 * EXPS[0])))
            dve.wait_ge(s_in, 32)
            bc = lambda a: a.unsqueeze(2).broadcast_to([P, NT, E])
            do(V.tensor_reduce(r0[:, :], lg[:, :, :], AX, ALU.max))
            V.tensor_tensor(t0[:, :, :], lg[:, :, :], bc(r0[:, :]), ALU.subtract).then_inc(s_sub, 1)
            dve.wait_ge(s_act, 1)
            do(V.tensor_reduce(r0[:, :], t1[:, :, :], AX, ALU.add))
            do(V.reciprocal(r0[:, :], r0[:, :]))
            do(V.tensor_tensor(pb[:, :, :], t1[:, :, :], bc(r0[:, :]), ALU.mult))
            revb = rev.unsqueeze(1).broadcast_to([P, NT, E])
            for k in range(2):
                src = pb if k == 0 else t1
                do(V.tensor_reduce(p12[:, k, :], src[:, :, :], AX, ALU.max))
                do(V.tensor_tensor(t0[:, :, :], src[:, :, :], bc(p12[:, k, :]), ALU.is_equal))
                do(V.tensor_tensor(t0[:, :, :], t0[:, :, :], revb, ALU.mult))
                do(V.tensor_reduce(r0[:, :], t0[:, :, :], AX, ALU.max))
                do(V.tensor_tensor(oh[:, k], t0[:, :, :], bc(r0[:, :]), ALU.is_equal))
                if k == 0:
                    do(V.scalar_tensor_tensor(out=t1[:, :, :], in0=oh[:, 0], scalar=-2.0, in1=pb[:, :, :],
                                              op0=ALU.mult, op1=ALU.add))
            do(V.tensor_tensor(t0[:, :, :], oh[:, 0], oh[:, 1], ALU.add))
            V.tensor_tensor(v[:, :, :].rearrange("p e t -> p t e"), t0[:, :, :], pb[:, :, :], ALU.mult).then_inc(s_v, 1)
            dve.wait_ge(s_v, 1)
            dve.wait_ge(s_vr, 16)

            def count(tick):
                do(V.tensor_scalar(cmp[:, :], vc[:, :], cand[:, 0:1], None, ALU.is_ge))
                V.tensor_reduce(cnt[:, :], cmp[:, :], AX, ALU.add).then_inc(s_cnt, 1)
                dve.wait_ge(s_tot, tick)

            for n in range(NI):
                nxt, r = EXPS[n + 1], EXPS[n + 1] / EXPS[n]
                count(n + 1)
                do(V.tensor_scalar(g[:, :], ps_c[:, 0:1], float(CAP), nxt - r, ALU.is_ge, ALU.mult))
                do(V.scalar_tensor_tensor(out=cand[:, :], in0=g[:, :], scalar=r, in1=cand[:, :], op0=ALU.add, op1=ALU.mult))
            do(V.tensor_scalar(delta[:, :], cand[:, :], 0.5, None, ALU.mult))
            do(V.tensor_tensor(cand[:, :], cand[:, :], delta[:, :], ALU.add))
            at = own.n
            with dve.Fori(0, NM - 1) as n:
                own = Chain(dve, s_dve, n * 5 + at)
                do(V.tensor_scalar(cmp[:, :], vc[:, :], cand[:, 0:1], None, ALU.is_ge))
                V.tensor_reduce(cnt[:, :], cmp[:, :], AX, ALU.add).then_inc(s_cnt, 1)
                dve.wait_ge(s_tot, n + NI + 1)
                do(V.tensor_scalar(g[:, :], ps_c[:, 0:1], float(CAP), 0.5, ALU.is_ge, ALU.subtract))
                do(V.tensor_tensor(g[:, :], g[:, :], delta[:, :], ALU.mult))
                do(V.tensor_tensor(cand[:, :], cand[:, :], g[:, :], ALU.add))
                do(V.tensor_scalar(delta[:, :], delta[:, :], 0.5, None, ALU.mult))
            own = Chain(dve, s_dve)
            own.n = at + 5 * (NM - 1)
            count(NI + NM)
            do(V.tensor_scalar(g[:, :], ps_c[:, 0:1], float(CAP), 1.0, ALU.is_ge, ALU.subtract))
            do(V.tensor_tensor(g[:, :], g[:, :], delta[:, :], ALU.mult))
            do(V.tensor_tensor(cand[:, :], cand[:, :], g[:, :], ALU.add))
            V.tensor_scalar(thr8[:, :], sel, cand[:, 0:1], None, ALU.mult).then_inc(s_thr, 1)
            dve.wait_ge(s_tot, NI + NM + 1)
            do(V.tensor_copy(thr[:, :], ps_g[:, 0:E]))
            thrb = thr[:, :].unsqueeze(2).broadcast_to([P, E, NT])
            do(V.tensor_tensor(gt[:, :, :], v[:, :, :], thrb, ALU.is_gt))
            V.tensor_tensor(eq[:, :, :], v[:, :, :], thrb, ALU.is_equal).then_inc(s_m, 1)

            def prefix():
                for e in range(E):
                    own(V.tensor_tensor_scan(out=inc[:, e, :], data0=ps_t[:, e * NT:(e + 1) * NT], data1=zero[:, :],
                                             initial=0.0, op0=ALU.add, op1=ALU.add))
                own.wait()
                do(V.tensor_tensor(pos[:, :, :].rearrange("p e t -> p (e t)"), inc[:, :, :].rearrange("p e t -> p (e t)"),
                                   ps_t[:, :], ALU.subtract))
                do(V.tensor_tensor(pos[:, :, :].rearrange("p e t -> p (e t)"), pos[:, :, :].rearrange("p e t -> p (e t)"),
                                   ps_i[:, :], ALU.add))

            dve.wait_ge(s_pm, 1)
            do(V.tensor_reduce(room[:, :], ps_c[:, :].rearrange("p (e t) -> p e t", e=E), AX, ALU.add))
            do(V.tensor_scalar(room[:, :], room[:, :], -1.0, float(CAP), ALU.mult, ALU.add))
            prefix()
            do(V.tensor_tensor(kp[:, :, :], pos[:, :, :], room[:, :].unsqueeze(2).broadcast_to([P, E, NT]), ALU.is_lt))
            do(V.tensor_tensor(kp[:, :, :], kp[:, :, :], eq[:, :, :], ALU.mult))
            V.tensor_tensor(kp[:, :, :], kp[:, :, :], gt[:, :, :], ALU.add).then_inc(s_m, 1)
            dve.wait_ge(s_pm, 2)
            prefix()
            do(V.tensor_tensor(pos[:, :, :], pos[:, :, :], ecap.unsqueeze(2).broadcast_to([P, E, NT]), ALU.add))
            for k in range(2):
                for src, dst in ((pos, s_k), (kp, kept)):
                    do(V.tensor_tensor(t0[:, :, :], oh[:, k], src[:, :, :].rearrange("p e t -> p t e"), ALU.mult))
                    do(V.tensor_reduce(dst[:, k, :], t0[:, :, :], AX, ALU.add))
            own(V.tensor_tensor(wk[:, :, :], kept[:, :, :], p12[:, :, :], ALU.mult))
            own(V.tensor_tensor(gidx[:, :, :], kept[:, :, :], s_k[:, :, :], ALU.mult))
            do(V.tensor_scalar(sf[:, :, :], kept[:, :, :], -BIG, BIG, ALU.mult, ALU.add))
            V.tensor_tensor(sidx[:, :, :], sf[:, :, :], s_k[:, :, :], ALU.add).then_inc(s_sidx, 1)


def experts_phase(nc, life, xg_d, w1, b1T, w2, b2, y_d, CAP):
    E, C, H = w1.shape
    KC, KH = C // P, H // P
    NR = -(-CAP // P)
    FULL = CAP // P
    TAIL = CAP - FULL * P
    NCH = 4
    CW = CAP // NCH
    assert CAP % NCH == 0 and CW <= 512 and TAIL
    with ExitStack() as ctx:
        m = Place(nc, ctx, life, "ex")
        xg = m.sb("xg", [P, 2, NR, C])
        xgT = m.sb("xgT", [P, KC, CAP])
        w1s = m.sb("w1", [P, 2, KC, H])
        w2s = m.sb("w2", [P, 2, KH, C])
        b1s = m.sb("b1", [P, KH, E])
        b1c = m.sb("b1c", [P, KH])
        b2s = m.sb("b2", [P, E, C])
        hT = m.sb("hT", [P, KH, CAP])
        o_sb = m.sb("o", [P, 4, C])
        ident = m.sb("ident", [P, P])
        ps1 = m.ps("1", [P, 4, 512])
        ps2 = m.ps("2", [P, 2, 512])
        ps_tp = m.ps("tp", [P, 2, 512])
        (s_id, s_w0, s_w1, s_b, s_x0, s_x1, s_tp, s_xT, s_p1, s_h, s_p2, s_o, s_y0, s_y1, s_y2, s_y3, s_bc, s_tick) = m.sems(
            "id w0 w1 b x0 x1 tp xT p1 h p2 o y0 y1 y2 y3 bc tick")
        s_w, s_x, s_y = [s_w0, s_w1], [s_x0, s_x1], [s_y0, s_y1, s_y2, s_y3]
        block = ctx.enter_context(nc.Block())
        size = lambda r: P if r < FULL else TAIL
        w1_v = w1.rearrange("e (k p) h -> e p k h", p=P)
        w2_v = w2.rearrange("e (k p) d -> e p k d", p=P)
        xg_v = xg_d.rearrange("(e r) c -> e r c", e=E)
        y_v = y_d.rearrange("(e r) c -> e r c", e=E)
        one = "o a b c -> a (o b) c"

        @block.sync
        def _(sp):
            for q in range(4):
                sp.sem_inc(s_y[q], 16)
            sp.dma_start(b1s[:, :, :], b1T.rearrange("(j p) e -> p j e", p=P)).then_inc(s_b, 16)
            sp.dma_start(b2s[:, :, :], b2.rearrange("(o e) d -> o e d", o=1).broadcast_to([P, E, C])).then_inc(s_b, 16)

            def load(e, q):
                sp.dma_start(xg[:, q, 0:FULL, :], xg_v[bass.ds(e, 1), 0:FULL * P].rearrange("o (r p) c -> p (o r) c", p=P)).then_inc(s_x[q], 16)
                sp.dma_start(xg[0:TAIL, q, FULL, :], xg_v[bass.ds(e, 1), FULL * P:CAP].rearrange("o r c -> r (o c)")).then_inc(s_x[q], 16)
                sp.dma_start(w1s[:, q], w1_v[bass.ds(e, 1)].rearrange("o p k h -> p (o k) h")).then_inc(s_w[q], 16)
                sp.dma_start(w2s[:, q], w2_v[bass.ds(e, 1)].rearrange("o p k h -> p (o k) h")).then_inc(s_w[q], 16)

            load(0, 0)
            load(1, 1)

            def expert(e, q, more):
                for r in range(NR):
                    sp.wait_ge(s_o, e * NR + r + 3)
                    sp.dma_start(y_v[bass.ds(e, 1), r * P:r * P + size(r)].rearrange("o r c -> r (o c)"),
                                 o_sb[0:size(r), (q * NR + r) % 4, :]).then_inc(s_y[(q * NR + r) % 4], 16)
                if more:
                    sp.wait_ge(s_p2, e * NR + NR)
                    load(e + 2, q)
            with sp.Fori(0, E // 2 - 1) as pair:
                for q in range(2):
                    expert(pair * 2 + q, q, True)
            for q in range(2):
                expert(E - 2 + q, q, False)
            for q in range(4):
                sp.wait_ge(s_y[q], 16 + 16 * (E * NR // 4))

        @block.gpsimd
        def _(pool):
            identity(nc, pool, ident, s_id)

        @block.tensor
        def _(pe):
            pe.wait_ge(s_id, 2)

            def turn(e, q):
                pe.wait_ge(s_x[q], (e - q) * 16 + 32)
                for r in range(NR):
                    n = size(r)
                    pe.wait_ge(s_xT, e * NR + r + 1)
                    for k in range(KC):
                        last = nc.tensor.transpose(ps_tp[:, r % 2, k * P:k * P + n], xg[0:n, q, r, k * P:k * P + P], ident[0:n, 0:n])
                    last.then_inc(s_tp, 1)

            def first(e, q):
                pe.wait_ge(s_w[q], (e - q) * 16 + 32)
                pe.wait_ge(s_xT, e * NR + NR + 2)
                for j in range(KH):
                    for n in range(NCH):
                        pe.wait_ge(s_h, (e * KH + j) * NCH + n + 1)
                        for k in range(KC):
                            last = nc.tensor.matmul(ps1[:, n, 0:CW], w1s[:, q, k, j * P:j * P + P], xgT[:, k, n * CW:(n + 1) * CW],
                                                    start=(k == 0), stop=(k == KC - 1))
                        last.then_inc(s_p1, 1)

            def second(e, q):
                pe.wait_ge(s_h, (e * KH + KH) * NCH + 4)
                for r in range(NR):
                    n = size(r)
                    pe.wait_ge(s_o, e * NR + r + 1)
                    for j in range(KH):
                        last = nc.tensor.matmul(ps2[0:n, r % 2, 0:C], hT[:, j, r * P:r * P + n], w2s[:, q, j, :],
                                                start=(j == 0), stop=(j == KH - 1))
                    last.then_inc(s_p2, 1)

            turn(0, 0)
            with pe.Fori(0, E // 2 - 1) as pair:
                for q in range(2):
                    first(pair * 2 + q, q)
                    turn(pair * 2 + q + 1, 1 - q)
                    second(pair * 2 + q, q)
            first(E - 2, 0)
            turn(E - 1, 1)
            second(E - 2, 0)
            first(E - 1, 1)
            second(E - 1, 1)

        @block.scalar
        def _(act):
            act.sem_inc(s_h, 4)
            act.wait_ge(s_b, 32)

            with act.Fori(0, E) as e:
                act.wait_ge(s_h, e * KH * NCH + 4)
                act.sem_inc(s_tick, 1)
                nc.scalar.activation(b1c[:, :], b1s[:, :, bass.ds(e, 1)].rearrange("p j o -> p (j o)"), ACT.Copy).then_inc(s_bc, 1)
                act.wait_ge(s_bc, e + 1)
                for j in range(KH):
                    for n in range(NCH):
                        act.wait_ge(s_p1, (e * KH + j) * NCH + n + 1)
                        nc.scalar.activation(hT[:, j, n * CW:(n + 1) * CW], ps1[:, n, 0:CW], ACT.Gelu,
                                             bias=b1c[:, j:j + 1]).then_inc(s_h, 1)

        @block.vector
        def _(dve):
            dve.sem_inc(s_xT, 2)
            dve.sem_inc(s_o, 2)

            def turned(e):
                for r in range(NR):
                    n = size(r)
                    dve.wait_ge(s_tp, e * NR + r + 1)
                    nc.vector.tensor_copy(xgT[:, :, r * P:r * P + n],
                                          ps_tp[:, r % 2, 0:KC * P].rearrange("p (k n) -> p k n", k=KC)[:, :, 0:n]).then_inc(s_xT, 1)

            def results(pair, q):
                e = pair * 2 + q
                for r in range(NR):
                    n, i = size(r), q * NR + r
                    dve.wait_ge(s_y[i % 4], pair * (32 * NR // 4) + 16 * (i // 4 + 1))
                    dve.wait_ge(s_p2, e * NR + r + 1)
                    nc.vector.tensor_tensor(o_sb[0:n, i % 4, :], ps2[0:n, r % 2, 0:C],
                                            b2s[0:n, bass.ds(e, 1), :].rearrange("p o d -> p (o d)"), ALU.add).then_inc(s_o, 1)

            dve.wait_ge(s_b, 32)
            turned(0)
            with dve.Fori(0, E // 2 - 1) as pair:
                for q in range(2):
                    turned(pair * 2 + q + 1)
                    results(pair, q)
            turned(E - 1)
            results(E // 2 - 1, 0)
            results(E // 2 - 1, 1)


def graph_phase(nc, life, keep, dinv, x1_d, y_d, adjT, weight, bias, x3_d, xn4T_d):
    gidx, wk = keep
    N = adjT.shape[0]
    T, C = x1_d.shape
    NT = N // P
    KC = C // P
    NP2 = T // N // 2
    TP = 2 * NT
    EPS = 1e-5
    LAG = dict(sum=3, norm=4, turn=5, support=6, keep=7, product=24, x3=26, norm4=27, turn4=28)
    with ExitStack() as ctx:
        m = Place(nc, ctx, life, "gr")
        aT = m.sb("aT", [P, NT, N])
        w_sb = m.sb("w", [P, KC, C])
        bias_bc = m.sb("bias", [P, C])
        ident = m.sb("ident", [P, P])
        neghalf = m.sb("neghalf", [P, 1])
        x1s = m.sb("x1", [P, 2, TP, C])
        gi = m.sb("gi", [P, 2, 2, TP], I32)
        wt = m.sb("wt", [P, 2, 2, TP])
        gat = m.sb("gat", [P, 4, 2, C])
        ta = m.sb("ta", [P, 2, C])
        x2 = m.sb("x2", [P, 2, C])
        x2b = m.sb("x2b", [P, 2, TP, C])
        xn = m.sb("xn", [P, 2, C])
        xnT = m.sb("xnT", [P, 2, C])
        sup = m.sb("sup", [P, 2, NT, 2, C])
        x3 = m.sb("x3", [P, 2, 2, C])
        xn4 = m.sb("xn4", [P, 2, C])
        xT4 = m.sb("xT4", [P, 4, C])
        st = [m.sb(f"st{k}", [P, 2, 6]) for k in range(2)]
        mv = [m.sb(f"mv{k}", [P, 2, 2]) for k in range(2)]
        ve = [m.sb(f"ve{k}", [P, 2]) for k in range(2)]
        rstd = [m.sb(f"rstd{k}", [P, 2]) for k in range(2)]
        ps_tp = m.ps("tp", [P, 2, 512])
        ps_t4 = m.ps("t4", [P, 2, 512])
        ps_s = m.ps("s", [P, 2, 512])
        ps_o = m.ps("o", [P, 2, 512])
        s_c, s_aT, s_id, s_gi, s_wt, s_x2, s_x2b, s_ta, s_sp, s_sup, s_po, s_x3, s_tick, s_pt = m.sems(
            "c aT id gi wt x2 x2b ta sp sup po x3 tick pt")
        s_x, s_g, s_st, s_s = m.sems("x0 x1"), m.sems("g0 g1 g2 g3"), m.sems("st0 st1"), m.sems("s0 s1 s2 s3")
        s_bn, s_mv, s_ve, s_rstd, s_xn, s_tp, s_xT = [m.sems(f"{n}a {n}b") for n in ("bn", "mv", "ve", "rstd", "xn", "tp", "xT")]
        block = ctx.enter_context(nc.Block())
        x1_v = x1_d.rearrange("(b q t p) c -> b p (q t) c", p=P, q=2, t=NT)
        x3_v = x3_d.rearrange("(b q t p) c -> b t p q c", p=P, q=2, t=NT)
        xT_v = xn4T_d.rearrange("k p (b i n) -> b i p k n", n=P, i=TP)

        def blocks(eng, body):
            body(0, 0)
            body(1, 1)
            with eng.Fori(0, NP2 // 2 - 1) as k:
                body(k * 2 + 2, 0)
                body(k * 2 + 3, 1)
            body(NP2, 0)
            body(NP2 + 1, 1)

        def item(p, slot, u, step):
            back, i = divmod(LAG.get(step, 0) - u + TP - 1, TP)
            i = TP - 1 - i
            if isinstance(p, int) and not 0 <= p - back < NP2:
                return None
            return p - back if back else p, (slot - back) % 2, i

        def turns(eng, steps):
            def body(p, slot):
                for u in range(TP):
                    for name, step in steps:
                        what = item(p, slot, u, name)
                        if what:
                            step(*what)
            blocks(eng, body)

        @block.sync
        def _(sp):
            for q in range(4):
                sp.sem_inc(s_s[q], 16)
            for q in range(2):
                sp.sem_inc(s_st[q], 16)
            sp.dma_start(w_sb[:, :, :], weight.rearrange("(k p) f -> p k f", p=P)).then_inc(s_c, 16)
            sp.dma_start(bias_bc[:, :], bias.rearrange("(o e) -> o e", o=1).broadcast_to([P, C])).then_inc(s_c, 16)
            sp.dma_start(x1s[:, 0], x1_v[0]).then_inc(s_x[0], 16)
            sp.dma_start(aT[:, :, :], adjT.rearrange("(t p) n -> p t n", p=P)).then_inc(s_aT, 16)
            sp.dma_start(x1s[:, 1], x1_v[1]).then_inc(s_x[1], 16)

            def load(p, q, i):
                if i == TP - 1 and not (isinstance(p, int) and p + 2 >= NP2):
                    sp.wait_ge(s_x2, p * TP + TP)
                    sp.dma_start(x1s[:, q], x1_v[bass.ds(p + 2, 1)].rearrange("o p t c -> p (o t) c")).then_inc(s_x[q], 16)

            def store(p, q, i):
                n, r = i // 2, i % 2
                if r == 0:
                    sp.wait_ge(s_x3, p * TP + i + 2)
                    sp.dma_start(x3_v[bass.ds(p, 1), n].rearrange("o p q c -> p (o q) c"), x3[:, n % 2]).then_inc(s_st[n % 2], 16)
                sp.wait_ge(s_xT[1], p * TP + i + 3)
                sp.dma_start(xT_v[bass.ds(p, 1), r * NT + n].rearrange("o p k n -> p (o k) n"),
                             xT4[:, i % 4, :].rearrange("p (k n) -> p k n", k=KC)).then_inc(s_s[i % 4], 16)
            turns(sp, (("keep", load), ("turn4", store)))
            for q in range(2):
                sp.wait_ge(s_st[q], 16 + 16 * NP2 * NT // 2)
            for q in range(4):
                sp.wait_ge(s_s[q], 16 + 16 * NP2 * TP // 4)

        @block.gpsimd
        def _(pool):
            pool.sem_inc(s_x2b, 2)
            identity(nc, pool, ident, s_id)
            nc.gpsimd.memset(neghalf[:, :], -0.5).then_inc(s_id, 1)
            pool.wait_ge(s_id, 3)

            def scale(k, p, i):
                s = i % 2
                pool.wait_ge(s_mv[k], p * TP + i + 1)
                pool.sem_inc(s_pt, 1)
                nc.gpsimd.tensor_scalar(ve[k][:, s:s + 1], mv[k][:, s, 1:2], EPS, None, ALU.add).then_inc(s_ve[k], 1)
                pool.wait_ge(s_ve[k], p * TP + i + 1)
                nc.gpsimd.tensor_tensor(rstd[k][:, s:s + 1], ve[k][:, s:s + 1], neghalf[:, :], ALU.pow).then_inc(s_rstd[k], 1)

            def gather(p, q, i):
                if i == 0:
                    nc.gpsimd.tensor_copy(gi[:, q], gidx[:, :, bass.ds(p * TP, TP)]).then_inc(s_gi, 1)
                    pool.wait_ge(s_gi, p + 1)
                    pool.sem_inc(s_pt, 1)
                if not (isinstance(p, int) and p * TP + i < 4):
                    pool.wait_ge(s_x2, p * TP + i - 3)
                    pool.sem_inc(s_pt, 1)
                for k in range(2):
                    pool.indirect_dma_start(out=gat[:, i % 4, k, :], out_offset=None, in_=y_d,
                                            in_offset=bass.IndirectOffsetOnAxis(ap=gi[:, q, k, i:i + 1], axis=0)).then_inc(s_g[i % 4], 16)

            def after_sum(p, q, i):
                scale(0, p, i)
                if i == 0 and isinstance(p, int) and p == 0:
                    pool.wait_ge(s_c, 32)
                if not (isinstance(p, int) and p < 2):
                    pool.wait_ge(s_x3, (p - 2) * TP + 2 * (i % NT) + i // NT + 1)
                nc.gpsimd.tensor_tensor(x2b[:, q, i, :], x2[:, i % 2, :], bias_bc[:, :], ALU.add).then_inc(s_x2b, 1)

            turns(pool, (("gather", gather), ("x3", lambda p, q, i: scale(1, p, i)), ("sum", after_sum)))

        @block.tensor
        def _(pe):
            for k in range(2):
                pe.sem_inc(s_tp[k], 2)
            pe.wait_ge(s_id, 2)
            pe.wait_ge(s_c, 32)

            def turn(k, src, dst, p, i):
                pe.wait_ge(s_xn[k], p * TP + i + 1)
                pe.wait_ge(s_xT[k], p * TP + i + 1)
                for c in range(KC):
                    last = nc.tensor.transpose(dst[:, i % 2, c * P:c * P + P], src[:, i % 2, c * P:c * P + P], ident[:, :])
                last.then_inc(s_tp[k], 1)

            def support(p, q, i):
                pe.wait_ge(s_xT[0], p * TP + i + 3)
                pe.wait_ge(s_sup, p * TP + i + 1)
                for c in range(KC):
                    last = nc.tensor.matmul(ps_s[:, i % 2, 0:C], xnT[:, i % 2, c * P:c * P + P], w_sb[:, c, :],
                                            start=(c == 0), stop=(c == KC - 1))
                last.then_inc(s_sp, 1)

            def product(p, q, i):
                n, half = i // 2, i % 2
                if i == 0:
                    pe.wait_ge(s_sup, p * TP + TP + 2)
                    if isinstance(p, int) and p == 0:
                        pe.wait_ge(s_aT, 16)
                if half == 0 and not (isinstance(p, int) and p * NT + n < 2):
                    pe.wait_ge(s_x3, p * TP + 2 * n - 2)
                for mt in range(half * NT // 2, (half + 1) * NT // 2):
                    last = nc.tensor.matmul(ps_o[:, n % 2, :], aT[:, mt, n * P:n * P + P],
                                            sup[:, q, mt, :, :].rearrange("p q c -> p (q c)"), start=(mt == 0), stop=(mt == NT - 1))
                if half == 1:
                    last.then_inc(s_po, 1)

            turns(pe, (("product", product), ("turn", lambda p, q, i: turn(0, xn, ps_tp, p, i)), ("support", support),
                       ("turn4", lambda p, q, i: turn(1, xn4, ps_t4, p, i))))

        @block.scalar
        def _(act):
            for k in range(2):
                act.sem_inc(s_xT[k], 2)
            act.sem_inc(s_sup, 2)

            def keep_support(p, q, i):
                act.wait_ge(s_sp, p * TP + i + 1)
                if i == 0 and not (isinstance(p, int) and p < 2):
                    act.wait_ge(s_po, (p - 1) * NT)
                nc.scalar.activation(sup[:, q, i % NT, i // NT, :], ps_s[:, i % 2, 0:C], ACT.Copy,
                                     scale=dinv[:, i % NT:i % NT + 1]).then_inc(s_sup, 1)

            def copy_turned(p, q, i):
                act.wait_ge(s_tp[0], p * TP + i + 3)
                nc.scalar.activation(xnT[:, i % 2, :], ps_tp[:, i % 2, 0:C], ACT.Copy).then_inc(s_xT[0], 1)

            def copy_turned4(p, q, i):
                act.wait_ge(s_tp[1], p * TP + i + 3)
                act.wait_ge(s_s[i % 4], p * (16 * TP // 4) + 16 * (i // 4 + 1))
                nc.scalar.activation(xT4[:, i % 4, :], ps_t4[:, i % 2, 0:C], ACT.Copy).then_inc(s_xT[1], 1)

            turns(act, (("keep", keep_support), ("turn", copy_turned), ("turn4", copy_turned4)))

        @block.vector
        def _(dve):
            V = nc.vector

            def statistics(k, src, p, i):
                V.bn_stats(st[k][:, i % 2, :], src).then_inc(s_bn[k], 1)
                dve.wait_ge(s_bn[k], p * TP + i + 1)
                dve.sem_inc(s_tick, 1)
                V.bn_aggr(mv[k][:, i % 2, :], st[k][:, i % 2, :]).then_inc(s_mv[k], 1)

            def normalise(k, src, dst, p, i):
                s = i % 2
                dve.wait_ge(s_mv[k], p * TP + i + 1)
                dve.wait_ge(s_rstd[k], p * TP + i + 1)
                dve.wait_ge(s_tp[k], p * TP + i + 1)
                V.tensor_scalar(dst, src, mv[k][:, s, 0:1], rstd[k][:, s:s + 1], ALU.subtract, ALU.mult).then_inc(s_xn[k], 1)

            def add_experts(p, q, i):
                s = i % 2
                if i == 0:
                    dve.wait_ge(s_x[q], p * 8 - q * 8 + 16)
                    V.tensor_copy(wt[:, q], wk[:, :, bass.ds(p * TP, TP)]).then_inc(s_wt, 1)
                    dve.wait_ge(s_wt, p + 1)
                dve.wait_ge(s_g[i % 4], p * (8 * TP) + 32 * (i // 4 + 1))
                V.scalar_tensor_tensor(out=ta[:, s, :], in0=gat[:, i % 4, 0, :], scalar=wt[:, q, 0, i:i + 1], in1=x1s[:, q, i, :],
                                       op0=ALU.mult, op1=ALU.add).then_inc(s_ta, 1)
                dve.wait_ge(s_ta, p * TP + i + 1)
                dve.wait_ge(s_x2b, p * TP + i + 1)
                V.scalar_tensor_tensor(out=x2[:, s, :], in0=gat[:, i % 4, 1, :], scalar=wt[:, q, 1, i:i + 1], in1=ta[:, s, :],
                                       op0=ALU.mult, op1=ALU.add).then_inc(s_x2, 1)
                dve.wait_ge(s_x2, p * TP + i + 1)
                statistics(0, x2[:, s, :], p, i)

            def add_graph(p, q, i):
                n, r = i // 2, i % 2
                if r == 0:
                    dve.wait_ge(s_po, p * NT + n + 1)
                    dve.wait_ge(s_st[n % 2], p * (8 * NT) + 16 * (n // 2 + 1))
                dve.wait_ge(s_x2b, p * TP + r * NT + n + 3)
                V.scalar_tensor_tensor(out=x3[:, n % 2, r, :], in0=ps_o[:, n % 2, r * C:r * C + C], scalar=dinv[:, n:n + 1],
                                       in1=x2b[:, q, r * NT + n, :], op0=ALU.mult, op1=ALU.add).then_inc(s_x3, 1)
                dve.wait_ge(s_x3, p * TP + i + 1)
                statistics(1, x3[:, n % 2, r, :], p, i)

            turns(dve, (("norm", lambda p, q, i: normalise(0, x2[:, i % 2, :], xn[:, i % 2, :], p, i)), ("sum", add_experts),
                        ("norm4", lambda p, q, i: normalise(1, x3[:, i // 2 % 2, i % 2, :], xn4[:, i % 2, :], p, i)),
                        ("x3", add_graph)))


def mamba_phase(nc, life, keep, xn4T_d, x3_d, conv_w, conv_b, W_xprojT, W_dtT, b_dt, A_log, D, b_fc2, out, L):
    wf, buz, wc = keep
    T, C = x3_d.shape
    DI, NS = A_log.shape
    R = W_dtT.shape[0]
    KC, KD = C // P, DI // P
    F = 512
    NCH = T // F
    assert L == 2 * F
    KW = conv_w.shape[1]
    NT = F // P
    XR = R + 2 * NS
    NI = KD // 2
    NM = NS * NI
    RING = 4
    RG = 4
    SKEW = 3
    CONV = KW
    LIMIT = 40.0
    U_PE, U_ACT, U_DVE = ((2, 6), (2, 4)), ((12, 6), (12, 4)), ((11, 6), (11, 4))
    SILU_U = (35, 30)
    X_PE, DBC_ACT = ((18, 2), (26, 1)), 36
    DT_PE, DT_ACT = ((22, 7), (31, 4)), ((31, 7), (40, 4))
    LN_ACT, DE_DVE = 53, 54
    Z_PE, Z_ACT, SILU_Z = ((32, 6), (32, 6)), ((42, 6), (42, 6)), 62
    OUT_PE, OUT_PART, OUT_DVE = (6, 8), 2, (17, 8)
    DIAG_ACT = 40

    def c_dve(m):
        return m % 16 not in (0, 5, 10)

    def turn(m, steps, later=0):
        i, off = divmod(m - later - steps[0], steps[1])
        return i if off == 0 and 0 <= i < NI else -1

    def by_dve(m):
        return sum(1 for r in range(m + 1) if c_dve(r))

    NCV = by_dve(NM - 1)
    NCP = NM - NCV
    with ExitStack() as ctx:
        m_ = Place(nc, ctx, life, "mb")
        xp = m_.sb("xp", [P, KD, XR])
        wdt = m_.sb("wdt", [R, DI])
        A = m_.sb("A", [P, KD, NS])
        cw = m_.sb("cw", [P, KD, KW])
        cb = m_.sb("cb", [P, KD])
        bdt = m_.sb("bdt", [P, KD])
        Dp = m_.sb("Dp", [P, KD])
        bo = m_.sb("bo", [P, C])
        ident = m_.sb("ident", [P, P])
        diagD = m_.sb("diagD", [P, NI, P])
        xT = m_.sb("xT", [P, 2, KC, F])
        carry = m_.sb("carry", [P, KD, KW - 1])
        u = m_.sb("u", [P, KD, F])
        z = m_.sb("z", [P, KD, F])
        delta = m_.sb("delta", [P, KD, F])
        du = m_.sb("du", [P, KD, F])
        dbc = m_.sb("dbc", [XR, F])
        BC = m_.sb("BC", [P, 2, NS, F])
        dA = m_.sb("dA", [P, RING, F])
        dBu = m_.sb("dBu", [P, RING, F])
        h = m_.sb("h", [P, RING, F])
        hC = m_.sb("hC", [P, RG, F])
        hl = m_.sb("hl", [P, KD, NS])
        o_sb = m_.sb("o", [P, 2, C])
        btap = m_.sb("btap", [P, KD])
        spare = [delta[:, NI * (1 - g):NI * (2 - g), :].rearrange("p i t -> p (i t)") for g in range(2)]
        uraw = [spare[g][:, 0:2 * (F + KW - 1)].rearrange("p (n t) -> p n t", n=2) for g in range(2)]
        ps_y = m_.ps("y", [P, NI, 512])
        ps_p = m_.ps("p", [P, 2, 512])
        ps_x = m_.ps("x", [P, 512])
        ps_o = m_.ps("o", [P, 512])
        (s_w, s_tap, s_A, s_id, s_diag, s_x0, s_x1, s_pu, s_fu, s_pz, s_fz, s_zs, s_conv, s_cv, s_u, s_xp, s_db, s_st, s_dp, s_df, s_ln) = m_.sems(
            "w tap A id diag x0 x1 pu fu pz fz zs conv cv u xp db st dp df ln")
        (s_de, s_du, s_da, s_dB, s_sc, s_hl, s_cp, s_cd, s_D, s_y, s_yr, s_om, s_oa, s_ov, s_x30, s_x31, s_o0, s_o1) = m_.sems(
            "de du da dB sc hl cp cd D y yr om oa ov x30 x31 o0 o1")
        s_B = m_.sems("B0 B1 B2 B3")
        s_tick, = m_.sems("tick")
        s_x, s_x3, s_o = [s_x0, s_x1], [s_x30, s_x31], [s_o0, s_o1]
        BC_d = nc.dram_tensor("mb_BC_dram", (2 * NS, F), F32, kind="Internal").ap()
        block = ctx.enter_context(nc.Block())
        xT_v = xn4T_d.rearrange("k p (c t) -> c p k t", t=F)
        x3_v = x3_d.rearrange("(c t p) d -> c t p d", t=NT, p=P)
        out_v = out.rearrange("b n d -> (b n) d").rearrange("(c t p) d -> c t p d", t=NT, p=P)

        def chunks(eng, body):
            body(0, 0, 0, True, False)
            with eng.Fori(0, NCH // 2 - 1) as b:
                body(b * 2 + 1, b, 1, False, False)
                body(b * 2 + 2, b + 1, 0, False, False)
            body(NCH - 1, NCH // 2 - 1, 1, False, True)

        def one(view, c):
            return view[bass.ds(c, 1)]

        @block.sync
        def _(sp):
            for q in range(2):
                sp.sem_inc(s_o[q], 16)
            sp.dma_start(xp[:, :, :], W_xprojT.rearrange("(k p) r -> p k r", p=P)).then_inc(s_w, 16)
            sp.dma_start(wdt[:, :], W_dtT).then_inc(s_w, 16)
            sp.dma_start(A[:, :, :], A_log.rearrange("(k p) s -> p k s", p=P)).then_inc(s_w, 16)
            sp.dma_start(cw[:, :, :], conv_w.rearrange("(k p) w -> p k w", p=P)).then_inc(s_w, 16)
            sp.dma_start(bo[:, :], b_fc2.rearrange("(o e) -> o e", o=1).broadcast_to([P, C])).then_inc(s_w, 16)
            for dst, src in ((cb, conv_b), (bdt, b_dt), (Dp, D)):
                sp.dma_start(dst[:, :], src.rearrange("(k p) -> p k", p=P), allow_slow_non_contiguous=True).then_inc(s_w, 16)

            def load_x(c, slot):
                sp.dma_start(xT[:, slot, :, :], one(xT_v, c).rearrange("o p k t -> p (o k) t")).then_inc(s_x[slot], 16)

            def share_bc(c, H, groups):
                if 0 in groups:
                    sp.wait_ge(s_db, c + 2)
                    sp.dma_start(BC_d, dbc[R:XR, :]).then_inc(s_st, 16)
                    sp.wait_ge(s_st, c * 16 + 16)
                for k in groups:
                    if H is not None:
                        sp.wait_ge(s_y, H * NM + (4 * k + 4) * NI + RG)
                        sp.sem_inc(s_tick, 1)
                    for r in range(2):
                        sp.dma_start(BC[:, r, 4 * k:4 * k + 4, :], BC_d.rearrange("(o r s) t -> o r s t", o=1, r=2)[:, r, 4 * k:4 * k + 4, :]
                                     .broadcast_to([P, 4, F])).then_inc(s_B[k], 16)

            def output(c):
                for t in range(NT):
                    sp.wait_ge(s_o[t % 2], c * (16 * NT // 2) + 16 * (t // 2 + 1))
                    sp.dma_start(o_sb[:, t % 2, :], one(x3_v, c)[:, t].rearrange("o p d -> p (o d)")).then_inc(s_x3[t % 2], 16)
                    if t >= 1:
                        store(c, t - 1)
                store(c, NT - 1)

            def store(c, t):
                sp.wait_ge(s_ov, c * NT + t + 1)
                sp.dma_start(one(out_v, c)[:, t].rearrange("o p d -> p (o d)"), o_sb[:, t % 2, :]).then_inc(s_o[t % 2], 16)

            def chunk(c, bt, hf, first, last):
                if not last:
                    if not first:
                        sp.wait_ge(s_pz, c * KD)
                    load_x(c + 1, 1 - hf)
                if not first:
                    share_bc(c, 2 * c - 1, [3])
                    output(c - 1)
                if not last:
                    for k in range(4):
                        sp.wait_ge(s_B[k], c * 32 + 32)
                        sp.sem_inc(s_tick, 1)
                    share_bc(c + 1, 2 * c + 1, [0, 1, 2])
            load_x(0, 0)
            share_bc(0, None, range(4))
            chunks(sp, chunk)
            output(NCH - 1)
            for q in range(2):
                sp.wait_ge(s_o[q], 16 + 16 * NCH * NT // 2)

        @block.tensor
        def _(pe):
            pe.sem_inc(s_y, RG)
            pe.wait_ge(s_id, 2)
            pe.wait_ge(s_w, 16 * 8)

            def project(bank, slot, n, k):
                return nc.tensor.matmul(ps_p[:, bank, :], wf[:, k, n * P:n * P + P], xT[:, slot, k, :], start=(k == 0), stop=(k == KC - 1))

            def x_product(c, k):
                pe.wait_ge(s_u, c * KD + k + 1)
                if k == 0:
                    pe.wait_ge(s_db, c + 1)
                last = nc.tensor.matmul(ps_x[0:XR, :], xp[:, k, :], u[:, k, :], start=(k == 0), stop=(k == KD - 1))
                if k == KD - 1:
                    last.then_inc(s_xp, 1)

            def dt_product(c, H, g, i):
                if i == 0:
                    pe.wait_ge(s_db, c + 2)
                pe.wait_ge(s_df, H * NI + i + 1)
                j = g * NI + i
                nc.tensor.matmul(ps_x[:, :], wdt[:, j * P:j * P + P], dbc[0:R, :], start=True, stop=True).then_inc(s_dp, 1)

            def out_product(c, t, part):
                if t == 0 and part == 0:
                    pe.wait_ge(s_yr, (c + 1) * KD + NI)
                if part == 0:
                    pe.wait_ge(s_oa, c * NT + t + 1)
                for k in range(part * KD // 4, (part + 1) * KD // 4):
                    last = nc.tensor.matmul(ps_o[:, 0:C], z[:, k, t * P:t * P + P], wc[:, k, :], start=(k == 0), stop=(k == KD - 1))
                if part == 3:
                    last.then_inc(s_om, 1)

            def chunk(c, bt, hf, first, last):
                for g in range(2):
                    H = c * 2 + g
                    for s in range(NS):
                        for i in range(NI):
                            m = s * NI + i
                            j = g * NI + i
                            if s == 0:
                                pe.wait_ge(s_yr, H * NI + i + 1)
                                pe.wait_ge(s_diag, H * NI + i + 1)
                                if first:
                                    pe.wait_ge(s_u, j + 1)
                                nc.tensor.matmul(ps_y[:, i, :], diagD[:, i, :], u[:, j, :], start=True, stop=False).then_inc(s_D, 1)
                            if c_dve(m):
                                pe.wait_ge(s_cd, H * NCV + by_dve(m) + NCV)
                            else:
                                pe.wait_ge(s_cp, H * NCP + (m + 1 - by_dve(m)) + NCP)
                            nc.tensor.matmul(ps_y[:, i, :], ident[:, :], hC[:, m % RG, :], start=False, stop=(s == NS - 1)).then_inc(s_y, 1)
                            for part in range(KC):
                                k = turn(m, U_PE[g], part)
                                if last or k < 0:
                                    continue
                                if part == 0:
                                    if k == 0 and g == 0:
                                        pe.wait_ge(s_x[1 - hf], (bt + 1) * 16 if hf == 0 else (bt + 2) * 16)
                                    if k < 2:
                                        pe.wait_ge(s_fz, H * NI + k + 3)
                                    else:
                                        pe.wait_ge(s_fu, (c + 1) * KD + g * NI + k - 1)
                                ins = project(k % 2, 1 - hf, g * NI + k, part)
                                if part == KC - 1:
                                    ins.then_inc(s_pu, 1)
                            for part in range(4):
                                k = turn(m, OUT_PE, part * OUT_PART)
                                if g == 0 and not first and k >= 0:
                                    out_product(c - 1, k, part)
                            for part in range(2):
                                k = turn(m, X_PE[part])
                                if g == 1 and k >= 0 and not last:
                                    if part == 0 and k == 0:
                                        pe.wait_ge(s_df, H * NI + NI + 1)
                                    x_product(c + 1, part * NI + k)
                            for part in range(KC):
                                k = turn(m, Z_PE[g], part)
                                if k < 0:
                                    continue
                                if part == 0:
                                    if k < 2 and not last:
                                        pe.wait_ge(s_fu, (c + 1) * KD + g * NI + k + 3)
                                    else:
                                        pe.wait_ge(s_fz, H * NI + k + 3)
                                ins = project(k % 2, hf, KD + g * NI + k, part)
                                if part == KC - 1:
                                    ins.then_inc(s_pz, 1)
                            k = turn(m, DT_PE[g])
                            if k >= 0 and not (last and g == 1):
                                dt_product(c + g, H + 1, 1 - g, k)
            pe.wait_ge(s_x[0], 16)
            for j in range(KD):
                if j >= 2:
                    pe.wait_ge(s_fu, j - 1)
                project(j % 2, 0, j, 0)
                project(j % 2, 0, j, 1).then_inc(s_pu, 1)
            for k in range(KD):
                x_product(0, k)
            for i in range(NI):
                dt_product(0, 0, 0, i)
            chunks(pe, chunk)
            for t in range(NT):
                for part in range(4):
                    out_product(NCH - 1, t, part)

        @block.gpsimd
        def _(pool):
            pool.sem_inc(s_cp, NCP)
            identity(nc, pool, ident, s_id)

            def times_C(H, g, m):
                if c_dve(m):
                    return
                pool.wait_ge(s_sc, H * NM + m + 1 + RING)
                pool.wait_ge(s_y, H * NM + m + 1)
                nc.gpsimd.tensor_tensor(hC[:, m % RG, :], h[:, m % RING, :], BC[:, 1, m // NI, :], ALU.mult).then_inc(s_cp, 1)

            def chunk(c, bt, hf, first, last):
                for g in range(2):
                    H = c * 2 + g
                    for m in range(NM):
                        s, i = m // NI, m % NI
                        if g == 0 and m % (4 * NI) == 0:
                            pool.wait_ge(s_B[s // 4], c * 32 + 32)
                        if s == 0:
                            pool.wait_ge(s_du, H * NI + i + 1)
                        pool.wait_ge(s_sc, H * NM + m + 1)
                        nc.gpsimd.tensor_tensor(dBu[:, m % RING, :], du[:, g * NI + i, :], BC[:, 0, s, :], ALU.mult).then_inc(s_dB, 1)
                        if m >= SKEW:
                            times_C(H, g, m - SKEW)
                        elif not (first and g == 0):
                            times_C(H - 1, 1 - g, m - SKEW + NM)
            chunks(pool, chunk)
            for m in range(NM - SKEW, NM):
                times_C(2 * NCH - 1, 1, m)

        @block.scalar
        def _(act):
            act.sem_inc(s_fz, NI)
            act.sem_inc(s_db, 1)
            act.sem_inc(s_df, 1)
            act.wait_ge(s_w, 16 * 8)
            nc.scalar.activation(A[:, :, :], A[:, :, :], ACT.Exp).then_inc(s_A, 1)
            act.wait_ge(s_A, 1)
            nc.scalar.activation(A[:, :, :], A[:, :, :], ACT.Copy, scale=-1.0).then_inc(s_A, 1)
            act.wait_ge(s_A, 2)
            act.wait_ge(s_id, 2)

            def diagonals(g):
                for i in range(NI):
                    nc.scalar.activation(diagD[:, i, :], ident[:, :], ACT.Copy, scale=Dp[:, g * NI + i:g * NI + i + 1]).then_inc(s_diag, 1)

            def copy_u(U, j):
                act.wait_ge(s_pu, U + 1)
                act.wait_ge(s_cv, U + 1)
                nc.scalar.activation(uraw[j // NI][:, j % 2, KW - 1:], ps_p[:, j % 2, :], ACT.Identity, bias=buz[:, j:j + 1])
                nc.scalar.activation(u[:, j, :], ps_p[:, j % 2, :], ACT.Identity, bias=btap[:, j:j + 1],
                                     scale=cw[:, j, KW - 1:KW]).then_inc(s_fu, 1)

            def silu_u(U, j):
                act.wait_ge(s_cv, U + 3)
                nc.scalar.activation(u[:, j, :], u[:, j, :], ACT.Silu, bias=cb[:, j:j + 1]).then_inc(s_u, 1)

            def copy_dbc(c):
                act.wait_ge(s_xp, c + 1)
                nc.scalar.activation(dbc[:, :], ps_x[0:XR, :], ACT.Copy).then_inc(s_db, 1)

            def exp_dt(H, g, i):
                j = g * NI + i
                act.wait_ge(s_dp, H * NI + i + 1)
                nc.scalar.activation(delta[:, j, :], ps_x[:, :], ACT.Identity, bias=bdt[:, j:j + 1])
                nc.scalar.activation(du[:, j, :], ps_x[:, :], ACT.Exp, bias=bdt[:, j:j + 1]).then_inc(s_df, 1)

            def keep_last(H, g, m):
                act.wait_ge(s_sc, H * NM + m + 1 + RING)
                nc.scalar.activation(hl[:, g * NI + m % NI, m // NI:m // NI + 1], h[:, m % RING, F - 1:F], ACT.Copy).then_inc(s_hl, 1)

            def ln_dt(H, g, i):
                act.wait_ge(s_df, H * NI + i + 2)
                j = g * NI + i
                nc.scalar.activation(du[:, j, :], du[:, j, :], ACT.Ln, bias=1.0).then_inc(s_ln, 1)

            def chunk(c, bt, hf, first, last):
                for g in range(2):
                    H = c * 2 + g
                    for s in range(NS):
                        for i in range(NI):
                            m = s * NI + i
                            if s == 0:
                                act.wait_ge(s_de, H * NI + i + 1)
                            act.wait_ge(s_sc, H * NM + m + 1)
                            nc.scalar.activation(dA[:, m % RING, :], delta[:, g * NI + i, :], ACT.Exp,
                                                 scale=A[:, g * NI + i, s:s + 1]).then_inc(s_da, 1)
                            if hf == 0 and m > RING:
                                keep_last(H, g, m - RING - 1)
                            if (hf == 0) == (g == 1) and m <= RING and not (first and g == 0):
                                keep_last(H - 1, 1 - g, m - RING - 1 + NM)
                            k = turn(m, U_ACT[g])
                            if k >= 0 and not last:
                                act.wait_ge(s_D, H * NI + k + 1)
                                copy_u((c + 1) * KD + g * NI + k, g * NI + k)
                            if m == SILU_U[g] and not last:
                                for k in range(NI):
                                    silu_u((c + 1) * KD + g * NI + k, g * NI + k)
                            if m == DIAG_ACT and not (last and g == 1):
                                act.wait_ge(s_D, H * NI + NI)
                                diagonals(1 - g)
                            if m == DBC_ACT and g == 1 and not last:
                                act.wait_ge(s_st, c * 16 + 16)
                                copy_dbc(c + 1)
                            k = turn(m, DT_ACT[g])
                            if k >= 0 and not (last and g == 1):
                                exp_dt(H + 1, 1 - g, k)
                            k = turn(m, Z_ACT[g])
                            if k >= 0:
                                act.wait_ge(s_pz, H * NI + k + 1)
                                if g == 0 and k == 0 and not first:
                                    act.wait_ge(s_om, c * NT)
                                nc.scalar.activation(z[:, g * NI + k, :], ps_p[:, k % 2, :], ACT.Identity,
                                                     bias=buz[:, KD + g * NI + k:KD + g * NI + k + 1]).then_inc(s_fz, 1)
                            if m == LN_ACT and not (last and g == 1):
                                for k in range(NI):
                                    ln_dt(H + 1, 1 - g, k)
                            if m == SILU_Z:
                                for k in range(NI):
                                    act.wait_ge(s_fz, H * NI + k + 1 + NI)
                                    nc.scalar.activation(z[:, g * NI + k, :], z[:, g * NI + k, :], ACT.Silu).then_inc(s_zs, 1)
            diagonals(0)
            act.wait_ge(s_tap, 1)
            for j in range(KD):
                copy_u(j, j)
            for j in range(KD):
                silu_u(j, j)
            copy_dbc(0)
            for i in range(NI):
                exp_dt(0, 0, i)
            for i in range(NI):
                ln_dt(0, 0, i)
            chunks(act, chunk)

        @block.vector
        def _(dve):
            V = nc.vector
            dve.sem_inc(s_cv, 2)
            dve.sem_inc(s_sc, RING)
            dve.sem_inc(s_yr, NI)
            dve.sem_inc(s_oa, 1)
            dve.sem_inc(s_cd, NCV)
            dve.wait_ge(s_w, 16 * 8)
            V.tensor_tensor(btap[:, :], buz[:, 0:KD], cw[:, :, KW - 1], ALU.mult).then_inc(s_tap, 1)

            def conv(c, j, hf, k):
                raw, U = uraw[j // NI][:, j % 2, :], c * KD + j
                if k == 0:
                    dve.wait_ge(s_fu, U + 1)
                    if hf == 0:
                        V.memset(raw[:, 0:KW - 1], 0.0).then_inc(s_conv, 1)
                    else:
                        V.tensor_copy(raw[:, 0:KW - 1], carry[:, j, :]).then_inc(s_conv, 1)
                    dve.wait_ge(s_conv, U * CONV + 1)
                    V.tensor_copy(carry[:, j, :], raw[:, F:F + KW - 1]).then_inc(s_conv, 1)
                else:
                    dve.wait_ge(s_conv, U * CONV + 2 + k)
                V.scalar_tensor_tensor(out=u[:, j, :], in0=raw[:, k:k + F], scalar=cw[:, j, k:k + 1], in1=u[:, j, :],
                                       op0=ALU.mult, op1=ALU.add).then_inc(s_cv if k == KW - 2 else s_conv, 1)

            def step_size(H, g, i):
                j = g * NI + i
                dve.wait_ge(s_ln, H * NI + i + 1)
                V.scalar_tensor_tensor(out=delta[:, j, :], in0=du[:, j, :], scalar=LIMIT, in1=delta[:, j, :],
                                       op0=ALU.min, op1=ALU.max).then_inc(s_de, 1)

            def step_u(H, g, i):
                j = g * NI + i
                dve.wait_ge(s_de, H * NI + i + 1)
                V.tensor_tensor(du[:, j, :], delta[:, j, :], u[:, j, :], ALU.mult).then_inc(s_du, 1)

            def gate(H, g, i):
                dve.wait_ge(s_y, (H + 1) * NM - NI + i + 1 + RG)
                dve.wait_ge(s_zs, H * NI + i + 1)
                V.tensor_tensor(z[:, g * NI + i, :], ps_y[:, i, :], z[:, g * NI + i, :], ALU.mult).then_inc(s_yr, 1)

            def out_sum(c, t, k):
                if k == 1:
                    dve.wait_ge(s_oa, c * NT + t + 2)
                    V.tensor_tensor(o_sb[:, t % 2, :], o_sb[:, t % 2, :], bo[:, :], ALU.add).then_inc(s_ov, 1)
                    return
                dve.wait_ge(s_x3[t % 2], c * (16 * NT // 2) + 16 * (t // 2 + 1))
                dve.wait_ge(s_om, c * NT + t + 1)
                V.tensor_tensor(o_sb[:, t % 2, :], ps_o[:, 0:C], o_sb[:, t % 2, :], ALU.add).then_inc(s_oa, 1)

            def times_C(H, m):
                if c_dve(m):
                    dve.wait_ge(s_sc, H * NM + m + 1 + RING)
                    dve.wait_ge(s_y, H * NM + m + 1)
                    V.tensor_tensor(hC[:, m % RG, :], h[:, m % RING, :], BC[:, 1, m // NI, :], ALU.mult).then_inc(s_cd, 1)

            def scan(bt, H, g, m, hf):
                s, i = m // NI, m % NI
                dve.wait_ge(s_dB, H * NM + m + 1)
                dve.wait_ge(s_da, H * NM + m + 1)
                back = (m - RING) % NM
                prior = H if m >= RING else H - 1
                if c_dve(back):
                    dve.wait_ge(s_cd, prior * NCV + by_dve(back) + NCV)
                else:
                    dve.wait_ge(s_cp, prior * NCP + (back + 1 - by_dve(back)) + NCP)
                kept = g * NM + m - RING + 1
                if hf == 0 and kept > 0:
                    dve.wait_ge(s_hl, bt * (2 * NM) + kept)
                if hf == 1 and g == 0 and m < RING:
                    dve.wait_ge(s_hl, bt * (2 * NM) + 2 * NM + kept)
                V.tensor_tensor_scan(out=h[:, m % RING, :], data0=dA[:, m % RING, :], data1=dBu[:, m % RING, :],
                                     initial=0.0 if hf == 0 else hl[:, g * NI + i, s:s + 1], op0=ALU.mult, op1=ALU.add).then_inc(s_sc, 1)

            def chunk(c, bt, hf, first, last):
                for g in range(2):
                    H = c * 2 + g
                    start = first and g == 0
                    end = last and g == 1
                    for m in range(NM):
                        s, i = m // NI, m % NI
                        scan(bt, H, g, m, hf)
                        if m >= 1:
                            times_C(H, m - 1)
                        elif not start:
                            times_C(H - 1, NM - 1)
                        if 1 <= m <= NI and not start:
                            gate(H - 1, 1 - g, m - 1)
                        for k in range(KW - 1):
                            unit = turn(m, U_DVE[g], k)
                            if unit >= 0 and not last:
                                conv(c + 1, g * NI + unit, 1 - hf, k)
                        for k in range(2):
                            t = turn(m, OUT_DVE, k)
                            if g == 0 and not first and t >= 0:
                                out_sum(c - 1, t, k)
                        if DE_DVE <= m < DE_DVE + 2 * NI and not end:
                            (step_size, step_u)[(m - DE_DVE) % 2](H + 1, 1 - g, (m - DE_DVE) // 2)
            for j in range(KD):
                for k in range(KW - 1):
                    conv(0, j, 0, k)
            for i in range(NI):
                step_size(0, 0, i)
                step_u(0, 0, i)
            chunks(dve, chunk)
            times_C(2 * NCH - 1, NM - 1)
            for i in range(NI):
                gate(2 * NCH - 1, 1, i)
            for t in range(NT):
                out_sum(NCH - 1, t, 0)
                out_sum(NCH - 1, t, 1)


def network(nc, consts, x, adj, adjT, gnn_W, gnn_a, gnn_beta, gate_wT, gate_b, w1, b1T, w2, b2, weight, bias,
            W_fc1, b_fc1, W_inT, conv_w, conv_b, W_xprojT, W_dtT, b_dt, A_log, D, W_out, W_fc2T, b_fc2, out):
    B, N, C = x.shape
    T = B * N
    E = w2.shape[0]
    CAP = int(1.2 * T / E)
    NT = T // P
    KC, E2, DI = C // P, W_inT.shape[1], A_log.shape[0]

    def dram(name, shape):
        return nc.dram_tensor(f"{name}_dram", shape, F32, kind="Internal").ap()

    x1_d, xn2_d, logit_d, x3_d, xn4T_d = (dram("x1", (T, C)), dram("xn2", (T, C)), dram("logit", (T, E)), dram("x3", (T, C)),
                                          dram("xn4T", (KC, P, T)))
    xg_d, y_d = dram("xg", (E * CAP, C)), dram("y", (E * CAP, C))
    with ExitStack() as life, ExitStack() as whole:
        m = Place(nc, whole, life, "fused")
        fused = (m.sb("wf", [P, KC, E2]), m.sb("buz", [P, E2 // P]), m.sb("wc", [P, DI // P, C]))
        with ExitStack() as ctx:
            m = Place(nc, ctx, life, "keep")
            gidx = m.sb("gidx", [P, 2, NT], I32)
            wk = m.sb("wk", [P, 2, NT])
            dinv = m.sb("dinv", [P, N // P])
            with ExitStack() as first:
                used = attention_phase(nc, first, dinv, x, adj, gnn_W, gnn_a, gnn_beta, gate_wT, gate_b, x1_d, xn2_d, logit_d, xg_d)
                clear(nc, used)
            routing_phase(nc, life, (gidx, wk), consts, logit_d, xn2_d, xg_d, CAP,
                          fused, (W_inT, W_fc1, b_fc1, W_out, W_fc2T))
            experts_phase(nc, life, xg_d, w1, b1T, w2, b2, y_d, CAP)
            graph_phase(nc, life, (gidx, wk), dinv, x1_d, y_d, adjT, weight, bias, x3_d, xn4T_d)
        mamba_phase(nc, life, fused, xn4T_d, x3_d, conv_w, conv_b, W_xprojT, W_dtT, b_dt, A_log, D, b_fc2, out, N)


_INS = ['consts', 'x', 'adj', 'adjT', 'L0_gnn_W', 'L0_gnn_a', 'L0_gnn_beta', 'L0_ffn_gate_wT', 'L0_ffn_gate_b',
        'L0_ffn_w1', 'L0_ffn_b1T', 'L0_ffn_w2', 'L0_ffn_b2', 'L1_gnn_weight', 'L1_gnn_bias', 'L1_ffn_W_fc1', 'L1_ffn_b_fc1',
        'L1_ffn_W_inT', 'L1_ffn_conv_w', 'L1_ffn_conv_b', 'L1_ffn_W_xprojT', 'L1_ffn_W_dtT', 'L1_ffn_b_dt', 'L1_ffn_A_log',
        'L1_ffn_D', 'L1_ffn_W_out', 'L1_ffn_W_fc2T', 'L1_ffn_b_fc2']
_OUTS = [((8, 1024, 256), 'float32')]


def constants(E, CAP):
    import numpy as _np
    p = _np.arange(128)
    e = _np.arange(E)
    blk = p[:, None] // (128 // E) == p[None, :] // (128 // E)
    tri = p[:, None] < p[None, :]
    first_slot = _np.tile(e * CAP, (128, 1))
    rank = _np.tile(E - e, (128, 1))
    sel = p[:, None] == e[None, :] * (128 // E)
    return _np.concatenate([blk, tri, first_slot, rank, sel], axis=1).astype(_np.float32)


def kernel(**inputs):
    import numpy as _np
    import concourse.bacc as _bacc
    from concourse import mybir as _mybir
    from concourse.bass_utils import run_bass_kernel_spmd as _run
    E = inputs["L0_ffn_w1"].shape[0]
    T = inputs["x"].shape[0] * inputs["x"].shape[1]
    nc = _bacc.Bacc("TRN2", target_bir_lowering=False, num_devices=1)
    arrays, args = {}, []
    for name in _INS:
        if name == "consts":
            a = constants(E, int(1.2 * T / E))
        elif name.endswith("T"):
            a = inputs[name[:-1]].T
        else:
            a = inputs[name]
        a = _np.ascontiguousarray(a)
        arrays[f"in_{name}_dram"] = a
        args.append(nc.dram_tensor(f"in_{name}_dram", a.shape, _mybir.dt.from_np(a.dtype), kind="ExternalInput").ap())
    for i, (shape, dtype) in enumerate(_OUTS):
        dt = _mybir.dt.from_np(_np.dtype(dtype))
        args.append(nc.dram_tensor(f"out_{i}_dram", shape, dt, kind="ExternalOutput").ap())
    network(nc, *args)
    r = _run(nc, [arrays], core_ids=[0])
    return r.results[0]["out_0_dram"]
```
